# Optimizing a Trainium2 kernel written in Bass

```python
import numpy as np
import jax
import jax.numpy as jnp

def _softmax(x, axis=-1):
    return jax.nn.softmax(x, axis=axis)

def _gelu(x):
    return jax.nn.gelu(x, approximate=True)

def _silu(x):
    return jax.nn.silu(x)

def _sigmoid(x):
    return jax.nn.sigmoid(x)

def _layernorm(x, axis=-1, eps=1e-05):
    m = jnp.mean(x, axis=axis, keepdims=True)
    v = jnp.var(x, axis=axis, keepdims=True)
    return (x - m) / jnp.sqrt(v + eps)

def _scatter_add(tgt, idx, src, axis=0):
    return tgt.at[idx].add(src)

def _segment_sum(src, seg, n):
    return jax.ops.segment_sum(src, seg, n)
kernel_name = 'mk_hybrid_d2_jaxref_r8_0ae5a7'

def setup_inputs(seed: int=0):
    np.random.seed(seed)
    _w = jnp.asarray

    def _L0_attn_a_setup():
        import jax, jax.numpy as jnp
        import numpy as np
        from jax import lax
        DIM = 128
        INNER = 256
        STATE = 64
        B, T = (4, 256)
        DECAY = 0.95
        INPUT_FACTOR = 0.05
        LN_EPS = 1e-05

        def _layernorm(x, g, b):
            mu = jnp.mean(x, axis=-1, keepdims=True)
            var = jnp.mean(jnp.square(x - mu), axis=-1, keepdims=True)
            return (x - mu) * lax.rsqrt(var + LN_EPS) * g + b
        key = jax.random.key(seed)
        ks = jax.random.split(key, 8)
        s = 0.02
        return {'x': jax.random.normal(ks[0], (B, T, DIM), jnp.float32), 'W_in': jax.random.normal(ks[1], (2 * INNER, DIM), jnp.float32) * s, 'conv_w': jax.random.normal(ks[2], (INNER, 1, 4), jnp.float32) * s, 'conv_b': jax.random.normal(ks[3], (INNER,), jnp.float32) * s, 'W_B': jax.random.normal(ks[4], (STATE, INNER), jnp.float32) * s, 'W_C': jax.random.normal(ks[5], (INNER, STATE), jnp.float32) * s, 'D_param': jax.random.normal(ks[6], (INNER,), jnp.float32) * s, 'W_out': jax.random.normal(ks[7], (DIM, INNER), jnp.float32) * s, 'ln_gamma': jnp.ones((DIM,), jnp.float32), 'ln_beta': jnp.zeros((DIM,), jnp.float32)}
    _L0_attn_a_in = _L0_attn_a_setup()

    def _L0_attn_b_setup():
        import jax, jax.numpy as jnp
        import numpy as np
        D_MODEL = 128
        N_HEADS = 16
        HEAD_DIM = D_MODEL // N_HEADS
        D_FF = 512
        WINDOW = 128
        LN_EPS = 1e-05
        NEG_INF = jnp.finfo(jnp.float32).min

        def layer_norm(x, w, b):
            mu = jnp.mean(x, axis=-1, keepdims=True)
            var = jnp.mean(jnp.square(x - mu), axis=-1, keepdims=True)
            return (x - mu) * jax.lax.rsqrt(var + LN_EPS) * w + b
        key = jax.random.key(seed)
        ks = jax.random.split(key, 12)
        B, L, D = (2, 256, D_MODEL)
        s = 1.0 / np.sqrt(D)
        inp = {'x': jax.random.normal(ks[0], (B, L, D), jnp.float32), 'Wq': jax.random.normal(ks[1], (D, D), jnp.float32) * s, 'bq': jnp.zeros((D,), jnp.float32), 'Wk': jax.random.normal(ks[2], (D, D), jnp.float32) * s, 'bk': jnp.zeros((D,), jnp.float32), 'Wv': jax.random.normal(ks[3], (D, D), jnp.float32) * s, 'bv': jnp.zeros((D,), jnp.float32), 'Wo': jax.random.normal(ks[4], (D, D), jnp.float32) * s, 'bo': jnp.zeros((D,), jnp.float32), 'W1': jax.random.normal(ks[5], (D, D_FF), jnp.float32) * s, 'b1': jnp.zeros((D_FF,), jnp.float32), 'W2': jax.random.normal(ks[6], (D_FF, D), jnp.float32) * (1.0 / np.sqrt(D_FF)), 'b2': jnp.zeros((D,), jnp.float32), 'ln1_w': jnp.ones((D,), jnp.float32), 'ln1_b': jnp.zeros((D,), jnp.float32), 'ln2_w': jnp.ones((D,), jnp.float32), 'ln2_b': jnp.zeros((D,), jnp.float32)}
        return inp
    _L0_attn_b_in = _L0_attn_b_setup()

    def _L0_ffn_setup():
        import jax, jax.numpy as jnp
        import numpy as np
        NUM_EXPERTS_TOTAL = 9
        TOP_K = 2
        key = jax.random.key(seed)
        k0, k1, k2, k3, k4 = jax.random.split(key, 5)
        B, S, H, I = (2, 256, 128, 352)
        E = NUM_EXPERTS_TOTAL
        x = jax.random.normal(k0, (B, S, H), dtype=jnp.float32)
        Wr = jax.random.normal(k1, (H, E), dtype=jnp.float32) * 0.02
        Wg = jax.random.normal(k2, (E, H, I), dtype=jnp.float32) * 0.02
        Wu = jax.random.normal(k3, (E, H, I), dtype=jnp.float32) * 0.02
        Wd = jax.random.normal(k4, (E, I, H), dtype=jnp.float32) * 0.02
        return {'x': x, 'Wr': Wr, 'Wg': Wg, 'Wu': Wu, 'Wd': Wd}
    _L0_ffn_in = _L0_ffn_setup()

    def _L1_attn_a_setup():
        import math
        import jax, jax.numpy as jnp
        import numpy as np
        H = 16
        WIN = 64
        BS = 64

        def _sliding_window_attn(q, k, v):
            B, Hn, T, hd = q.shape
            nb = T // BS
            nw1 = WIN // BS + 1
            scale = 1.0 / math.sqrt(hd)
            qb = q.reshape(B, Hn, nb, BS, hd)
            kb = k.reshape(B, Hn, nb, BS, hd)
            vb = v.reshape(B, Hn, nb, BS, hd)
            offs = jnp.arange(-(WIN // BS), 1)
            idx_raw = jnp.arange(nb)[:, None] + offs[None, :]
            idx = jnp.clip(idx_raw, 0, nb - 1)
            kg = jnp.take(kb, idx, axis=2)
            vg = jnp.take(vb, idx, axis=2)
            scores = jnp.einsum('bhnqd,bhnwkd->bhnqwk', qb, kg) * scale
            qpos = (jnp.arange(nb) * BS)[:, None, None, None] + jnp.arange(BS)[None, :, None, None]
            kpos = (idx_raw * BS)[:, None, :, None] + jnp.arange(BS)[None, None, None, :]
            valid = (idx_raw[:, None, :, None] >= 0) & (kpos <= qpos) & (qpos - kpos < WIN)
            scores = jnp.where(valid[None, None], scores, -1000000000.0)
            p = jax.nn.softmax(scores.reshape(B, Hn, nb, BS, nw1 * BS), axis=-1)
            p = p.reshape(B, Hn, nb, BS, nw1, BS)
            out = jnp.einsum('bhnqwk,bhnwkd->bhnqd', p, vg)
            return out.reshape(B, Hn, T, hd)
        key = jax.random.key(seed)
        ks = jax.random.split(key, 5)
        B, T, D = (2, 512, 128)
        x = jax.random.normal(ks[0], (B, T, D), dtype=jnp.float32)
        init = 0.02
        Wq = jax.random.normal(ks[1], (D, D), dtype=jnp.float32) * init
        Wk = jax.random.normal(ks[2], (D, D), dtype=jnp.float32) * init
        Wv = jax.random.normal(ks[3], (D, D), dtype=jnp.float32) * init
        Wo = jax.random.normal(ks[4], (D, D), dtype=jnp.float32) * init
        return {'x': x, 'Wq': Wq, 'Wk': Wk, 'Wv': Wv, 'Wo': Wo}
    _L1_attn_a_in = _L1_attn_a_setup()

    def _L1_attn_b_setup():
        import jax, jax.numpy as jnp
        import numpy as np
        DIM = 128

        def _circ_conv(x, key):
            D = x.shape[-1]
            return jnp.fft.irfft(jnp.fft.rfft(x, axis=-1) * jnp.fft.rfft(key), n=D, axis=-1)

        def _circ_corr(x, key):
            D = x.shape[-1]
            return jnp.fft.irfft(jnp.fft.rfft(x, axis=-1) * jnp.conj(jnp.fft.rfft(key)), n=D, axis=-1)
        key = jax.random.key(seed)
        k0, k1, k2 = jax.random.split(key, 3)
        B, T, D = (4, 256, DIM)
        x = jax.random.normal(k0, (B, T, D), dtype=jnp.float32)
        bind_key = jax.random.normal(k1, (D,), dtype=jnp.float32) * 0.02
        unbind_key = jax.random.normal(k2, (D,), dtype=jnp.float32) * 0.02
        gate = jnp.ones((1,), dtype=jnp.float32)
        decay = jnp.asarray(0.9, dtype=jnp.float32)
        return {'x': x, 'bind_key': bind_key, 'unbind_key': unbind_key, 'gate': gate, 'decay': decay}
    _L1_attn_b_in = _L1_attn_b_setup()

    def _L1_ffn_setup():
        import jax, jax.numpy as jnp
        import numpy as np
        D_MODEL = 128
        N_HEADS = 16
        D_HEAD = D_MODEL // N_HEADS
        N_EXPERTS = 8
        TOP_K = 2
        D_FF = 256
        EPS = 1e-06

        def rmsnorm(x, w):
            return x * jax.lax.rsqrt(jnp.mean(x * x, axis=-1, keepdims=True) + EPS) * w

        def swiglu(x, w_gate, w_up, w_down):
            return jax.nn.silu(x @ w_gate) * (x @ w_up) @ w_down
        key = jax.random.key(seed)
        ks = jax.random.split(key, 16)
        s = 0.02
        B, S = (2, 256)
        return {'X': jax.random.normal(ks[0], (B, S, D_MODEL), dtype=jnp.float32), 'norm1_w': jnp.ones((D_MODEL,), jnp.float32), 'norm2_w': jnp.ones((D_MODEL,), jnp.float32), 'wq': jax.random.normal(ks[1], (D_MODEL, D_MODEL), jnp.float32) * s, 'wk': jax.random.normal(ks[2], (D_MODEL, D_MODEL), jnp.float32) * s, 'wv': jax.random.normal(ks[3], (D_MODEL, D_MODEL), jnp.float32) * s, 'wo': jax.random.normal(ks[4], (D_MODEL, D_MODEL), jnp.float32) * s, 'router_w': jax.random.normal(ks[5], (D_MODEL, N_EXPERTS), jnp.float32) * s, 'sh_gate': jax.random.normal(ks[6], (D_MODEL, D_FF), jnp.float32) * s, 'sh_up': jax.random.normal(ks[7], (D_MODEL, D_FF), jnp.float32) * s, 'sh_down': jax.random.normal(ks[8], (D_FF, D_MODEL), jnp.float32) * s, 'e_gate': jax.random.normal(ks[9], (N_EXPERTS, D_MODEL, D_FF), jnp.float32) * s, 'e_up': jax.random.normal(ks[10], (N_EXPERTS, D_MODEL, D_FF), jnp.float32) * s, 'e_down': jax.random.normal(ks[11], (N_EXPERTS, D_FF, D_MODEL), jnp.float32) * s}
    _L1_ffn_in = _L1_ffn_setup()
    _d = {'L0_attn_a_x': _L0_attn_a_in['x'], 'L0_attn_a_W_in': _L0_attn_a_in['W_in'], 'L0_attn_a_conv_w': _L0_attn_a_in['conv_w'], 'L0_attn_a_conv_b': _L0_attn_a_in['conv_b'], 'L0_attn_a_W_B': _L0_attn_a_in['W_B'], 'L0_attn_a_W_C': _L0_attn_a_in['W_C'], 'L0_attn_a_D_param': _L0_attn_a_in['D_param'], 'L0_attn_a_W_out': _L0_attn_a_in['W_out'], 'L0_attn_a_ln_gamma': _L0_attn_a_in['ln_gamma'], 'L0_attn_a_ln_beta': _L0_attn_a_in['ln_beta'], 'L0_attn_b_Wq': _L0_attn_b_in['Wq'], 'L0_attn_b_bq': _L0_attn_b_in['bq'], 'L0_attn_b_Wk': _L0_attn_b_in['Wk'], 'L0_attn_b_bk': _L0_attn_b_in['bk'], 'L0_attn_b_Wv': _L0_attn_b_in['Wv'], 'L0_attn_b_bv': _L0_attn_b_in['bv'], 'L0_attn_b_Wo': _L0_attn_b_in['Wo'], 'L0_attn_b_bo': _L0_attn_b_in['bo'], 'L0_attn_b_W1': _L0_attn_b_in['W1'], 'L0_attn_b_b1': _L0_attn_b_in['b1'], 'L0_attn_b_W2': _L0_attn_b_in['W2'], 'L0_attn_b_b2': _L0_attn_b_in['b2'], 'L0_attn_b_ln1_w': _L0_attn_b_in['ln1_w'], 'L0_attn_b_ln1_b': _L0_attn_b_in['ln1_b'], 'L0_attn_b_ln2_w': _L0_attn_b_in['ln2_w'], 'L0_attn_b_ln2_b': _L0_attn_b_in['ln2_b'], 'L0_ffn_Wr': _L0_ffn_in['Wr'], 'L0_ffn_Wg': _L0_ffn_in['Wg'], 'L0_ffn_Wu': _L0_ffn_in['Wu'], 'L0_ffn_Wd': _L0_ffn_in['Wd'], 'L1_attn_a_Wq': _L1_attn_a_in['Wq'], 'L1_attn_a_Wk': _L1_attn_a_in['Wk'], 'L1_attn_a_Wv': _L1_attn_a_in['Wv'], 'L1_attn_a_Wo': _L1_attn_a_in['Wo'], 'L1_attn_b_bind_key': _L1_attn_b_in['bind_key'], 'L1_attn_b_unbind_key': _L1_attn_b_in['unbind_key'], 'L1_attn_b_gate': _L1_attn_b_in['gate'], 'L1_attn_b_decay': _L1_attn_b_in['decay'], 'L1_ffn_norm1_w': _L1_ffn_in['norm1_w'], 'L1_ffn_norm2_w': _L1_ffn_in['norm2_w'], 'L1_ffn_wq': _L1_ffn_in['wq'], 'L1_ffn_wk': _L1_ffn_in['wk'], 'L1_ffn_wv': _L1_ffn_in['wv'], 'L1_ffn_wo': _L1_ffn_in['wo'], 'L1_ffn_router_w': _L1_ffn_in['router_w'], 'L1_ffn_sh_gate': _L1_ffn_in['sh_gate'], 'L1_ffn_sh_up': _L1_ffn_in['sh_up'], 'L1_ffn_sh_down': _L1_ffn_in['sh_down'], 'L1_ffn_e_gate': _L1_ffn_in['e_gate'], 'L1_ffn_e_up': _L1_ffn_in['e_up'], 'L1_ffn_e_down': _L1_ffn_in['e_down']}
    _x0 = _d['L0_attn_a_x']
    _d['L0_attn_a_x'] = jax.random.normal(jax.random.fold_in(jax.random.key(seed), 1), (1, 2048, 128), dtype=_x0.dtype)
    del _x0
    return _d

def reference(L0_attn_a_x, L0_attn_a_W_in, L0_attn_a_conv_w, L0_attn_a_conv_b, L0_attn_a_W_B, L0_attn_a_W_C, L0_attn_a_D_param, L0_attn_a_W_out, L0_attn_a_ln_gamma, L0_attn_a_ln_beta, L0_attn_b_Wq, L0_attn_b_bq, L0_attn_b_Wk, L0_attn_b_bk, L0_attn_b_Wv, L0_attn_b_bv, L0_attn_b_Wo, L0_attn_b_bo, L0_attn_b_W1, L0_attn_b_b1, L0_attn_b_W2, L0_attn_b_b2, L0_attn_b_ln1_w, L0_attn_b_ln1_b, L0_attn_b_ln2_w, L0_attn_b_ln2_b, L0_ffn_Wr, L0_ffn_Wg, L0_ffn_Wu, L0_ffn_Wd, L1_attn_a_Wq, L1_attn_a_Wk, L1_attn_a_Wv, L1_attn_a_Wo, L1_attn_b_bind_key, L1_attn_b_unbind_key, L1_attn_b_gate, L1_attn_b_decay, L1_ffn_norm1_w, L1_ffn_norm2_w, L1_ffn_wq, L1_ffn_wk, L1_ffn_wv, L1_ffn_wo, L1_ffn_router_w, L1_ffn_sh_gate, L1_ffn_sh_up, L1_ffn_sh_down, L1_ffn_e_gate, L1_ffn_e_up, L1_ffn_e_down):

    def _L0_attn_a_ref(x, W_in, conv_w, conv_b, W_B, W_C, D_param, W_out, ln_gamma, ln_beta):
        import jax, jax.numpy as jnp
        import numpy as np
        from jax import lax
        DIM = 128
        INNER = 256
        STATE = 64
        B, T = (4, 256)
        DECAY = 0.95
        INPUT_FACTOR = 0.05
        LN_EPS = 1e-05

        def _layernorm(x, g, b):
            mu = jnp.mean(x, axis=-1, keepdims=True)
            var = jnp.mean(jnp.square(x - mu), axis=-1, keepdims=True)
            return (x - mu) * lax.rsqrt(var + LN_EPS) * g + b
        Bn, Tn, Dn = x.shape
        x_proj = jnp.einsum('btd,ed->bte', x, W_in)
        x_input, x_gate = jnp.split(x_proj, 2, axis=-1)
        xc = lax.conv_general_dilated(x_input.transpose(0, 2, 1), conv_w, window_strides=(1,), padding=[(3, 0)], feature_group_count=INNER) + conv_b[None, :, None]
        u = jax.nn.silu(xc).transpose(0, 2, 1)
        Bu = jnp.einsum('btc,sc->bts', u, W_B)

        def step(h, bu_t):
            h = DECAY * h + INPUT_FACTOR * bu_t
            return (h, h)
        h0 = jnp.zeros((Bn, STATE), x.dtype)
        _, hs = lax.scan(step, h0, Bu.transpose(1, 0, 2))
        hs = hs.transpose(1, 0, 2)
        y = jnp.einsum('bts,cs->btc', hs, W_C) + D_param * u
        y = y * jax.nn.silu(x_gate)
        y = jnp.einsum('btc,dc->btd', y, W_out)
        return _layernorm(y + x, ln_gamma, ln_beta)

    def _L0_attn_b_ref(x, Wq, bq, Wk, bk, Wv, bv, Wo, bo, W1, b1, W2, b2, ln1_w, ln1_b, ln2_w, ln2_b):
        import jax, jax.numpy as jnp
        import numpy as np
        D_MODEL = 128
        N_HEADS = 16
        HEAD_DIM = D_MODEL // N_HEADS
        D_FF = 512
        WINDOW = 128
        LN_EPS = 1e-05
        NEG_INF = jnp.finfo(jnp.float32).min

        def layer_norm(x, w, b):
            mu = jnp.mean(x, axis=-1, keepdims=True)
            var = jnp.mean(jnp.square(x - mu), axis=-1, keepdims=True)
            return (x - mu) * jax.lax.rsqrt(var + LN_EPS) * w + b
        B, L, D = x.shape
        i = jnp.arange(L)[:, None]
        j = jnp.arange(L)[None, :]
        band = (j > i) | (i - j > WINDOW)
        bias = jnp.where(band, NEG_INF, 0.0).astype(x.dtype)
        h = layer_norm(x, ln1_w, ln1_b)
        q = (h @ Wq + bq).reshape(B, L, N_HEADS, HEAD_DIM)
        k = (h @ Wk + bk).reshape(B, L, N_HEADS, HEAD_DIM)
        v = (h @ Wv + bv).reshape(B, L, N_HEADS, HEAD_DIM)
        scale = 1.0 / np.sqrt(HEAD_DIM)
        scores = jnp.einsum('blhd,bmhd->bhlm', q, k) * scale + bias
        attn = jax.nn.softmax(scores, axis=-1)
        ctx = jnp.einsum('bhlm,bmhd->blhd', attn, v).reshape(B, L, D)
        x = x + ctx @ Wo + bo
        h2 = layer_norm(x, ln2_w, ln2_b)
        x = x + jax.nn.gelu(h2 @ W1 + b1) @ W2 + b2
        return x

    def _L0_ffn_ref(x, Wr, Wg, Wu, Wd):
        import jax, jax.numpy as jnp
        import numpy as np
        NUM_EXPERTS_TOTAL = 9
        TOP_K = 2
        B, S, H = x.shape
        E = NUM_EXPERTS_TOTAL
        T = B * S
        logits = jnp.einsum('bsh,he->bse', x, Wr)
        probs = jax.nn.softmax(logits, axis=-1)
        topk_w, topk_idx = jax.lax.top_k(probs, TOP_K)
        topk_w = topk_w / jnp.sum(topk_w, axis=-1, keepdims=True)
        xf = x.reshape(T, H)
        wf = topk_w.reshape(T, TOP_K)
        idxf = topk_idx.reshape(T, TOP_K)
        cw = jnp.zeros((T, E), dtype=x.dtype).at[jnp.arange(T)[:, None], idxf].add(wf)
        gate = jax.nn.silu(jnp.einsum('th,ehi->tei', xf, Wg))
        hidden = gate * jnp.einsum('th,ehi->tei', xf, Wu)
        out = jnp.einsum('tei,eih,te->th', hidden, Wd, cw)
        return out.reshape(B, S, H)

    def _L1_attn_a_ref(x, Wq, Wk, Wv, Wo):
        import math
        import jax, jax.numpy as jnp
        import numpy as np
        H = 16
        WIN = 64
        BS = 64

        def _sliding_window_attn(q, k, v):
            B, Hn, T, hd = q.shape
            nb = T // BS
            nw1 = WIN // BS + 1
            scale = 1.0 / math.sqrt(hd)
            qb = q.reshape(B, Hn, nb, BS, hd)
            kb = k.reshape(B, Hn, nb, BS, hd)
            vb = v.reshape(B, Hn, nb, BS, hd)
            offs = jnp.arange(-(WIN // BS), 1)
            idx_raw = jnp.arange(nb)[:, None] + offs[None, :]
            idx = jnp.clip(idx_raw, 0, nb - 1)
            kg = jnp.take(kb, idx, axis=2)
            vg = jnp.take(vb, idx, axis=2)
            scores = jnp.einsum('bhnqd,bhnwkd->bhnqwk', qb, kg) * scale
            qpos = (jnp.arange(nb) * BS)[:, None, None, None] + jnp.arange(BS)[None, :, None, None]
            kpos = (idx_raw * BS)[:, None, :, None] + jnp.arange(BS)[None, None, None, :]
            valid = (idx_raw[:, None, :, None] >= 0) & (kpos <= qpos) & (qpos - kpos < WIN)
            scores = jnp.where(valid[None, None], scores, -1000000000.0)
            p = jax.nn.softmax(scores.reshape(B, Hn, nb, BS, nw1 * BS), axis=-1)
            p = p.reshape(B, Hn, nb, BS, nw1, BS)
            out = jnp.einsum('bhnqwk,bhnwkd->bhnqd', p, vg)
            return out.reshape(B, Hn, T, hd)
        B, T, D = x.shape
        hd = D // H

        def proj(W):
            return (x @ W.T).reshape(B, T, H, hd).transpose(0, 2, 1, 3)
        q, k, v = (proj(Wq), proj(Wk), proj(Wv))
        out = _sliding_window_attn(q, k, v)
        out = out.transpose(0, 2, 1, 3).reshape(B, T, D)
        return out @ Wo.T

    def _L1_attn_b_ref(x, bind_key, unbind_key, gate, decay):
        import jax, jax.numpy as jnp
        import numpy as np
        DIM = 128

        def _circ_conv(x, key):
            D = x.shape[-1]
            return jnp.fft.irfft(jnp.fft.rfft(x, axis=-1) * jnp.fft.rfft(key), n=D, axis=-1)

        def _circ_corr(x, key):
            D = x.shape[-1]
            return jnp.fft.irfft(jnp.fft.rfft(x, axis=-1) * jnp.conj(jnp.fft.rfft(key)), n=D, axis=-1)
        B, T, D = x.shape
        bound = _circ_conv(x, bind_key)
        d = jax.nn.sigmoid(decay)
        pos = jnp.arange(T, dtype=x.dtype)
        diff = pos[:, None] - pos[None, :]
        causal = diff >= 0
        decay_matrix = jnp.where(causal, d ** jnp.maximum(diff, 0.0), 0.0)
        hologram = jnp.einsum('ts,bsd->btd', decay_matrix, bound)
        retrieved = _circ_corr(hologram, unbind_key)
        return x + gate * retrieved

    def _L1_ffn_ref(X, norm1_w, norm2_w, wq, wk, wv, wo, router_w, sh_gate, sh_up, sh_down, e_gate, e_up, e_down):
        import jax, jax.numpy as jnp
        import numpy as np
        D_MODEL = 128
        N_HEADS = 16
        D_HEAD = D_MODEL // N_HEADS
        N_EXPERTS = 8
        TOP_K = 2
        D_FF = 256
        EPS = 1e-06

        def rmsnorm(x, w):
            return x * jax.lax.rsqrt(jnp.mean(x * x, axis=-1, keepdims=True) + EPS) * w

        def swiglu(x, w_gate, w_up, w_down):
            return jax.nn.silu(x @ w_gate) * (x @ w_up) @ w_down
        B, S, d = X.shape
        scale = 1.0 / jnp.sqrt(jnp.asarray(D_HEAD, X.dtype))
        h = rmsnorm(X, norm1_w)
        q = (h @ wq).reshape(B, S, N_HEADS, D_HEAD)
        k = (h @ wk).reshape(B, S, N_HEADS, D_HEAD)
        v = (h @ wv).reshape(B, S, N_HEADS, D_HEAD)
        scores = jnp.einsum('bshd,bthd->bhst', q, k) * scale
        attn = jax.nn.softmax(scores, axis=-1)
        ctx = jnp.einsum('bhst,bthd->bshd', attn, v).reshape(B, S, d)
        X = X + ctx @ wo
        h2 = rmsnorm(X, norm2_w).reshape(B * S, d)
        logits = h2 @ router_w
        probs = jax.nn.softmax(logits, axis=-1)
        topw, topi = jax.lax.top_k(probs, TOP_K)
        topw = jax.nn.softmax(topw, axis=-1)
        combine = jnp.sum(jax.nn.one_hot(topi, N_EXPERTS, dtype=h2.dtype) * topw[..., None], axis=1)
        shared = swiglu(h2, sh_gate, sh_up, sh_down)
        gate = jnp.einsum('td,edf->etf', h2, e_gate)
        up = jnp.einsum('td,edf->etf', h2, e_up)
        eout = jnp.einsum('etf,efd->etd', jax.nn.silu(gate) * up, e_down)
        spec = jnp.einsum('etd,te->td', eout, combine)
        moe_out = (shared + spec).reshape(B, S, d)
        return X + moe_out
    x = L0_attn_a_x
    x = x + _L0_attn_a_ref(_layernorm(x, axis=-1), L0_attn_a_W_in, L0_attn_a_conv_w, L0_attn_a_conv_b, L0_attn_a_W_B, L0_attn_a_W_C, L0_attn_a_D_param, L0_attn_a_W_out, L0_attn_a_ln_gamma, L0_attn_a_ln_beta)
    x = x + _L0_ffn_ref(_layernorm(x, axis=-1), L0_ffn_Wr, L0_ffn_Wg, L0_ffn_Wu, L0_ffn_Wd)
    x = x + _L0_attn_b_ref(_layernorm(x, axis=-1), L0_attn_b_Wq, L0_attn_b_bq, L0_attn_b_Wk, L0_attn_b_bk, L0_attn_b_Wv, L0_attn_b_bv, L0_attn_b_Wo, L0_attn_b_bo, L0_attn_b_W1, L0_attn_b_b1, L0_attn_b_W2, L0_attn_b_b2, L0_attn_b_ln1_w, L0_attn_b_ln1_b, L0_attn_b_ln2_w, L0_attn_b_ln2_b)
    x = x + _L0_ffn_ref(_layernorm(x, axis=-1), L0_ffn_Wr, L0_ffn_Wg, L0_ffn_Wu, L0_ffn_Wd)
    x = x + _L1_attn_a_ref(_layernorm(x, axis=-1), L1_attn_a_Wq, L1_attn_a_Wk, L1_attn_a_Wv, L1_attn_a_Wo)
    x = x + _L1_ffn_ref(_layernorm(x, axis=-1), L1_ffn_norm1_w, L1_ffn_norm2_w, L1_ffn_wq, L1_ffn_wk, L1_ffn_wv, L1_ffn_wo, L1_ffn_router_w, L1_ffn_sh_gate, L1_ffn_sh_up, L1_ffn_sh_down, L1_ffn_e_gate, L1_ffn_e_up, L1_ffn_e_down)
    x = x + _L1_attn_b_ref(_layernorm(x, axis=-1), L1_attn_b_bind_key, L1_attn_b_unbind_key, L1_attn_b_gate, L1_attn_b_decay)
    x = x + _L1_ffn_ref(_layernorm(x, axis=-1), L1_ffn_norm1_w, L1_ffn_norm2_w, L1_ffn_wq, L1_ffn_wk, L1_ffn_wv, L1_ffn_wo, L1_ffn_router_w, L1_ffn_sh_gate, L1_ffn_sh_up, L1_ffn_sh_down, L1_ffn_e_gate, L1_ffn_e_up, L1_ffn_e_down)
    return x

_drawn_inputs = setup_inputs


def setup_inputs(seed=0):
    import zlib

    import numpy as np

    out = dict(_drawn_inputs(seed))
    spreads = {'L0_attn_a_ln_gamma': (1.0, 0.2),
     'L0_attn_a_ln_beta': (0.0, 0.1),
     'L0_attn_b_bq': (0.0, 0.8),
     'L0_attn_b_bk': (0.0, 0.8),
     'L0_attn_b_bv': (0.0, 0.1),
     'L0_attn_b_bo': (0.0, 0.1),
     'L0_attn_b_b1': (0.0, 0.354),
     'L0_attn_b_b2': (0.0, 0.1),
     'L0_attn_b_ln1_w': (1.0, 0.539),
     'L0_attn_b_ln1_b': (0.0, 0.1),
     'L0_attn_b_ln2_w': (1.0, 0.2),
     'L0_attn_b_ln2_b': (0.0, 0.372),
     'L1_ffn_norm1_w': (1.0, 0.6),
     'L1_ffn_norm2_w': (1.0, 0.6)}
    factors = {'L0_attn_a_W_in': 8.0,
     'L0_attn_a_conv_w': 8.0,
     'L0_attn_a_conv_b': 8.0,
     'L0_attn_a_W_B': 8.0,
     'L0_attn_a_W_C': 8.0,
     'L0_attn_a_D_param': 8.0,
     'L0_attn_a_W_out': 8.0,
     'L0_ffn_Wr': 8.0,
     'L0_ffn_Wg': 8.0,
     'L0_ffn_Wu': 8.0,
     'L0_ffn_Wd': 8.0,
     'L1_attn_a_Wq': 8.0,
     'L1_attn_a_Wk': 8.0,
     'L1_attn_a_Wv': 8.0,
     'L1_attn_a_Wo': 8.0,
     'L1_attn_b_bind_key': 3.874,
     'L1_attn_b_unbind_key': 3.875,
     'L1_ffn_wq': 8.0,
     'L1_ffn_wk': 8.0,
     'L1_ffn_wv': 8.0,
     'L1_ffn_wo': 8.0,
     'L1_ffn_router_w': 8.0,
     'L1_ffn_sh_gate': 8.0,
     'L1_ffn_sh_up': 8.0,
     'L1_ffn_sh_down': 8.0,
     'L1_ffn_e_gate': 8.0,
     'L1_ffn_e_up': 8.0,
     'L1_ffn_e_down': 8.0}
    for name, (base, spread) in spreads.items():
        noise = np.random.default_rng([zlib.crc32(name.encode()), seed]).standard_normal(out[name].shape)
        drawn = base * np.exp(spread * noise) if base else spread * noise
        out[name] = jnp.asarray(drawn.astype(out[name].dtype))
    for name, factor in factors.items():
        out[name] = (out[name] * factor).astype(out[name].dtype)
    return out
```

```python
import concourse.bass as bass
from concourse import mybir
from contextlib import ExitStack

fp32 = mybir.dt.float32
bf16 = mybir.dt.bfloat16
u32 = mybir.dt.uint32
ALU = mybir.AluOpType
ACT = mybir.ActivationFunctionType
AX = mybir.AxisListType

P = 128
N_TOK = 2048
D = 128
TILES = N_TOK // P
CHUNK = 512
CHUNKS = N_TOK // CHUNK
TPC = CHUNK // P
HEADS = 16
HD = D // HEADS
INNER = 256
STATE = 64
TAPS = 4
D_FF = 512
LN_EPS = 1e-5
RMS_EPS = 1e-6
MASKED = -1.0e30
PARTS = 3
STACK = PARTS * PARTS * HD
SHIFT_AT = 96
UNIT = 1024
P_UNITS = 8
OUT_ROWS = 32


class Count:

    def __init__(self, sem):
        self.sem = sem
        self.at = 0

    def after(self, n):
        return self.sem, self.at + n

    def passed(self, n):
        self.at = self.at + n


class Core:

    def __init__(self, nc, ctx):
        self.nc = nc
        self.ctx = ctx
        self.counts = {}

    def sbuf(self, name, shape, dt=fp32):
        return self.ctx.enter_context(self.nc.sbuf_tensor(name, shape, dt))

    def count(self, name):
        if name not in self.counts:
            self.counts[name] = Count(self.ctx.enter_context(self.nc.semaphore(name)))
        return self.counts[name]


class Chain:

    def __init__(self, engine, steps):
        self.engine = engine
        self.steps = steps
        self.n = 0
        self.offset = 0

    def mark(self, ins):
        ins.then_inc(self.steps.sem, 1)
        self.n += 1

    def link(self, ins):
        self.mark(ins)
        self.engine.wait_ge(*self.steps.after(self.offset + self.n))


def bank(c, n, width=CHUNK):
    return c.ps[:, n * CHUNK:n * CHUNK + width]


def constants_stage(c):
    nc = c.nc
    built = c.count("const_built")
    zeroed = c.count("const_zeroed")
    loaded = c.count("const_loaded")
    n_loaded = [0]
    n_pool = [0]
    with nc.Block() as block:

        @block.gpsimd
        def _(pool):
            def step(ins):
                ins.then_inc(built.sem, 1)
                n_pool[0] += 1
                pool.wait_ge(*built.after(n_pool[0]))

            def keep(view, width, base, coef, step_, fill):
                step(pool.affine_select(out=view, in_=view, compare_op=ALU.is_ge, fill=fill, base=base,
                                        pattern=[[step_, width]], channel_multiplier=coef))

            step(pool.memset(c.minus_half[:], -0.5))
            step(pool.memset(c.ident[:], 0.0))
            step(pool.affine_select(out=c.ident[:], in_=c.ident[:], compare_op=ALU.not_equal, fill=1.0,
                                    base=0, pattern=[[-1, P]], channel_multiplier=1))
            step(pool.tensor_copy(c.ident16[:], c.ident[:]))
            step(pool.memset(c.flip[:], 0.0))
            for total in (0, D):
                step(pool.affine_select(out=c.flip[:], in_=c.flip[:], compare_op=ALU.not_equal, fill=1.0,
                                        base=-total, pattern=[[1, P]], channel_multiplier=1))
            step(pool.iota(c.expert_ids_i[:], pattern=[[1, 16]], base=0, channel_multiplier=0))
            step(pool.tensor_copy(c.expert_ids[:], c.expert_ids_i[:]))
            for n, back in enumerate((128, 63)):
                for first in (False, True):
                    m = c.mask_q[:, n, 1 if first else 0, :]
                    step(pool.memset(m, 0.0))
                    keep(m, 2 * P, P, 1, -1, MASKED)
                    keep(m, 2 * P, back - P, -1, 1, MASKED)
                    if first:
                        keep(m, 2 * P, -P, 0, 1, MASKED)
                m = c.mask_k[:, n, :]
                step(pool.memset(m, 0.0))
                keep(m, 2 * P, 0, -1, 1, MASKED)
                keep(m, 2 * P, back, 1, -1, MASKED)

        @block.vector
        def _(dve):
            nc.vector.memset(c.q_max[:], 0.0).then_inc(zeroed.sem, 1)
            nc.vector.memset(c.q_exp[:], 0.0).then_inc(zeroed.sem, 1)
            nc.vector.memset(c.k_max[:], 0.0).then_inc(zeroed.sem, 1)
            nc.vector.memset(c.k_exp[:], 0.0).then_inc(zeroed.sem, 1)
            dve.wait_ge(*zeroed.after(4))
            nc.vector.memset(c.k_exp[SHIFT_AT:P], 1.0).then_inc(zeroed.sem, 1)
            nc.vector.memset(c.v_head[:], 0.0).then_inc(zeroed.sem, 1)
            dve.wait_ge(*zeroed.after(6))
            nc.vector.memset(c.v_head[:, :, :, HD:2 * HD], 1.0).then_inc(zeroed.sem, 1)

        @block.sync
        def _(sp):
            def load(dst, src):
                sp.dma_start(dst, src).then_inc(loaded.sem, 16)
                n_loaded[0] += 1

            load(c.x[:], c.i["L0_attn_a_x"].rearrange("b (t p) d -> p (b t) d", p=P))
            for name, dst in c.columns.items():
                for n in range(dst.shape[1]):
                    load(dst[:, n:n + 1], c.i[name][n * P:(n + 1) * P].rearrange("(p o) -> p o", o=1))
            for name, dst in c.rows.items():
                load(dst, c.i[name].partition_broadcast(P))
            load(c.conv_w[:], c.i["L0_attn_a_conv_w"].rearrange("(n p) o k -> p n (o k)", p=P))
            load(c.w_in[:], c.i["L0_attn_a_W_in_T"])
            load(c.w_b[:], c.i["L0_attn_a_W_B_T"].rearrange("(n p) s -> p n s", p=P))
            load(c.w_c[:], c.i["L0_attn_a_W_C_T"])
            load(c.w_out[:], c.i["L0_attn_a_W_out_T"].rearrange("(n p) d -> p n d", p=P))
            load(c.w1[:], c.i["L0_attn_b_W1"])
            load(c.w2[:], c.i["L0_attn_b_W2"].rearrange("(n p) d -> p n d", p=P))
            load(c.router0[:], c.i["L0_ffn_Wr"])
            load(c.router1[:], c.i["L1_ffn_router_w"])
            for n, name in enumerate(c.proj_names):
                load(c.proj[:, n, :], c.i[name])
            for s, name in enumerate(("bind", "unbind")):
                key = c.i[f"L1_attn_b_{name}_key"].rearrange("(o n) -> o n", o=1)
                for half in range(2):
                    load(c.keys_twice[s:s + 1, half * D:(half + 1) * D], key)
            sp.wait_ge(*loaded.after(16 * n_loaded[0]))

    built.passed(n_pool[0])
    zeroed.passed(7)
    loaded.passed(16 * n_loaded[0])


def norm_stage(c, src, dst, rms=False, transpose=False, scale=None, shift=None, add=None):
    nc = c.nc
    eps = RMS_EPS if rms else LN_EPS
    chain_s = c.count("dve_chain")
    stats_ready = c.count("norm_stats_ready")
    rstd_ready = c.count("norm_rstd_ready")
    tile_ready = c.count("norm_tile_ready")
    bank_ready = c.count("norm_bank_ready")
    bank_taken = c.count("norm_bank_taken")
    links = [0]
    with nc.Block() as block:

        @block.vector
        def _(dve):
            chain = Chain(dve, chain_s)
            for t in range(TILES):
                ins = nc.vector.bn_stats(c.bn[:, t, :], src[:, t, :])
            chain.link(ins)
            for t in range(TILES):
                ins = nc.vector.bn_aggr(c.mv[:, t, :], c.bn[:, t, :])
            if rms:
                chain.link(ins)
                chain.link(nc.vector.tensor_tensor(c.mean2[:], c.mv[:, :, 0], c.mv[:, :, 0], ALU.mult))
                ins = nc.vector.tensor_tensor(c.mv[:, :, 1], c.mv[:, :, 1], c.mean2[:], ALU.add)
            ins.then_inc(stats_ready.sem, 1)
            dve.wait_ge(*rstd_ready.after(2))
            for t in range(TILES):
                if rms:
                    ins = nc.vector.tensor_scalar(dst[:, t, :], src[:, t, :], c.rstd[:, t:t + 1], None, ALU.mult)
                else:
                    ins = nc.vector.tensor_scalar(dst[:, t, :], src[:, t, :], c.mv[:, t, 0:1], c.rstd[:, t:t + 1],
                                                  ALU.subtract, ALU.mult)
                ins.then_inc(tile_ready.sem, 1)
            links[0] = chain.n

        @block.gpsimd
        def _(pool):
            pool.wait_ge(*stats_ready.after(1))
            pool.tensor_scalar(c.rstd[:], c.mv[:, :, 1], eps, None, ALU.add).then_inc(rstd_ready.sem, 1)
            pool.wait_ge(*rstd_ready.after(1))
            pool.tensor_tensor(c.rstd[:], c.rstd[:], c.minus_half[:], ALU.pow).then_inc(rstd_ready.sem, 1)

        if transpose:
            @block.tensor
            def _(pe):
                for t in range(TILES):
                    pe.wait_ge(*tile_ready.after(t + 1))
                    out = bank(c, t // TPC)[:, (t % TPC) * P:(t % TPC + 1) * P]
                    ins = nc.tensor.transpose(out, dst[:, t, :], c.ident[:])
                    if t % TPC == TPC - 1:
                        ins.then_inc(bank_ready.sem, 1)

            @block.scalar
            def _(act):
                for b in range(CHUNKS):
                    act.wait_ge(*bank_ready.after(b + 1))
                    out = c.ht[:, b * CHUNK:(b + 1) * CHUNK]
                    if scale is None:
                        nc.scalar.activation(out, bank(c, b), ACT.Copy).then_inc(bank_taken.sem, 1)
                    else:
                        nc.scalar.activation(out, bank(c, b), ACT.Identity, scale=scale,
                                             bias=shift if shift is not None else 0.0).then_inc(bank_taken.sem, 1)

    chain_s.passed(links[0])
    stats_ready.passed(1)
    rstd_ready.passed(2)
    tile_ready.passed(TILES)
    if transpose:
        bank_ready.passed(CHUNKS)
        bank_taken.passed(CHUNKS)


def state_space_stage(c):
    nc = c.nc
    proj_ready = c.count("ss_proj_ready")
    proj_taken = c.count("ss_proj_taken")
    gate_taken = c.count("ss_gate_taken")
    conv_ready = c.count("ss_conv_ready")
    u_ready = c.count("ss_u_ready")
    bu_ready = c.count("ss_bu_ready")
    bu_taken = c.count("ss_bu_taken")
    state_ready = c.count("ss_state_ready")
    y_ready = c.count("ss_y_ready")
    y_taken = c.count("ss_y_taken")
    out_ready = c.count("ss_out_ready")
    added = c.count("ss_added")
    chain_s = c.count("dve_chain")
    blocks = INNER // P
    xin, u, gate = c.big[:, 0:2, :], c.big[:, 2:4, :], c.big[:, 4:6, :]
    PAD = TAPS - 1
    links = [0]
    with nc.Block() as block:

        @block.tensor
        def _(pe):
            for b in range(2 * blocks):
                for k in range(CHUNKS):
                    n = b * CHUNKS + k
                    if n >= 8:
                        pe.wait_ge(*proj_taken.after(n - 7))
                    nc.tensor.matmul(bank(c, n % 8), c.w_in[:, b * P:(b + 1) * P],
                                     c.ht[:, k * CHUNK:(k + 1) * CHUNK], start=True, stop=True).then_inc(proj_ready.sem, 1)
            pe.wait_ge(*u_ready.after(blocks))
            pe.wait_ge(*proj_taken.after(4 * blocks * 2))
            for k in range(CHUNKS):
                for b in range(blocks):
                    ins = nc.tensor.matmul(bank(c, k)[0:STATE, :], c.w_b[:, b, :], u[:, b, k * CHUNK:(k + 1) * CHUNK],
                                           start=(b == 0), stop=(b == blocks - 1))
                ins.then_inc(bu_ready.sem, 1)
            pe.wait_ge(*state_ready.after(1))
            for b in range(blocks):
                for k in range(CHUNKS):
                    nc.tensor.matmul(bank(c, b * CHUNKS + k), c.w_c[:, b * P:(b + 1) * P],
                                     c.state[0:STATE, k * CHUNK:(k + 1) * CHUNK], start=True, stop=True).then_inc(y_ready.sem, 1)
            pe.wait_ge(*y_taken.after(blocks * CHUNKS))
            for t in range(TILES):
                for b in range(blocks):
                    ins = nc.tensor.matmul(bank(c, t // TPC)[:, (t % TPC) * P:(t % TPC + 1) * P],
                                           u[:, b, t * P:(t + 1) * P], c.w_out[:, b, :], start=(b == 0), stop=(b == blocks - 1))
                if t % TPC == TPC - 1:
                    ins.then_inc(out_ready.sem, 1)

        @block.scalar
        def _(act):
            for n in range(2 * blocks * CHUNKS):
                b, k = n // CHUNKS, n % CHUNKS
                act.wait_ge(*proj_ready.after(n + 1))
                if b < blocks:
                    out = xin[:, b, k * CHUNK:(k + 1) * CHUNK]
                    nc.scalar.activation(out, bank(c, n % 8), ACT.Copy).then_inc(proj_taken.sem, 1)
                else:
                    out = gate[:, b - blocks, k * CHUNK:(k + 1) * CHUNK]
                    nc.scalar.activation(out, bank(c, n % 8), ACT.Silu).then_inc(proj_taken.sem, 1)
            for b in range(blocks):
                act.wait_ge(*conv_ready.after(b + 1))
                nc.scalar.activation(u[:, b, :], c.conv[:, b, :], ACT.Silu).then_inc(u_ready.sem, 1)
            for k in range(CHUNKS):
                act.wait_ge(*bu_ready.after(k + 1))
                nc.scalar.activation(c.bu[0:STATE, k * CHUNK:(k + 1) * CHUNK], bank(c, k)[0:STATE, :], ACT.Copy,
                                     scale=0.05).then_inc(bu_taken.sem, 1)

        @block.vector
        def _(dve):
            chain = Chain(dve, chain_s)
            chain.link(nc.vector.memset(c.decay[:], 0.95))
            for b in range(blocks):
                dve.wait_ge(*proj_taken.after((b + 1) * CHUNKS))
                chain.link(nc.vector.tensor_scalar(c.conv[:, b, :], xin[:, b, :], c.conv_w[:, b, PAD:TAPS],
                                                   c.columns["L0_attn_a_conv_b"][:, b:b + 1], ALU.mult, ALU.add))
                for back in range(1, TAPS):
                    tail = c.conv[:, b, back:N_TOK]
                    ins = nc.vector.scalar_tensor_tensor(tail, xin[:, b, 0:N_TOK - back], c.conv_w[:, b, PAD - back:TAPS - back],
                                                         tail, ALU.mult, ALU.add)
                    if back < PAD:
                        chain.link(ins)
                ins.then_inc(conv_ready.sem, 1)
            dve.wait_ge(*bu_taken.after(CHUNKS))
            nc.vector.tensor_tensor_scan(c.state[0:STATE, :], c.decay[0:STATE, 0:1].broadcast_to((STATE, N_TOK)),
                                         c.bu[0:STATE, :], 0.0, ALU.mult, ALU.add).then_inc(state_ready.sem, 1)
            for b in range(blocks):
                for k in range(CHUNKS):
                    part = u[:, b, k * CHUNK:(k + 1) * CHUNK]
                    dve.wait_ge(*y_ready.after(b * CHUNKS + k + 1))
                    chain.link(nc.vector.scalar_tensor_tensor(part, part, c.columns["L0_attn_a_D_param"][:, b:b + 1],
                                                              bank(c, b * CHUNKS + k), ALU.mult, ALU.add))
                    nc.vector.tensor_tensor(part, part, gate[:, b, k * CHUNK:(k + 1) * CHUNK],
                                            ALU.mult).then_inc(y_taken.sem, 1)
            for k in range(CHUNKS):
                dve.wait_ge(*out_ready.after(k + 1))
                tiles = c.h[:, k * TPC:(k + 1) * TPC, :]
                nc.vector.tensor_tensor(tiles, tiles, bank(c, k).rearrange("p (t d) -> p t d", d=D), ALU.add).then_inc(added.sem, 1)
            links[0] = chain.n

    chain_s.passed(links[0])
    proj_ready.passed(2 * blocks * CHUNKS)
    proj_taken.passed(2 * blocks * CHUNKS)
    conv_ready.passed(blocks)
    u_ready.passed(blocks)
    bu_ready.passed(CHUNKS)
    bu_taken.passed(CHUNKS)
    state_ready.passed(1)
    y_ready.passed(blocks * CHUNKS)
    y_taken.passed(blocks * CHUNKS)
    out_ready.passed(CHUNKS)
    added.passed(CHUNKS)


def add_stage(c, dst, *terms, row=None, scale_row=None):
    nc = c.nc
    chain_s = c.count("dve_chain")
    links = [0]

    def along(r):
        return r.rearrange("p (o d) -> p o d", o=1).broadcast_to((P, TILES, D))

    with nc.Block() as block:
        @block.vector
        def _(dve):
            chain = Chain(dve, chain_s)
            for term in terms:
                if scale_row is not None:
                    chain.link(nc.vector.tensor_tensor(term[:], term[:], along(scale_row), ALU.mult))
                chain.link(nc.vector.tensor_tensor(dst[:], dst[:], term[:], ALU.add))
            if row is not None:
                chain.link(nc.vector.tensor_tensor(dst[:], dst[:], along(row), ALU.add))
            links[0] = chain.n
    chain_s.passed(links[0])


def hologram_stage(c):
    nc = c.nc
    written = c.count("holo_keys_written")
    circ_loaded = c.count("holo_circ_loaded")
    decay_ready = c.count("holo_decay_ready")
    scan_ready = c.count("holo_scan_ready")
    unbind_ready = c.count("holo_unbind_ready")
    unbind_taken = c.count("holo_unbind_taken")
    map_ready = c.count("holo_map_ready")
    map_taken = c.count("holo_map_taken")
    out_ready = c.count("holo_out_ready")
    added = c.count("holo_added")
    with nc.Block() as block:

        @block.sync
        def _(sp):
            sp.dma_start(c.keys_dram, c.keys_twice[0:2, :]).then_inc(written.sem, 16)
            sp.wait_ge(*written.after(16))
            for s in range(2):
                src = bass.AP(c.keys_dram.tensor, s * 2 * D, [[1, D], [1, D]])
                sp.dma_start(c.circ[:, s, :], src).then_inc(circ_loaded.sem, 16)

        @block.scalar
        def _(act):
            nc.scalar.activation(c.decay[:], c.rows["L1_attn_b_decay"], ACT.Sigmoid).then_inc(decay_ready.sem, 1)

        @block.tensor
        def _(pe):
            pe.wait_ge(*circ_loaded.after(32))
            nc.tensor.matmul(bank(c, 0, P), c.circ[:, 1, :], c.flip[:], start=True, stop=True).then_inc(unbind_ready.sem, 1)
            pe.wait_ge(*unbind_taken.after(1))
            nc.tensor.matmul(bank(c, 1, P), c.circ[:, 0, :], c.circ_a[:], start=True, stop=True).then_inc(unbind_ready.sem, 1)
            pe.wait_ge(*unbind_taken.after(2))
            nc.tensor.matmul(bank(c, 2, P), c.flip[:], c.circ_b[:], start=True, stop=True).then_inc(map_ready.sem, 1)
            pe.wait_ge(*map_taken.after(1))
            pe.wait_ge(*scan_ready.after(1))
            for t in range(TILES):
                ins = nc.tensor.matmul(bank(c, 4 + t // TPC)[:, (t % TPC) * P:(t % TPC + 1) * P],
                                       c.big[:, 0, t * P:(t + 1) * P], c.circ_a[:], start=True, stop=True)
                if t % TPC == TPC - 1:
                    ins.then_inc(out_ready.sem, 1)

        @block.vector
        def _(dve):
            dve.wait_ge(*unbind_ready.after(1))
            nc.vector.tensor_copy(c.circ_a[:], bank(c, 0, P)).then_inc(unbind_taken.sem, 1)
            dve.wait_ge(*unbind_ready.after(2))
            nc.vector.tensor_copy(c.circ_b[:], bank(c, 1, P)).then_inc(unbind_taken.sem, 1)
            dve.wait_ge(*map_ready.after(1))
            nc.vector.tensor_scalar(c.circ_a[:], bank(c, 2, P), c.rows["L1_attn_b_gate"], None, ALU.mult).then_inc(map_taken.sem, 1)
            dve.wait_ge(*decay_ready.after(1))
            nc.vector.tensor_tensor_scan(c.big[:, 0, :], c.decay[:, 0:1].broadcast_to((P, N_TOK)), c.ht[:], 0.0,
                                         ALU.mult, ALU.add).then_inc(scan_ready.sem, 1)
            for k in range(CHUNKS):
                dve.wait_ge(*out_ready.after(k + 1))
                tiles = c.h[:, k * TPC:(k + 1) * TPC, :]
                nc.vector.tensor_tensor(tiles, tiles, bank(c, 4 + k).rearrange("p (t d) -> p t d", d=D), ALU.add).then_inc(added.sem, 1)

    for s, n in ((written, 16), (circ_loaded, 32), (decay_ready, 1), (scan_ready, 1), (unbind_ready, 2),
                 (unbind_taken, 2), (map_ready, 1), (map_taken, 1), (out_ready, CHUNKS), (added, CHUNKS)):
        s.passed(n)


def project_stage(c, w, bq=None, bk=None, bv=None):
    nc = c.nc
    qk_ready = c.count("proj_qk_ready")
    q_taken = c.count("proj_q_taken")
    k_taken = c.count("proj_k_taken")
    v_ready = c.count("proj_v_ready")
    v_taken = c.count("proj_v_taken")
    q_split = c.count("proj_q_split")
    k_split = c.count("proj_k_split")
    stored = c.count("proj_parts_stored")
    SPLIT_STEPS = 3
    with nc.Block() as block:

        @block.tensor
        def _(pe):
            for n in range(2):
                for k in range(CHUNKS):
                    nc.tensor.matmul(bank(c, n * CHUNKS + k), c.proj[:, w + n, :], c.ht[:, k * CHUNK:(k + 1) * CHUNK],
                                     start=True, stop=True).then_inc(qk_ready.sem, 1)
            for t in range(TILES):
                if t % TPC == 0:
                    pe.wait_ge(*q_taken.after(2 * (t // TPC + 1)))
                ins = nc.tensor.matmul(bank(c, t // TPC)[:, (t % TPC) * P:(t % TPC + 1) * P], c.ht[:, t * P:(t + 1) * P],
                                       c.proj[:, w + 2, :], start=True, stop=True)
                if t % TPC == TPC - 1:
                    ins.then_inc(v_ready.sem, 1)

        @block.scalar
        def _(act):
            for n, (b, taken) in enumerate(((bq, q_taken), (bk, k_taken))):
                for k in range(CHUNKS):
                    cols = slice(k * CHUNK, (k + 1) * CHUNK)
                    act.wait_ge(*qk_ready.after(n * CHUNKS + k + 1))
                    for out in (c.big[:, n, cols], c.parts[:, n, 0, cols]):
                        nc.scalar.activation(out, bank(c, n * CHUNKS + k), ACT.Identity,
                                             bias=b if b is not None else 0.0).then_inc(taken.sem, 1)
            for k in range(CHUNKS):
                act.wait_ge(*v_ready.after(k + 1))
                nc.scalar.activation(c.v[:, k * TPC:(k + 1) * TPC, :].rearrange("p t d -> p (t d)"), bank(c, k),
                                     ACT.Copy).then_inc(v_taken.sem, 1)

        @block.vector
        def _(dve):
            for n, (taken, split_done) in enumerate(((q_taken, q_split), (k_taken, k_split))):
                for k in range(CHUNKS):
                    cols = slice(k * CHUNK, (k + 1) * CHUNK)
                    x, part = c.big[:, n, cols], c.parts[:, n, :, cols]
                    dve.wait_ge(*taken.after(2 * (k + 1)))
                    nc.vector.tensor_tensor(x, x, part[:, 0, :], ALU.subtract).then_inc(split_done.sem, 1)
                    dve.wait_ge(*split_done.after(SPLIT_STEPS * k + 1))
                    nc.vector.tensor_copy(part[:, 1, :], x).then_inc(split_done.sem, 1)
                    dve.wait_ge(*split_done.after(SPLIT_STEPS * k + 2))
                    nc.vector.tensor_tensor(part[:, 2, :], x, part[:, 1, :], ALU.subtract).then_inc(split_done.sem, 1)
            if bv is not None:
                dve.wait_ge(*v_taken.after(CHUNKS))
                nc.vector.tensor_tensor(c.v[:], c.v[:], bv.rearrange("p (o d) -> p o d", o=1).broadcast_to((P, TILES, D)),
                                        ALU.add)

        @block.sync
        def _(sp):
            for n, ready in enumerate((q_split, k_split)):
                for k in range(CHUNKS):
                    cols = slice(k * CHUNK, (k + 1) * CHUNK)
                    sp.wait_ge(*ready.after(SPLIT_STEPS * (k + 1)))
                    sp.dma_start(c.parts_dram[n, :, :, cols].rearrange("s p n -> p s n"), c.parts[:, n, :, cols])\
                        .then_inc(stored.sem, 16)
            sp.wait_ge(*stored.after(2 * CHUNKS * 16))

    qk_ready.passed(2 * CHUNKS)
    q_taken.passed(2 * CHUNKS)
    k_taken.passed(2 * CHUNKS)
    v_ready.passed(CHUNKS)
    v_taken.passed(CHUNKS)
    q_split.passed(CHUNKS * SPLIT_STEPS)
    k_split.passed(CHUNKS * SPLIT_STEPS)
    stored.passed(2 * CHUNKS * 16)


def heads_stage(c, window=None):
    nc = c.nc
    stack_loaded = [c.count(f"head_stack_loaded_{p}") for p in range(2)]
    stack_copied = [c.count(f"head_stack_copied_{p}") for p in range(2)]
    v_staged = c.count("head_v_staged")
    max_ready = c.count("head_max_scores_ready")
    max_taken = c.count("head_max_scores_taken")
    shift_ready = c.count("head_shift_rows_ready")
    shift_taken = c.count("head_shift_rows_taken")
    st_ready = c.count("head_scores_ready")
    exp_done = c.count("head_exp_done")
    pv_done = c.count("head_pv_done")
    out_taken = c.count("head_out_taken")
    out_stored = [c.count(f"head_out_stored_{p}") for p in range(2)]
    small = c.count("head_small_steps")
    full = window is None
    scale = float(HD) ** -0.5
    MAX_UNITS = TILES * CHUNKS if full else TILES // 2
    EXP_UNITS = TILES * N_TOK // UNIT if full else TILES * 2 * P // UNIT
    PV_STEPS = TILES if full else 1
    LOADS = 2 * PARTS
    COPIES = 2
    SMALL = 5

    def step_tensor(pe, p, i, with_max, with_exp):
        s = 2 * i + p

        def max_unit(w):
            out = bank(c, 4 + w % 2)
            if w >= 2:
                pe.wait_ge(*max_taken.after(s * MAX_UNITS + (w - 1)))
            elif type(s) is not int or s > 0:
                pe.wait_ge(*max_taken.after(s * MAX_UNITS + (w - 1)))
            if full:
                t, k = w // CHUNKS, w % CHUNKS
                ins = nc.tensor.matmul(out, c.q_max[:, p, t * P:(t + 1) * P], c.k_max[:, p, k * CHUNK:(k + 1) * CHUNK],
                                       start=True, stop=True)
            else:
                for j in range(2):
                    t = 2 * w + j
                    half = out[:, j * 2 * P:(j + 1) * 2 * P]
                    nc.tensor.matmul(half, c.ident16[:], c.mask_q[:, window, 1 if t == 0 else 0, :], start=True, stop=False)
                    if t == 0:
                        ins = nc.tensor.matmul(half[:, P:2 * P], c.q_max[:, p, 0:P], c.k_max[:, p, 0:P], start=False, stop=True)
                    else:
                        ins = nc.tensor.matmul(half, c.q_max[:, p, t * P:(t + 1) * P], c.k_max[:, p, (t - 1) * P:(t + 1) * P],
                                               start=False, stop=True)
            ins.then_inc(max_ready.sem, 1)

        def exp_unit(u):
            q, k_ = c.q_exp[:, 1 - p], c.k_exp[:, 1 - p]
            done = (s - 1) * EXP_UNITS + (u - 1)
            if u >= 2 or type(s) is not int or s > 1:
                pe.wait_ge(*exp_done.after(done))
            chunks = (2, 4)[u] if full and u < 2 else min(u + 2, CHUNKS) if not full else 0
            if chunks:
                pe.wait_ge(*shift_taken.after((s - 1) * CHUNKS + chunks))
            at = 2 * (u % 2)
            if full:
                kb, half = u // 2, u % 2
                for j in range(2):
                    col = half * UNIT + j * CHUNK
                    ins = nc.tensor.matmul(bank(c, at + j), k_[:, kb * P:(kb + 1) * P], q[:, col:col + CHUNK],
                                           start=True, stop=True)
            else:
                for j in range(4):
                    kb = 4 * u + j
                    width = 2 * P if kb < TILES - 1 else P
                    out = c.ps[:, at * CHUNK + j * 2 * P:at * CHUNK + j * 2 * P + width]
                    nc.tensor.matmul(out, c.ident16[:], c.mask_k[:, window, 0:width], start=True, stop=False)
                    ins = nc.tensor.matmul(out, k_[:, kb * P:(kb + 1) * P], q[:, kb * P:kb * P + width], start=False, stop=True)
            ins.then_inc(st_ready.sem, 1)

        def pv_step(kb):
            v = c.v_head[:, 1 - p]
            for g in range(4):
                out = c.ps[OUT_ROWS * g:OUT_ROWS * (g + 1), 6 * CHUNK:7 * CHUNK]
                unit = c.prob[:, (2 * kb + g // 2) % P_UNITS, (g % 2) * CHUNK:(g % 2 + 1) * CHUNK]
                ins = nc.tensor.matmul(out, v[:, kb, :], unit, start=(kb == 0), stop=(kb == TILES - 1), skip_group_check=True)
            ins.then_inc(pv_done.sem, 1)

        def pv_window():
            v = c.v_head[:, 1 - p]
            half = EXP_UNITS * (1 - p)
            for j in range(TPC):
                if with_max and j >= 2:
                    shift_rows(pe, s, j - 2)
                for own in range(2):
                    for g in range(4):
                        t = TPC * g + j
                        kb = t if own else t - 1
                        if kb < 0:
                            continue
                        col = (kb % 4) * 2 * P + (0 if own else P)
                        first = j == 0 and (own == 0 or t == 0)
                        ins = nc.tensor.matmul(c.ps[OUT_ROWS * g:OUT_ROWS * (g + 1), 6 * CHUNK + j * P:6 * CHUNK + (j + 1) * P],
                                               v[:, kb, :], c.prob[:, half + kb // 4, col:col + P],
                                               start=first, stop=(own == 1), skip_group_check=True)
            ins.then_inc(pv_done.sem, 1)
            if with_max:
                shift_rows(pe, s, 2)
                shift_rows(pe, s, 3)

        w = 0
        if with_max:
            pe.wait_ge(*stack_loaded[p].after((i + 1) * LOADS * 16))
        if with_exp:
            pe.wait_ge(*stack_copied[1 - p].after((i + p) * COPIES * 16))
        if with_exp and full:
            for kb in range(TILES + 1):
                todo = ["max"] + ["exp", "max"] * 2 if kb < TILES else []
                todo += (["pv", "max"] if kb else []) + (["max"] if kb % 2 else [])
                half = 0
                for what in todo:
                    if what == "exp":
                        exp_unit(2 * kb + half)
                        if with_max and kb == TILES - 1:
                            shift_rows(pe, s, half)
                        half += 1
                    elif what == "pv":
                        pv_wait(pe, s, kb - 1)
                        pv_step(kb - 1)
                        if with_max and kb >= TILES - 1:
                            shift_rows(pe, s, 2 + kb - (TILES - 1))
                    elif with_max and w < MAX_UNITS:
                        max_unit(w)
                        w += 1
            assert w == (MAX_UNITS if with_max else 0)
        elif with_exp:
            for u in range(EXP_UNITS):
                if with_max:
                    max_unit(2 * u)
                    max_unit(2 * u + 1)
                exp_unit(u)
            pv_wait(pe, s, 0)
            pv_window()
        else:
            for w in range(MAX_UNITS):
                max_unit(w)
            for k in range(CHUNKS):
                shift_rows(pe, s, k)

    def shift_rows(pe, s, k):
        if k == 0:
            pe.wait_ge(*small.after((s + 1) * SMALL))
        if k or type(s) is not int or s:
            pe.wait_ge(*shift_taken.after(s * CHUNKS + k))
        for j in range(TPC):
            ins = nc.tensor.matmul(c.ps[SHIFT_AT:SHIFT_AT + PARTS, 7 * CHUNK + j * P:7 * CHUNK + (j + 1) * P],
                                   c.shift[:, :, k * TPC + j], c.ident16[:], start=True, stop=True)
        ins.then_inc(shift_ready.sem, 1)

    def take_shift(act, p, s, k):
        act.wait_ge(*shift_ready.after(s * CHUNKS + k + 1))
        nc.scalar.activation(c.q_exp[SHIFT_AT:SHIFT_AT + PARTS, p, k * CHUNK:(k + 1) * CHUNK],
                             c.ps[SHIFT_AT:SHIFT_AT + PARTS, 7 * CHUNK:8 * CHUNK], ACT.Copy).then_inc(shift_taken.sem, 1)

    def pv_wait(pe, s, kb):
        if kb == 0:
            pe.wait_ge(*v_staged.after(s))
            if type(s) is not int or s > 1:
                pe.wait_ge(*out_taken.after(s - 1))
        units = 2 * (kb + 1) if full else EXP_UNITS
        pe.wait_ge(*exp_done.after((s - 1) * EXP_UNITS + units))

    def step_scalar(act, p, i, with_max, with_exp):
        s = 2 * i + p
        if not with_exp:
            for k in range(CHUNKS):
                take_shift(act, p, s, k)
            return
        for u in range(EXP_UNITS):
            act.wait_ge(*st_ready.after((s - 1) * EXP_UNITS + u + 1))
            if full:
                buf = u % P_UNITS
                if u >= P_UNITS or type(s) is not int or s > 1:
                    act.wait_ge(*pv_done.after((s - 1) * PV_STEPS + (u - P_UNITS) // 2 + 1))
            else:
                buf = EXP_UNITS * (1 - p) + u
                if type(s) is not int or s > 2:
                    act.wait_ge(*pv_done.after(s - 2))
            width = UNIT if full or u < EXP_UNITS - 1 else UNIT - P
            nc.scalar.activation(c.prob[:, buf, 0:width], c.ps[:, 2 * (u % 2) * CHUNK:2 * (u % 2) * CHUNK + width],
                                 ACT.Exp, scale=scale).then_inc(exp_done.sem, 1)
            if full and with_max and u >= EXP_UNITS - 2:
                take_shift(act, p, s, u - (EXP_UNITS - 2))
        if with_max:
            for k in range(2 if full else 0, CHUNKS):
                take_shift(act, p, s, k)

    def step_vector(dve, p, i, with_max, with_exp):
        s = 2 * i + p
        if with_max:
            for w in range(MAX_UNITS):
                dve.wait_ge(*max_ready.after(s * MAX_UNITS + w + 1))
                if full:
                    nc.vector.reduce_max(c.mx[:, w // CHUNKS, w % CHUNKS:w % CHUNKS + 1], bank(c, 4 + w % 2), AX.X)\
                        .then_inc(max_taken.sem, 1)
                else:
                    nc.vector.reduce_max(c.mx[:, 2 * w:2 * w + 2, 0], bank(c, 4 + w % 2).rearrange("p (a n) -> p a n", a=2), AX.X)\
                        .then_inc(max_taken.sem, 1)
            dve.wait_ge(*max_taken.after((s + 1) * MAX_UNITS))
            cols = CHUNKS if full else 1
            base = s * SMALL
            nc.vector.tensor_reduce(c.rowmax[:], c.mx[:, :, 0:cols], AX.X, ALU.max, negate=True).then_inc(small.sem, 1)
            dve.wait_ge(*small.after(base + 1))
            if type(s) is not int or s > 0:
                dve.wait_ge(*shift_ready.after(s * CHUNKS))
            nc.vector.tensor_copy(c.shift[:, 0, :], c.rowmax[:]).then_inc(small.sem, 1)
            dve.wait_ge(*small.after(base + 2))
            nc.vector.tensor_tensor(c.rowmax[:], c.rowmax[:], c.shift[:, 0, :], ALU.subtract).then_inc(small.sem, 1)
            dve.wait_ge(*small.after(base + 3))
            nc.vector.tensor_copy(c.shift[:, 1, :], c.rowmax[:]).then_inc(small.sem, 1)
            dve.wait_ge(*small.after(base + 4))
            nc.vector.tensor_tensor(c.shift[:, 2, :], c.rowmax[:], c.shift[:, 1, :], ALU.subtract).then_inc(small.sem, 1)
        if with_exp:
            dve.wait_ge(*pv_done.after(s * PV_STEPS))
            if type(s) is not int or s > 2:
                dve.wait_ge(*out_stored[1 - p].after((i - 1 + p) * 16))
            nc.vector.tensor_copy(c.out_head[:, 1 - p, :], bank(c, 6)).then_inc(out_taken.sem, 1)

    def step_pool(pool, p, i):
        s = 2 * i + p
        if type(s) is not int or s > 1:
            pool.wait_ge(*pv_done.after((s - 1) * PV_STEPS))
        cols = slice(s * HD, (s + 1) * HD) if type(s) is int else bass.ds(s * HD, HD)
        pool.tensor_copy(c.v_head[:, p, :, 0:HD], c.v[:, :, cols]).then_inc(v_staged.sem, 1)

    def load_stacks(sp, p, i):
        s = 2 * i + p
        if type(s) is not int or s > 1:
            sp.wait_ge(*st_ready.after((s - 2) * EXP_UNITS + 1))
        rows = slice(s * HD, (s + 1) * HD) if type(s) is int else bass.ds(s * HD, HD)
        q, k = (c.parts_dram[n, :, rows, :] for n in range(2))
        for a in range(PARTS):
            group = slice(a * PARTS * HD, (a + 1) * PARTS * HD)
            same = q[a:a + 1].broadcast_to((PARTS, HD, N_TOK))
            sp.dma_start(c.q_max[group, p, :], same).then_inc(stack_loaded[p].sem, 16)
            sp.dma_start(c.k_max[group, p, :], k).then_inc(stack_loaded[p].sem, 16)

    def copy_stacks(sp, p, i):
        s = 2 * i + p
        if type(s) is not int or s > 1:
            sp.wait_ge(*pv_done.after((s - 1) * PV_STEPS))
        sp.wait_ge(*stack_loaded[p].after((i + 1) * LOADS * 16))
        sp.dma_start(c.q_exp[0:STACK, p, :], c.q_max[0:STACK, p, :]).then_inc(stack_copied[p].sem, 16)
        sp.dma_start(c.k_exp[0:STACK, p, :], c.k_max[0:STACK, p, :]).then_inc(stack_copied[p].sem, 16)

    def store_out(pool, p, i):
        s = 2 * i + p
        pool.wait_ge(*out_taken.after(s))
        dst = c.out_dram[s - 1] if type(s) is int else c.out_dram[bass.ds(s - 1, 1)].rearrange("o p n -> (o p) n")
        pool.dma_start(dst, c.out_head[:, 1 - p, :]).then_inc(out_stored[1 - p].sem, 16)

    with nc.Block() as block:

        @block.tensor
        def _(pe):
            step_tensor(pe, 0, 0, True, False)
            step_tensor(pe, 1, 0, True, True)
            with pe.Fori(1, HEADS // 2) as i:
                step_tensor(pe, 0, i, True, True)
                step_tensor(pe, 1, i, True, True)
            step_tensor(pe, 0, HEADS // 2, False, True)

        @block.scalar
        def _(act):
            step_scalar(act, 0, 0, True, False)
            step_scalar(act, 1, 0, True, True)
            with act.Fori(1, HEADS // 2) as i:
                step_scalar(act, 0, i, True, True)
                step_scalar(act, 1, i, True, True)
            step_scalar(act, 0, HEADS // 2, False, True)

        @block.vector
        def _(dve):
            step_vector(dve, 0, 0, True, False)
            step_vector(dve, 1, 0, True, True)
            with dve.Fori(1, HEADS // 2) as i:
                step_vector(dve, 0, i, True, True)
                step_vector(dve, 1, i, True, True)
            step_vector(dve, 0, HEADS // 2, False, True)

        @block.gpsimd
        def _(pool):
            step_pool(pool, 0, 0)
            step_pool(pool, 1, 0)
            store_out(pool, 1, 0)
            with pool.Fori(1, HEADS // 2) as i:
                step_pool(pool, 0, i)
                store_out(pool, 0, i)
                step_pool(pool, 1, i)
                store_out(pool, 1, i)
            store_out(pool, 0, HEADS // 2)
            for p in range(2):
                pool.wait_ge(*out_stored[p].after(HEADS // 2 * 16))

        @block.sync
        def _(sp):
            load_stacks(sp, 0, 0)
            load_stacks(sp, 1, 0)
            copy_stacks(sp, 0, 0)
            with sp.Fori(1, HEADS // 2) as i:
                load_stacks(sp, 0, i)
                copy_stacks(sp, 1, i - 1)
                load_stacks(sp, 1, i)
                copy_stacks(sp, 0, i)
            copy_stacks(sp, 1, HEADS // 2 - 1)

    for p in range(2):
        stack_loaded[p].passed(HEADS // 2 * LOADS * 16)
        stack_copied[p].passed(HEADS // 2 * COPIES * 16)
        out_stored[p].passed(HEADS // 2 * 16)
    for sig, n in ((v_staged, HEADS), (max_ready, HEADS * MAX_UNITS),
                   (max_taken, HEADS * MAX_UNITS), (shift_ready, HEADS * CHUNKS),
                   (shift_taken, HEADS * CHUNKS), (small, HEADS * SMALL),
                   (st_ready, HEADS * EXP_UNITS),
                   (exp_done, HEADS * EXP_UNITS), (pv_done, HEADS * PV_STEPS), (out_taken, HEADS)):
        sig.passed(n)


def output_stage(c, w, dst):
    nc = c.nc
    fetched = c.count("out_fetched")
    inverse = c.count("out_inverse")
    ctx_ready = c.count("out_ctx_ready")
    out_ready = c.count("out_ready")
    added = c.count("out_added")
    with nc.Block() as block:

        @block.sync
        def _(sp):
            for k in range(CHUNKS):
                for n in range(2):
                    at = OUT_ROWS * k + n * HD
                    sp.dma_start(c.big[:, n, k * CHUNK:(k + 1) * CHUNK], c.out_dram[:, at:at + HD, :])\
                        .then_inc(fetched.sem, 16)

        @block.vector
        def _(dve):
            dve.wait_ge(*fetched.after(2 * CHUNKS * 16))
            for k in range(CHUNKS):
                num, den = (c.big[:, n, k * CHUNK:(k + 1) * CHUNK] for n in range(2))
                nc.vector.reciprocal(den, den).then_inc(inverse.sem, 1)
                dve.wait_ge(*inverse.after(k + 1))
                nc.vector.tensor_tensor(num, num, den, ALU.mult).then_inc(ctx_ready.sem, 1)
            for k in range(CHUNKS):
                dve.wait_ge(*out_ready.after(k + 1))
                tiles = dst[:, k * TPC:(k + 1) * TPC, :]
                nc.vector.tensor_tensor(tiles, tiles, bank(c, k).rearrange("p (t d) -> p t d", d=D), ALU.add).then_inc(added.sem, 1)

        @block.tensor
        def _(pe):
            for t in range(TILES):
                if t % TPC == 0:
                    pe.wait_ge(*ctx_ready.after(t // TPC + 1))
                ins = nc.tensor.matmul(bank(c, t // TPC)[:, (t % TPC) * P:(t % TPC + 1) * P], c.big[:, 0, t * P:(t + 1) * P],
                                       c.proj[:, w + 3, :], start=True, stop=True)
                if t % TPC == TPC - 1:
                    ins.then_inc(out_ready.sem, 1)

    fetched.passed(2 * CHUNKS * 16)
    inverse.passed(CHUNKS)
    ctx_ready.passed(CHUNKS)
    out_ready.passed(CHUNKS)
    added.passed(CHUNKS)


def feed_forward_stage(c, dst):
    nc = c.nc
    up_ready = c.count("ff_up_ready")
    act_ready = c.count("ff_act_ready")
    out_ready = c.count("ff_out_ready")
    added = c.count("ff_added")
    blocks = D_FF // P
    with nc.Block() as block:

        @block.tensor
        def _(pe):
            def down(k):
                pe.wait_ge(*act_ready.after(blocks * (k + 1)))
                if k >= 2:
                    pe.wait_ge(*added.after(k - 1))
                for t in range(TPC):
                    for b in range(blocks):
                        ins = nc.tensor.matmul(bank(c, 4 + k % 2)[:, t * P:(t + 1) * P], c.hid[:, k % 2, b, t * P:(t + 1) * P],
                                               c.w2[:, b, :], start=(b == 0), stop=(b == blocks - 1))
                ins.then_inc(out_ready.sem, 1)

            for k in range(CHUNKS):
                for b in range(blocks):
                    n = k * blocks + b
                    if n >= 4:
                        pe.wait_ge(*act_ready.after(n - 3))
                    nc.tensor.matmul(bank(c, n % 4), c.w1[:, b * P:(b + 1) * P], c.ht[:, k * CHUNK:(k + 1) * CHUNK],
                                     start=True, stop=True).then_inc(up_ready.sem, 1)
                if k:
                    down(k - 1)
            down(CHUNKS - 1)

        @block.scalar
        def _(act):
            for n in range(CHUNKS * blocks):
                k, b = n // blocks, n % blocks
                act.wait_ge(*up_ready.after(n + 1))
                if k >= 2:
                    act.wait_ge(*out_ready.after(k - 1))
                nc.scalar.activation(c.hid[:, k % 2, b, :], bank(c, n % 4), ACT.Gelu_apprx_tanh,
                                     bias=c.columns["L0_attn_b_b1"][:, b:b + 1]).then_inc(act_ready.sem, 1)

        @block.vector
        def _(dve):
            for k in range(CHUNKS):
                dve.wait_ge(*out_ready.after(k + 1))
                tiles = dst[:, k * TPC:(k + 1) * TPC, :]
                nc.vector.tensor_tensor(tiles, tiles, bank(c, 4 + k % 2).rearrange("p (t d) -> p t d", d=D), ALU.add)\
                    .then_inc(added.sem, 1)

    up_ready.passed(CHUNKS * blocks)
    act_ready.passed(CHUNKS * blocks)
    out_ready.passed(CHUNKS)
    added.passed(CHUNKS)


def router_stage(c, router, experts, soft_of_probs):
    nc = c.nc
    logits_ready = c.count("router_logits_ready")
    chain_s = c.count("dve_chain")
    shifted_ready = c.count("router_shifted_ready")
    exp_ready = c.count("router_exp_ready")
    links = [0]
    E = experts
    with nc.Block() as block:

        @block.tensor
        def _(pe):
            for t in range(TILES):
                ins = nc.tensor.matmul(bank(c, 0)[:, t * 16:t * 16 + E], c.ht[:, t * P:(t + 1) * P], router[:, 0:E],
                                       start=True, stop=True)
            ins.then_inc(logits_ready.sem, 1)

        @block.scalar
        def _(act):
            act.wait_ge(*shifted_ready.after(1))
            nc.scalar.activation(c.probs[:, :, 0:E], c.logits[:, :, 0:E], ACT.Exp).then_inc(exp_ready.sem, 1)
            act.wait_ge(*shifted_ready.after(2))
            nc.scalar.activation(c.top_gap[:], c.top_gap[:], ACT.Exp).then_inc(exp_ready.sem, 1)

        @block.vector
        def _(dve):
            chain = Chain(dve, chain_s)
            v = nc.vector
            logits = c.logits[:, :, 0:E]

            def wide(a):
                return a.broadcast_to((P, TILES, E))

            dve.wait_ge(*logits_ready.after(1))
            chain.link(v.tensor_copy(logits, bank(c, 0, TILES * 16).rearrange("p (t e) -> p t e", e=16)[:, :, 0:E]))
            for t in range(TILES):
                ins = v.max(c.top[:, t, :], c.logits[:, t, 0:E])
            chain.link(ins)
            for t in range(TILES):
                ins = v.max_index(c.top_i[:, t, :], c.top[:, t, :], c.logits[:, t, 0:E])
            chain.link(ins)
            chain.link(v.tensor_copy(c.top_f[:], c.top_i[:, :, 0:2]))
            v.tensor_tensor(logits, logits, wide(c.top[:, :, 0:1]), ALU.subtract).then_inc(shifted_ready.sem, 1)
            if soft_of_probs:
                dve.wait_ge(*exp_ready.after(1))
                chain.link(v.reduce_sum(c.total[:], c.probs[:, :, 0:E], AX.X))
                chain.link(v.reciprocal(c.total[:], c.total[:]))
                for_second = c.second[:]
                chain.link(v.tensor_tensor(c.pick[:, :, 0:E], c.ids_wide(E), wide(c.top_f[:, :, 1:2]), ALU.is_equal))
                chain.link(v.tensor_tensor(c.pick[:, :, 0:E], c.pick[:, :, 0:E], c.probs[:, :, 0:E], ALU.mult))
                chain.link(v.reduce_sum(for_second, c.pick[:, :, 0:E], AX.X))
                chain.link(v.tensor_scalar(for_second, for_second, 1.0, None, ALU.subtract))
                v.tensor_tensor(c.top_gap[:], for_second, c.total[:], ALU.mult).then_inc(shifted_ready.sem, 1)
            else:
                v.tensor_tensor(c.top_gap[:], c.top[:, :, 1], c.top[:, :, 0], ALU.subtract).then_inc(shifted_ready.sem, 1)
            dve.wait_ge(*exp_ready.after(2))
            chain.link(v.tensor_scalar(c.total[:], c.top_gap[:], 1.0, None, ALU.add))
            chain.link(v.reciprocal(c.total[:], c.total[:]))
            chain.link(v.tensor_tensor(c.second[:], c.top_gap[:], c.total[:], ALU.mult))
            out = c.cw[:, 0:E, :].rearrange("p e t -> p t e")
            for n, weight in enumerate((c.total, c.second)):
                chain.link(v.tensor_tensor(c.pick[:, :, 0:E], c.ids_wide(E), wide(c.top_f[:, :, n:n + 1]), ALU.is_equal))
                w3 = wide(weight[:].rearrange("p (t o) -> p t o", o=1))
                chain.link(v.tensor_tensor(c.probs[:, :, 0:E] if n else out, c.pick[:, :, 0:E], w3, ALU.mult))
            chain.link(v.tensor_tensor(out, out, c.probs[:, :, 0:E], ALU.add))
            links[0] = chain.n

    logits_ready.passed(1)
    shifted_ready.passed(2)
    exp_ready.passed(2)
    chain_s.passed(links[0])


def experts_stage(c, gate_w, up_w, down_w, inner, last=None):
    nc = c.nc
    weights_loaded = [c.count(f"moe_weights_loaded_{p}") for p in range(2)]
    cw_staged = c.count("moe_cw_staged")
    pair_ready = c.count("moe_gate_up_ready")
    gate_taken = c.count("moe_gate_taken")
    hid_ready = c.count("moe_hidden_ready")
    out_ready = c.count("moe_out_ready")
    out_added = c.count("moe_out_added")
    J = (inner + P - 1) // P
    sizes = [min(P, inner - j * P) for j in range(J)]
    whole = inner // P
    LOADS = 3 + (1 if inner % P else 0)

    def load(sp, p, n, src=None):
        if type(n) is not int or n > 1:
            sp.wait_ge(*out_ready.after((n - 1) * CHUNKS))
        if src is None:
            if type(n) is int:
                g, u, d = gate_w[n], up_w[n], down_w[n]
            else:
                g, u, d = (a[bass.ds(n, 1)].rearrange("o a b -> (o a) b") for a in (gate_w, up_w, down_w))
        else:
            g, u, d = src
        sp.dma_start(c.wg[:, p, 0:inner], g).then_inc(weights_loaded[p].sem, 16)
        sp.dma_start(c.wu[:, p, 0:inner], u).then_inc(weights_loaded[p].sem, 16)
        sp.dma_start(c.wd[:, p, 0:whole, :], d[0:whole * P, :].rearrange("(j p) d -> p j d", p=P)).then_inc(weights_loaded[p].sem, 16)
        if inner % P:
            sp.dma_start(c.wd[0:inner % P, p, whole, :], d[whole * P:inner, :]).then_inc(weights_loaded[p].sem, 16)

    def expert_tensor(pe, p, i):
        n = 2 * i + p
        pe.wait_ge(*weights_loaded[p].after((i + 1) * LOADS * 16))

        def up(k):
            for j in range(J):
                unit = k * J + j
                b = unit % 2
                if unit >= 2 or type(n) is not int or n > 0:
                    pe.wait_ge(*hid_ready.after((n * CHUNKS) * J + unit - 1))
                m = sizes[j]
                cols = slice(j * P, j * P + m)
                nc.tensor.matmul(bank(c, b)[0:m], c.wg[:, p, cols], c.ht[:, k * CHUNK:(k + 1) * CHUNK], start=True, stop=True)
                nc.tensor.matmul(bank(c, 2 + b)[0:m], c.wu[:, p, cols], c.ht[:, k * CHUNK:(k + 1) * CHUNK],
                                 start=True, stop=True).then_inc(pair_ready.sem, 1)

        def down(k):
            pe.wait_ge(*hid_ready.after((n * CHUNKS + k + 1) * J))
            if k >= 2 or type(n) is not int or n > 0:
                pe.wait_ge(*out_added.after(n * CHUNKS + k - 1))
            for t in range(TPC):
                for j in range(J):
                    m = sizes[j]
                    ins = nc.tensor.matmul(bank(c, 4 + k % 2)[:, t * P:(t + 1) * P], c.hid[0:m, k % 2, j, t * P:(t + 1) * P],
                                           c.wd[0:m, p, j, :], start=(j == 0), stop=(j == J - 1))
            ins.then_inc(out_ready.sem, 1)
            return ins

        for k in range(CHUNKS):
            up(k)
            if k:
                down(k - 1)
        down(CHUNKS - 1)

    def expert_scalar(act, n):
        for k in range(CHUNKS):
            for j in range(J):
                unit = k * J + j
                m = sizes[j]
                act.wait_ge(*pair_ready.after(n * CHUNKS * J + unit + 1))
                if unit >= 2 or type(n) is not int or n > 0:
                    act.wait_ge(*hid_ready.after(n * CHUNKS * J + unit - 1))
                nc.scalar.activation(c.silu[0:m, unit % 2, :], bank(c, unit % 2)[0:m], ACT.Silu).then_inc(gate_taken.sem, 1)

    def expert_vector(dve, p, n, weighted=True):
        def add(k):
            dve.wait_ge(*out_ready.after(n * CHUNKS + k + 1))
            if k == 0 and weighted:
                dve.wait_ge(*cw_staged.after(n + 1))
            for t in range(TPC):
                tile = c.x[:, k * TPC + t, :]
                out = bank(c, 4 + k % 2)[:, t * P:(t + 1) * P]
                if weighted:
                    ins = nc.vector.scalar_tensor_tensor(tile, out, c.cw_now[:, p, k * TPC + t:k * TPC + t + 1], tile,
                                                         ALU.mult, ALU.add)
                else:
                    ins = nc.vector.tensor_tensor(tile, tile, out, ALU.add)
            ins.then_inc(out_added.sem, 1)

        for k in range(CHUNKS):
            for j in range(J):
                unit = k * J + j
                m = sizes[j]
                dve.wait_ge(*gate_taken.after(n * CHUNKS * J + unit + 1))
                if j == 0 and (k >= 2 or type(n) is not int or n > 0):
                    dve.wait_ge(*out_ready.after(n * CHUNKS + k - 1))
                nc.vector.tensor_tensor(c.hid[0:m, k % 2, j, :], c.silu[0:m, unit % 2, :], bank(c, 2 + unit % 2)[0:m],
                                        ALU.mult).then_inc(hid_ready.sem, 1)
            if k:
                add(k - 1)
        add(CHUNKS - 1)

    def expert_pool(pool, p, n):
        if type(n) is not int or n > 1:
            pool.wait_ge(*out_added.after((n - 1) * CHUNKS))
        src = c.cw[:, n, :] if type(n) is int else c.cw[:, bass.ds(n, 1), :].rearrange("p o t -> p (o t)")
        pool.tensor_copy(c.cw_now[:, p, :], src).then_inc(cw_staged.sem, 1)

    PAIRS = 4
    with nc.Block() as block:

        @block.sync
        def _(sp):
            load(sp, 0, 0)
            load(sp, 1, 1)
            with sp.Fori(1, PAIRS) as i:
                load(sp, 0, 2 * i)
                load(sp, 1, 2 * i + 1)
            load(sp, 0, 2 * PAIRS, last)

        @block.tensor
        def _(pe):
            expert_tensor(pe, 0, 0)
            expert_tensor(pe, 1, 0)
            with pe.Fori(1, PAIRS) as i:
                expert_tensor(pe, 0, i)
                expert_tensor(pe, 1, i)
            expert_tensor(pe, 0, PAIRS)

        @block.scalar
        def _(act):
            expert_scalar(act, 0)
            expert_scalar(act, 1)
            with act.Fori(1, PAIRS) as i:
                expert_scalar(act, 2 * i)
                expert_scalar(act, 2 * i + 1)
            expert_scalar(act, 2 * PAIRS)

        @block.vector
        def _(dve):
            expert_vector(dve, 0, 0)
            expert_vector(dve, 1, 1)
            with dve.Fori(1, PAIRS) as i:
                expert_vector(dve, 0, 2 * i)
                expert_vector(dve, 1, 2 * i + 1)
            expert_vector(dve, 0, 2 * PAIRS, weighted=last is None)

        @block.gpsimd
        def _(pool):
            expert_pool(pool, 0, 0)
            expert_pool(pool, 1, 1)
            with pool.Fori(1, PAIRS) as i:
                expert_pool(pool, 0, 2 * i)
                expert_pool(pool, 1, 2 * i + 1)
            if last is None:
                expert_pool(pool, 0, 2 * PAIRS)

    N = 2 * PAIRS + 1
    for p in range(2):
        weights_loaded[p].passed((PAIRS + 1 - p) * LOADS * 16)
    cw_staged.passed(N if last is None else N - 1)
    pair_ready.passed(N * CHUNKS * J)
    gate_taken.passed(N * CHUNKS * J)
    hid_ready.passed(N * CHUNKS * J)
    out_ready.passed(N * CHUNKS)
    out_added.passed(N * CHUNKS)


def store_stage(c, out):
    nc = c.nc
    stored = c.count("result_stored")
    with nc.Block() as block:
        @block.sync
        def _(sp):
            sp.dma_start(out.rearrange("b (t p) d -> p (b t) d", p=P), c.x[:]).then_inc(stored.sem, 16)
            sp.wait_ge(*stored.after(16))
    stored.passed(16)


PROJ = [f"L0_attn_b_W{x}" for x in "qkvo"] + [f"L1_attn_a_W{x}_T" for x in "qkvo"] + [f"L1_ffn_w{x}" for x in "qkvo"]


def hybrid_stack(nc, i, out, layers="abcdefgh"):
    with ExitStack() as ctx:
        c = Core(nc, ctx)
        c.i = i
        c.x = c.sbuf("x", [P, TILES, D])
        c.h = c.sbuf("h", [P, TILES, D])
        c.n = c.sbuf("n", [P, TILES, D])
        c.ht = c.sbuf("ht", [P, N_TOK])
        c.big = c.sbuf("big", [P, 6, N_TOK])
        scratch = c.sbuf("scratch", [P, 6 * N_TOK], bf16)
        c.conv = scratch[:, 0:4 * N_TOK].bitcast(fp32).rearrange("p (b n) -> p b n", b=2)
        c.bu = c.conv[:, 0, :]
        c.state = c.conv[:, 1, :]
        c.decay = c.sbuf("decay", [P, 1])
        c.v = c.n
        c.parts = scratch[:, :].rearrange("p (a s n) -> p a s n", a=2, s=3)
        c.q_max = c.sbuf("q_max", [P, 2, N_TOK], bf16)
        c.q_exp = c.sbuf("q_exp", [P, 2, N_TOK], bf16)
        c.k_max = c.sbuf("k_max", [P, 2, N_TOK], bf16)
        c.k_exp = c.sbuf("k_exp", [P, 2, N_TOK], bf16)
        c.v_head = c.sbuf("v_head", [P, 2, TILES, OUT_ROWS])
        c.prob = c.big[:, 2:6, :].rearrange("p a (b n) -> p (a b) n", n=UNIT)
        c.out_head = c.sbuf("out_head", [P, 2, CHUNK])
        c.mx = c.sbuf("mx", [P, TILES, CHUNKS])
        c.rowmax = c.sbuf("rowmax", [P, TILES])
        c.shift = c.sbuf("shift", [P, PARTS, TILES], bf16)
        c.ident = c.sbuf("ident", [P, P])
        c.ident16 = c.sbuf("ident16", [P, P], bf16)
        c.flip = c.sbuf("flip", [P, P])
        c.mask_q = c.sbuf("mask_q", [P, 2, 2, 2 * P], bf16)
        c.mask_k = c.sbuf("mask_k", [P, 2, 2 * P], bf16)
        c.bn = c.sbuf("bn", [P, TILES, 6])
        c.mv = c.sbuf("mv", [P, TILES, 2])
        c.mean2 = c.sbuf("mean2", [P, TILES])
        c.rstd = c.sbuf("rstd", [P, TILES])
        c.minus_half = c.sbuf("minus_half", [P, TILES])
        c.expert_ids_i = c.sbuf("expert_ids_i", [P, 16], mybir.dt.int32)
        c.expert_ids = c.sbuf("expert_ids", [P, 16])
        c.ids_wide = lambda e: c.expert_ids[:, 0:e].rearrange("p (o e) -> p o e", o=1).broadcast_to((P, TILES, e))
        c.logits = c.sbuf("logits", [P, TILES, 16])
        c.probs = c.sbuf("probs", [P, TILES, 16])
        c.pick = c.sbuf("pick", [P, TILES, 16])
        c.top = c.sbuf("top", [P, TILES, 8])
        c.top_i = c.sbuf("top_i", [P, TILES, 8], u32)
        c.top_f = c.sbuf("top_f", [P, TILES, 2])
        c.top_gap = c.sbuf("top_gap", [P, TILES])
        c.total = c.sbuf("total", [P, TILES])
        c.second = c.sbuf("second", [P, TILES])
        c.cw = c.sbuf("cw", [P, 9, TILES])
        c.cw_now = c.sbuf("cw_now", [P, 2, TILES])
        c.wg = c.sbuf("wg", [P, 2, 352])
        c.wu = c.sbuf("wu", [P, 2, 352])
        c.wd = c.sbuf("wd", [P, 2, 3, D])
        c.silu = c.sbuf("silu", [P, 2, CHUNK])
        c.hid = c.sbuf("hid", [P, 2, 4, CHUNK])
        c.conv_w = c.sbuf("conv_w", [P, 2, TAPS])
        c.w_in = c.sbuf("w_in", [P, 2 * INNER])
        c.w_b = c.sbuf("w_b", [P, 2, STATE])
        c.w_c = c.sbuf("w_c", [STATE, INNER])
        c.w_out = c.sbuf("w_out", [P, 2, D])
        c.w1 = c.sbuf("w1", [P, D_FF])
        c.w2 = c.sbuf("w2", [P, D_FF // P, D])
        c.router0 = c.sbuf("router0", [P, 9])
        c.router1 = c.sbuf("router1", [P, 8])
        c.proj_names = PROJ
        c.proj = c.sbuf("proj", [P, len(PROJ), D])
        c.keys_twice = c.sbuf("keys_twice", [2, 2 * D])
        c.circ = c.sbuf("circ", [P, 2, D])
        c.circ_a = c.sbuf("circ_a", [P, D])
        c.circ_b = c.sbuf("circ_b", [P, D])
        c.columns = {name: c.sbuf("col_" + name, [P, n])[:] for name, n in (
            ("L0_attn_a_conv_b", 2), ("L0_attn_a_D_param", 2), ("L0_attn_b_bq", 1), ("L0_attn_b_bk", 1),
            ("L0_attn_b_ln1_w", 1), ("L0_attn_b_ln1_b", 1), ("L0_attn_b_ln2_w", 1), ("L0_attn_b_ln2_b", 1),
            ("L0_attn_b_b1", 4), ("L1_ffn_norm1_w", 1), ("L1_ffn_norm2_w", 1))}
        c.rows = {name: c.sbuf("row_" + name, [P, n])[:] for name, n in (
            ("L0_attn_a_ln_gamma", D), ("L0_attn_a_ln_beta", D), ("L0_attn_b_bv", D), ("L0_attn_b_bo", D),
            ("L0_attn_b_b2", D), ("L1_attn_b_decay", 1), ("L1_attn_b_gate", 1))}
        c.ps = ctx.enter_context(nc.psum_tensor("ps", [P, 8 * CHUNK], fp32))
        c.parts_dram = nc.dram_tensor("parts_dram", (2, 3, D, N_TOK), bf16).ap()
        c.out_dram = nc.dram_tensor("out_dram", (HEADS, P, CHUNK), fp32).ap()
        c.keys_dram = nc.dram_tensor("keys_dram", (2, 2 * D), fp32).ap()

        constants_stage(c)

        def experts0():
            norm_stage(c, c.x, c.h, transpose=True)
            router_stage(c, c.router0, 9, False)
            experts_stage(c, i["L0_ffn_Wg"], i["L0_ffn_Wu"], i["L0_ffn_Wd"], 352)

        def attention(w, window=None, dst=None, bq=None, bk=None, bv=None):
            project_stage(c, w, bq, bk, bv)
            heads_stage(c, window)
            output_stage(c, w, dst)

        def experts1():
            norm_stage(c, c.x, c.h)
            norm_stage(c, c.h, c.n, rms=True, transpose=True, scale=c.columns["L1_ffn_norm1_w"])
            attention(8, dst=c.h)
            norm_stage(c, c.h, c.n, rms=True, transpose=True, scale=c.columns["L1_ffn_norm2_w"])
            add_stage(c, c.x, c.h)
            router_stage(c, c.router1, 8, True)
            experts_stage(c, i["L1_ffn_e_gate"], i["L1_ffn_e_up"], i["L1_ffn_e_down"], 256,
                          last=(i["L1_ffn_sh_gate"], i["L1_ffn_sh_up"], i["L1_ffn_sh_down"]))

        if "a" in layers:
            norm_stage(c, c.x, c.h, transpose=True)
            state_space_stage(c)
            norm_stage(c, c.h, c.n)
            add_stage(c, c.x, c.n, scale_row=c.rows["L0_attn_a_ln_gamma"], row=c.rows["L0_attn_a_ln_beta"])
        if "b" in layers:
            experts0()
        if "c" in layers:
            norm_stage(c, c.x, c.h)
            norm_stage(c, c.h, c.n, transpose=True, scale=c.columns["L0_attn_b_ln1_w"], shift=c.columns["L0_attn_b_ln1_b"])
            attention(0, window=0, dst=c.h, bq=c.columns["L0_attn_b_bq"], bk=c.columns["L0_attn_b_bk"],
                      bv=c.rows["L0_attn_b_bv"])
            add_stage(c, c.h, row=c.rows["L0_attn_b_bo"])
            norm_stage(c, c.h, c.n, transpose=True, scale=c.columns["L0_attn_b_ln2_w"], shift=c.columns["L0_attn_b_ln2_b"])
            feed_forward_stage(c, c.h)
            add_stage(c, c.x, c.h, row=c.rows["L0_attn_b_b2"])
        if "d" in layers:
            experts0()
        if "e" in layers:
            norm_stage(c, c.x, c.h, transpose=True)
            attention(4, window=1, dst=c.x)
        if "f" in layers:
            experts1()
        if "g" in layers:
            norm_stage(c, c.x, c.h, transpose=True)
            hologram_stage(c)
            add_stage(c, c.x, c.h)
        if "h" in layers:
            experts1()
        store_stage(c, out)


TRANSPOSED = ("L0_attn_a_W_in", "L0_attn_a_W_B", "L0_attn_a_W_C", "L0_attn_a_W_out",
              "L1_attn_a_Wq", "L1_attn_a_Wk", "L1_attn_a_Wv", "L1_attn_a_Wo")


def kernel(**inputs):
    import numpy as _np
    import concourse.bacc as _bacc
    from concourse import mybir as _mybir
    from concourse.bass_utils import run_bass_kernel_spmd as _run

    nc = _bacc.Bacc("TRN2", target_bir_lowering=False, num_devices=1)
    arrays, aps = {}, {}
    for name, a in inputs.items():
        a = _np.asarray(a)
        if name in TRANSPOSED:
            name, a = name + "_T", a.T
        a = _np.ascontiguousarray(a if a.ndim else a.reshape(1))
        arrays[f"in_{name}_dram"] = a
        aps[name] = nc.dram_tensor(f"in_{name}_dram", a.shape, _mybir.dt.from_np(a.dtype), kind="ExternalInput").ap()
    out = nc.dram_tensor("out_0_dram", (1, N_TOK, D), fp32, kind="ExternalOutput").ap()
    hybrid_stack(nc, aps, out)
    r = _run(nc, [arrays], core_ids=[0])
    return r.results[0]["out_0_dram"]
```

```python
import concourse.bass as bass
from concourse import mybir
from contextlib import ExitStack

fp32 = mybir.dt.float32
bf16 = mybir.dt.bfloat16
fp32r = mybir.dt.float32r
u32 = mybir.dt.uint32
ALU = mybir.AluOpType
ACT = mybir.ActivationFunctionType
AX = mybir.AxisListType

P = 128
N_TOK = 2048
D = 128
TILES = N_TOK // P
CHUNK = 512
CHUNKS = N_TOK // CHUNK
TPC = CHUNK // P
HEADS = 16
HD = D // HEADS
INNER = 256
STATE = 64
TAPS = 4
D_FF = 512
LN_EPS = 1e-5
RMS_EPS = 1e-6
MASKED = -1.0e30
PARTS = 3
STACK = PARTS * PARTS * HD
SHIFT_AT = 96
UNIT = 1024
P_UNITS = 8
OUT_ROWS = 32


class Count:

    def __init__(self, sem):
        self.sem = sem
        self.at = 0

    def after(self, n):
        return self.sem, self.at + n

    def passed(self, n):
        self.at = self.at + n


class Core:

    def __init__(self, nc, ctx):
        self.nc = nc
        self.ctx = ctx
        self.counts = {}
        self.layers = 0

    def sbuf(self, name, shape, dt=fp32):
        return self.ctx.enter_context(self.nc.sbuf_tensor(name, shape, dt))

    def layer(self, buffers):
        held = ExitStack()
        self.layers = self.layers + 1
        made = {name: held.enter_context(self.nc.sbuf_tensor(f"{name}_{self.layers}", shape, dt))
                for name, shape, dt in buffers}
        return held, made

    def count(self, name):
        if name not in self.counts:
            self.counts[name] = Count(self.ctx.enter_context(self.nc.semaphore(name)))
        return self.counts[name]


class Chain:

    def __init__(self, engine, steps):
        self.engine = engine
        self.steps = steps
        self.n = 0
        self.offset = 0

    def mark(self, ins):
        ins.then_inc(self.steps.sem, 1)
        self.n += 1

    def link(self, ins):
        self.mark(ins)
        self.engine.wait_ge(*self.steps.after(self.offset + self.n))


def bank(c, n, width=CHUNK):
    return c.ps[:, n * CHUNK:n * CHUNK + width]


def constants_stage(c):
    nc = c.nc
    built = c.count("const_built")
    loaded = c.count("const_loaded")
    n_loaded = [0]
    n_pool = [0]
    with nc.Block() as block:

        @block.gpsimd
        def _(pool):
            def step(ins):
                ins.then_inc(built.sem, 1)
                n_pool[0] += 1
                pool.wait_ge(*built.after(n_pool[0]))

            def keep(view, width, base, coef, step_, fill):
                step(pool.affine_select(out=view, in_=view, compare_op=ALU.is_ge, fill=fill, base=base,
                                        pattern=[[step_, width]], channel_multiplier=coef))

            step(pool.memset(c.minus_half[:], -0.5))
            step(pool.memset(c.ident[:], 0.0))
            step(pool.affine_select(out=c.ident[:], in_=c.ident[:], compare_op=ALU.not_equal, fill=1.0,
                                    base=0, pattern=[[-1, P]], channel_multiplier=1))
            step(pool.tensor_copy(c.ident16[:], c.ident[:]))
            step(pool.memset(c.flip[:], 0.0))
            for total in (0, D):
                step(pool.affine_select(out=c.flip[:], in_=c.flip[:], compare_op=ALU.not_equal, fill=1.0,
                                        base=-total, pattern=[[1, P]], channel_multiplier=1))
            step(pool.iota(c.expert_ids_i[:], pattern=[[1, 16]], base=0, channel_multiplier=0))
            step(pool.tensor_copy(c.expert_ids[:], c.expert_ids_i[:]))
            for n, back in enumerate((128, 63)):
                for first in (False, True):
                    m = c.mask_q[:, n, 1 if first else 0, :]
                    step(pool.memset(m, 0.0))
                    keep(m, 2 * P, P, 1, -1, MASKED)
                    keep(m, 2 * P, back - P, -1, 1, MASKED)
                    if first:
                        keep(m, 2 * P, -P, 0, 1, MASKED)
                m = c.mask_k[:, n, :]
                step(pool.memset(m, 0.0))
                keep(m, 2 * P, 0, -1, 1, MASKED)
                keep(m, 2 * P, back, 1, -1, MASKED)

        @block.sync
        def _(sp):
            def load(dst, src):
                sp.dma_start(dst, src).then_inc(loaded.sem, 16)
                n_loaded[0] += 1

            load(c.x[:], c.i["L0_attn_a_x"].rearrange("b (t p) d -> p (b t) d", p=P))
            for name, dst in c.columns.items():
                for n in range(dst.shape[1]):
                    load(dst[:, n:n + 1], c.i[name][n * P:(n + 1) * P].rearrange("(p o) -> p o", o=1))
            for name, dst in c.rows.items():
                load(dst, c.i[name].partition_broadcast(P))
            load(c.conv_w[:], c.i["L0_attn_a_conv_w"].rearrange("(n p) o k -> p n (o k)", p=P))
            load(c.w_in[:], c.i["L0_attn_a_W_in_T"])
            load(c.w_b[:], c.i["L0_attn_a_W_B_T"].rearrange("(n p) s -> p n s", p=P))
            load(c.w_c[:], c.i["L0_attn_a_W_C_T"])
            load(c.w_out[:], c.i["L0_attn_a_W_out_T"].rearrange("(n p) d -> p n d", p=P))
            load(c.w1[:], c.i["L0_attn_b_W1"])
            load(c.w2[:], c.i["L0_attn_b_W2"].rearrange("(n p) d -> p n d", p=P))
            load(c.router0[:], c.i["L0_ffn_Wr"])
            load(c.router1[:], c.i["L1_ffn_router_w"])
            for n, name in enumerate(c.proj_names):
                load(c.proj[:, n, :], c.i[name])
            for s, name in enumerate(("bind", "unbind")):
                key = c.i[f"L1_attn_b_{name}_key"].rearrange("(o n) -> o n", o=1)
                for half in range(2):
                    load(c.keys_twice[s:s + 1, half * D:(half + 1) * D], key)
            sp.wait_ge(*loaded.after(16 * n_loaded[0]))

    built.passed(n_pool[0])
    loaded.passed(16 * n_loaded[0])


def norm_stage(c, src, dst, rms=False, transpose=False, scale=None, shift=None, add=None):
    nc = c.nc
    eps = RMS_EPS if rms else LN_EPS
    chain_s = c.count("dve_chain")
    stats_ready = c.count("norm_stats_ready")
    rstd_ready = c.count("norm_rstd_ready")
    tile_ready = c.count("norm_tile_ready")
    bank_ready = c.count("norm_bank_ready")
    bank_taken = c.count("norm_bank_taken")
    links = [0]
    with nc.Block() as block:

        @block.vector
        def _(dve):
            chain = Chain(dve, chain_s)
            for t in range(TILES):
                ins = nc.vector.bn_stats(c.bn[:, t, :], src[:, t, :])
            chain.link(ins)
            for t in range(TILES):
                ins = nc.vector.bn_aggr(c.mv[:, t, :], c.bn[:, t, :])
            if rms:
                chain.link(ins)
                chain.link(nc.vector.tensor_tensor(c.mean2[:], c.mv[:, :, 0], c.mv[:, :, 0], ALU.mult))
                ins = nc.vector.tensor_tensor(c.mv[:, :, 1], c.mv[:, :, 1], c.mean2[:], ALU.add)
            ins.then_inc(stats_ready.sem, 1)
            dve.wait_ge(*rstd_ready.after(2))
            for t in range(TILES):
                if rms:
                    ins = nc.vector.tensor_scalar(dst[:, t, :], src[:, t, :], c.rstd[:, t:t + 1], None, ALU.mult)
                else:
                    ins = nc.vector.tensor_scalar(dst[:, t, :], src[:, t, :], c.mv[:, t, 0:1], c.rstd[:, t:t + 1],
                                                  ALU.subtract, ALU.mult)
                ins.then_inc(tile_ready.sem, 1)
            links[0] = chain.n

        @block.gpsimd
        def _(pool):
            pool.wait_ge(*stats_ready.after(1))
            pool.tensor_scalar(c.rstd[:], c.mv[:, :, 1], eps, None, ALU.add).then_inc(rstd_ready.sem, 1)
            pool.wait_ge(*rstd_ready.after(1))
            pool.tensor_tensor(c.rstd[:], c.rstd[:], c.minus_half[:], ALU.pow).then_inc(rstd_ready.sem, 1)

        if transpose:
            @block.tensor
            def _(pe):
                for t in range(TILES):
                    pe.wait_ge(*tile_ready.after(t + 1))
                    out = bank(c, t // TPC)[:, (t % TPC) * P:(t % TPC + 1) * P]
                    ins = nc.tensor.transpose(out, dst[:, t, :], c.ident[:])
                    if t % TPC == TPC - 1:
                        ins.then_inc(bank_ready.sem, 1)

            @block.scalar
            def _(act):
                for b in range(CHUNKS):
                    act.wait_ge(*bank_ready.after(b + 1))
                    out = c.ht[:, b * CHUNK:(b + 1) * CHUNK]
                    if scale is None:
                        nc.scalar.activation(out, bank(c, b), ACT.Copy).then_inc(bank_taken.sem, 1)
                    else:
                        nc.scalar.activation(out, bank(c, b), ACT.Identity, scale=scale,
                                             bias=shift if shift is not None else 0.0).then_inc(bank_taken.sem, 1)

    chain_s.passed(links[0])
    stats_ready.passed(1)
    rstd_ready.passed(2)
    tile_ready.passed(TILES)
    if transpose:
        bank_ready.passed(CHUNKS)
        bank_taken.passed(CHUNKS)


def state_space_stage(c):
    nc = c.nc
    proj_ready = c.count("ss_proj_ready")
    proj_taken = c.count("ss_proj_taken")
    gate_taken = c.count("ss_gate_taken")
    conv_ready = c.count("ss_conv_ready")
    u_ready = c.count("ss_u_ready")
    bu_ready = c.count("ss_bu_ready")
    bu_taken = c.count("ss_bu_taken")
    state_ready = c.count("ss_state_ready")
    y_ready = c.count("ss_y_ready")
    y_taken = c.count("ss_y_taken")
    out_ready = c.count("ss_out_ready")
    added = c.count("ss_added")
    chain_s = c.count("dve_chain")
    blocks = INNER // P
    xin, u, gate = c.big[:, 0:2, :], c.big[:, 2:4, :], c.big[:, 4:6, :]
    PAD = TAPS - 1
    links = [0]
    with nc.Block() as block:

        @block.tensor
        def _(pe):
            for b in range(2 * blocks):
                for k in range(CHUNKS):
                    n = b * CHUNKS + k
                    if n >= 8:
                        pe.wait_ge(*proj_taken.after(n - 7))
                    nc.tensor.matmul(bank(c, n % 8), c.w_in[:, b * P:(b + 1) * P],
                                     c.ht[:, k * CHUNK:(k + 1) * CHUNK], start=True, stop=True).then_inc(proj_ready.sem, 1)
            pe.wait_ge(*u_ready.after(blocks))
            pe.wait_ge(*proj_taken.after(4 * blocks * 2))
            for k in range(CHUNKS):
                for b in range(blocks):
                    ins = nc.tensor.matmul(bank(c, k)[0:STATE, :], c.w_b[:, b, :], u[:, b, k * CHUNK:(k + 1) * CHUNK],
                                           start=(b == 0), stop=(b == blocks - 1))
                ins.then_inc(bu_ready.sem, 1)
            pe.wait_ge(*state_ready.after(1))
            for b in range(blocks):
                for k in range(CHUNKS):
                    nc.tensor.matmul(bank(c, b * CHUNKS + k), c.w_c[:, b * P:(b + 1) * P],
                                     c.state[0:STATE, k * CHUNK:(k + 1) * CHUNK], start=True, stop=True).then_inc(y_ready.sem, 1)
            pe.wait_ge(*y_taken.after(blocks * CHUNKS))
            for t in range(TILES):
                for b in range(blocks):
                    ins = nc.tensor.matmul(bank(c, t // TPC)[:, (t % TPC) * P:(t % TPC + 1) * P],
                                           u[:, b, t * P:(t + 1) * P], c.w_out[:, b, :], start=(b == 0), stop=(b == blocks - 1))
                if t % TPC == TPC - 1:
                    ins.then_inc(out_ready.sem, 1)

        @block.scalar
        def _(act):
            for n in range(2 * blocks * CHUNKS):
                b, k = n // CHUNKS, n % CHUNKS
                act.wait_ge(*proj_ready.after(n + 1))
                if b < blocks:
                    out = xin[:, b, k * CHUNK:(k + 1) * CHUNK]
                    nc.scalar.activation(out, bank(c, n % 8), ACT.Copy).then_inc(proj_taken.sem, 1)
                else:
                    out = gate[:, b - blocks, k * CHUNK:(k + 1) * CHUNK]
                    nc.scalar.activation(out, bank(c, n % 8), ACT.Silu).then_inc(proj_taken.sem, 1)
            for b in range(blocks):
                act.wait_ge(*conv_ready.after(b + 1))
                nc.scalar.activation(u[:, b, :], c.conv[:, b, :], ACT.Silu).then_inc(u_ready.sem, 1)
            for k in range(CHUNKS):
                act.wait_ge(*bu_ready.after(k + 1))
                nc.scalar.activation(c.bu[0:STATE, k * CHUNK:(k + 1) * CHUNK], bank(c, k)[0:STATE, :], ACT.Copy,
                                     scale=0.05).then_inc(bu_taken.sem, 1)

        @block.vector
        def _(dve):
            chain = Chain(dve, chain_s)
            chain.link(nc.vector.memset(c.decay[:], 0.95))
            for b in range(blocks):
                dve.wait_ge(*proj_taken.after((b + 1) * CHUNKS))
                chain.link(nc.vector.tensor_scalar(c.conv[:, b, :], xin[:, b, :], c.conv_w[:, b, PAD:TAPS],
                                                   c.columns["L0_attn_a_conv_b"][:, b:b + 1], ALU.mult, ALU.add))
                for back in range(1, TAPS):
                    tail = c.conv[:, b, back:N_TOK]
                    ins = nc.vector.scalar_tensor_tensor(tail, xin[:, b, 0:N_TOK - back], c.conv_w[:, b, PAD - back:TAPS - back],
                                                         tail, ALU.mult, ALU.add)
                    if back < PAD:
                        chain.link(ins)
                ins.then_inc(conv_ready.sem, 1)
            dve.wait_ge(*bu_taken.after(CHUNKS))
            nc.vector.tensor_tensor_scan(c.state[0:STATE, :], c.decay[0:STATE, 0:1].broadcast_to((STATE, N_TOK)),
                                         c.bu[0:STATE, :], 0.0, ALU.mult, ALU.add).then_inc(state_ready.sem, 1)
            for b in range(blocks):
                for k in range(CHUNKS):
                    part = u[:, b, k * CHUNK:(k + 1) * CHUNK]
                    dve.wait_ge(*y_ready.after(b * CHUNKS + k + 1))
                    chain.link(nc.vector.scalar_tensor_tensor(part, part, c.columns["L0_attn_a_D_param"][:, b:b + 1],
                                                              bank(c, b * CHUNKS + k), ALU.mult, ALU.add))
                    nc.vector.tensor_tensor(part, part, gate[:, b, k * CHUNK:(k + 1) * CHUNK],
                                            ALU.mult).then_inc(y_taken.sem, 1)
            for k in range(CHUNKS):
                dve.wait_ge(*out_ready.after(k + 1))
                tiles = c.h[:, k * TPC:(k + 1) * TPC, :]
                nc.vector.tensor_tensor(tiles, tiles, bank(c, k).rearrange("p (t d) -> p t d", d=D), ALU.add).then_inc(added.sem, 1)
            links[0] = chain.n

    chain_s.passed(links[0])
    proj_ready.passed(2 * blocks * CHUNKS)
    proj_taken.passed(2 * blocks * CHUNKS)
    conv_ready.passed(blocks)
    u_ready.passed(blocks)
    bu_ready.passed(CHUNKS)
    bu_taken.passed(CHUNKS)
    state_ready.passed(1)
    y_ready.passed(blocks * CHUNKS)
    y_taken.passed(blocks * CHUNKS)
    out_ready.passed(CHUNKS)
    added.passed(CHUNKS)


def add_stage(c, dst, *terms, row=None, scale_row=None):
    nc = c.nc
    chain_s = c.count("dve_chain")
    links = [0]

    def along(r):
        return r.rearrange("p (o d) -> p o d", o=1).broadcast_to((P, TILES, D))

    with nc.Block() as block:
        @block.vector
        def _(dve):
            chain = Chain(dve, chain_s)
            for term in terms:
                if scale_row is not None:
                    chain.link(nc.vector.tensor_tensor(term[:], term[:], along(scale_row), ALU.mult))
                chain.link(nc.vector.tensor_tensor(dst[:], dst[:], term[:], ALU.add))
            if row is not None:
                chain.link(nc.vector.tensor_tensor(dst[:], dst[:], along(row), ALU.add))
            links[0] = chain.n
    chain_s.passed(links[0])


def hologram_stage(c):
    nc = c.nc
    written = c.count("holo_keys_written")
    circ_loaded = c.count("holo_circ_loaded")
    decay_ready = c.count("holo_decay_ready")
    scan_ready = c.count("holo_scan_ready")
    unbind_ready = c.count("holo_unbind_ready")
    unbind_taken = c.count("holo_unbind_taken")
    map_ready = c.count("holo_map_ready")
    map_taken = c.count("holo_map_taken")
    out_ready = c.count("holo_out_ready")
    added = c.count("holo_added")
    with nc.Block() as block:

        @block.sync
        def _(sp):
            sp.dma_start(c.keys_dram, c.keys_twice[0:2, :]).then_inc(written.sem, 16)
            sp.wait_ge(*written.after(16))
            for s in range(2):
                src = bass.AP(c.keys_dram.tensor, s * 2 * D, [[1, D], [1, D]])
                sp.dma_start(c.circ[:, s, :], src).then_inc(circ_loaded.sem, 16)

        @block.scalar
        def _(act):
            nc.scalar.activation(c.decay[:], c.rows["L1_attn_b_decay"], ACT.Sigmoid).then_inc(decay_ready.sem, 1)

        @block.tensor
        def _(pe):
            pe.wait_ge(*circ_loaded.after(32))
            nc.tensor.matmul(bank(c, 0, P), c.circ[:, 1, :], c.flip[:], start=True, stop=True).then_inc(unbind_ready.sem, 1)
            pe.wait_ge(*unbind_taken.after(1))
            nc.tensor.matmul(bank(c, 1, P), c.circ[:, 0, :], c.circ_a[:], start=True, stop=True).then_inc(unbind_ready.sem, 1)
            pe.wait_ge(*unbind_taken.after(2))
            nc.tensor.matmul(bank(c, 2, P), c.flip[:], c.circ_b[:], start=True, stop=True).then_inc(map_ready.sem, 1)
            pe.wait_ge(*map_taken.after(1))
            pe.wait_ge(*scan_ready.after(1))
            for t in range(TILES):
                ins = nc.tensor.matmul(bank(c, 4 + t // TPC)[:, (t % TPC) * P:(t % TPC + 1) * P],
                                       c.big[:, 0, t * P:(t + 1) * P], c.circ_a[:], start=True, stop=True)
                if t % TPC == TPC - 1:
                    ins.then_inc(out_ready.sem, 1)

        @block.vector
        def _(dve):
            dve.wait_ge(*unbind_ready.after(1))
            nc.vector.tensor_copy(c.circ_a[:], bank(c, 0, P)).then_inc(unbind_taken.sem, 1)
            dve.wait_ge(*unbind_ready.after(2))
            nc.vector.tensor_copy(c.circ_b[:], bank(c, 1, P)).then_inc(unbind_taken.sem, 1)
            dve.wait_ge(*map_ready.after(1))
            nc.vector.tensor_scalar(c.circ_a[:], bank(c, 2, P), c.rows["L1_attn_b_gate"], None, ALU.mult).then_inc(map_taken.sem, 1)
            dve.wait_ge(*decay_ready.after(1))
            nc.vector.tensor_tensor_scan(c.big[:, 0, :], c.decay[:, 0:1].broadcast_to((P, N_TOK)), c.ht[:], 0.0,
                                         ALU.mult, ALU.add).then_inc(scan_ready.sem, 1)
            for k in range(CHUNKS):
                dve.wait_ge(*out_ready.after(k + 1))
                tiles = c.h[:, k * TPC:(k + 1) * TPC, :]
                nc.vector.tensor_tensor(tiles, tiles, bank(c, 4 + k).rearrange("p (t d) -> p t d", d=D), ALU.add).then_inc(added.sem, 1)

    for s, n in ((written, 16), (circ_loaded, 32), (decay_ready, 1), (scan_ready, 1), (unbind_ready, 2),
                 (unbind_taken, 2), (map_ready, 1), (map_taken, 1), (out_ready, CHUNKS), (added, CHUNKS)):
        s.passed(n)


def project_stage(c, w, bq=None, bk=None, bv=None):
    nc = c.nc
    qk_ready = c.count("proj_qk_ready")
    q_taken = c.count("proj_q_taken")
    k_taken = c.count("proj_k_taken")
    v_ready = c.count("proj_v_ready")
    v_taken = c.count("proj_v_taken")
    q_split = c.count("proj_q_split")
    k_split = c.count("proj_k_split")
    stored = c.count("proj_parts_stored")
    zeroed = c.count("proj_rows_zeroed")
    SPLIT_STEPS = 3
    with nc.Block() as block:

        @block.tensor
        def _(pe):
            for n in range(2):
                for k in range(CHUNKS):
                    nc.tensor.matmul(bank(c, n * CHUNKS + k), c.proj[:, w + n, :], c.ht[:, k * CHUNK:(k + 1) * CHUNK],
                                     start=True, stop=True).then_inc(qk_ready.sem, 1)
            for t in range(TILES):
                if t % TPC == 0:
                    pe.wait_ge(*q_taken.after(2 * (t // TPC + 1)))
                ins = nc.tensor.matmul(bank(c, t // TPC)[:, (t % TPC) * P:(t % TPC + 1) * P], c.ht[:, t * P:(t + 1) * P],
                                       c.proj[:, w + 2, :], start=True, stop=True)
                if t % TPC == TPC - 1:
                    ins.then_inc(v_ready.sem, 1)

        @block.scalar
        def _(act):
            for n, (b, taken) in enumerate(((bq, q_taken), (bk, k_taken))):
                for k in range(CHUNKS):
                    cols = slice(k * CHUNK, (k + 1) * CHUNK)
                    act.wait_ge(*qk_ready.after(n * CHUNKS + k + 1))
                    for out in (c.big[:, n, cols], c.parts[:, n, 0, cols]):
                        nc.scalar.activation(out, bank(c, n * CHUNKS + k), ACT.Identity,
                                             bias=b if b is not None else 0.0).then_inc(taken.sem, 1)
            for k in range(CHUNKS):
                act.wait_ge(*v_ready.after(k + 1))
                nc.scalar.activation(c.v[:, k * TPC:(k + 1) * TPC, :].rearrange("p t d -> p (t d)"), bank(c, k),
                                     ACT.Copy).then_inc(v_taken.sem, 1)

        @block.vector
        def _(dve):
            for n, (taken, split_done) in enumerate(((q_taken, q_split), (k_taken, k_split))):
                for k in range(CHUNKS):
                    cols = slice(k * CHUNK, (k + 1) * CHUNK)
                    x, part = c.big[:, n, cols], c.parts[:, n, :, cols]
                    dve.wait_ge(*taken.after(2 * (k + 1)))
                    nc.vector.tensor_tensor(x, x, part[:, 0, :], ALU.subtract).then_inc(split_done.sem, 1)
                    dve.wait_ge(*split_done.after(SPLIT_STEPS * k + 1))
                    nc.vector.tensor_copy(part[:, 1, :], x).then_inc(split_done.sem, 1)
                    dve.wait_ge(*split_done.after(SPLIT_STEPS * k + 2))
                    nc.vector.tensor_tensor(part[:, 2, :], x, part[:, 1, :], ALU.subtract).then_inc(split_done.sem, 1)
            if bv is not None:
                dve.wait_ge(*v_taken.after(CHUNKS))
                nc.vector.tensor_tensor(c.v[:], c.v[:], bv.rearrange("p (o d) -> p o d", o=1).broadcast_to((P, TILES, D)),
                                        ALU.add)

        @block.gpsimd
        def _(pool):
            for n, (rows, value) in enumerate(((c.q_max[64:P], 0.0), (c.q_exp[64:P], 0.0), (c.k_max[64:P], 0.0),
                                               (c.k_exp[64:SHIFT_AT], 0.0), (c.k_exp[SHIFT_AT:P], 1.0),
                                               (c.v_head[:], 0.0), (c.v_head[:, :, :, HD:2 * HD], 1.0))):
                if n:
                    pool.wait_ge(*zeroed.after(n))
                pool.memset(rows, value).then_inc(zeroed.sem, 1)

        @block.sync
        def _(sp):
            for n, ready in enumerate((q_split, k_split)):
                for k in range(CHUNKS):
                    cols = slice(k * CHUNK, (k + 1) * CHUNK)
                    sp.wait_ge(*ready.after(SPLIT_STEPS * (k + 1)))
                    sp.dma_start(c.parts_dram[n, :, :, cols].rearrange("s p n -> p s n"), c.parts[:, n, :, cols])\
                        .then_inc(stored.sem, 16)
            sp.wait_ge(*stored.after(2 * CHUNKS * 16))

    qk_ready.passed(2 * CHUNKS)
    q_taken.passed(2 * CHUNKS)
    k_taken.passed(2 * CHUNKS)
    v_ready.passed(CHUNKS)
    v_taken.passed(CHUNKS)
    q_split.passed(CHUNKS * SPLIT_STEPS)
    k_split.passed(CHUNKS * SPLIT_STEPS)
    stored.passed(2 * CHUNKS * 16)
    zeroed.passed(7)


def heads_stage(c, window=None):
    nc = c.nc
    stack_loaded = [c.count(f"head_stack_loaded_{p}") for p in range(2)]
    stack_copied = [c.count(f"head_stack_copied_{p}") for p in range(2)]
    v_staged = c.count("head_v_staged")
    max_ready = c.count("head_max_scores_ready")
    max_taken = c.count("head_max_scores_taken")
    shift_ready = c.count("head_shift_rows_ready")
    shift_taken = c.count("head_shift_rows_taken")
    st_ready = c.count("head_scores_ready")
    exp_done = c.count("head_exp_done")
    pv_done = c.count("head_pv_done")
    out_taken = c.count("head_out_taken")
    out_stored = [c.count(f"head_out_stored_{p}") for p in range(2)]
    small = c.count("head_small_steps")
    full = window is None
    scale = float(HD) ** -0.5
    MAX_UNITS = TILES * CHUNKS if full else TILES // 2
    EXP_UNITS = TILES * N_TOK // UNIT if full else TILES * 2 * P // UNIT
    PV_STEPS = TILES if full else 1
    LOADS = 2 * PARTS
    COPIES = 2
    SMALL = 5
    MAX_BANKS = (4, 5, 7)
    SHIFT_BANKS = (7, 4, 5, 7)

    def step_tensor(pe, p, i, with_max, with_exp):
        s = 2 * i + p

        def max_unit(w):
            out = bank(c, MAX_BANKS[w % 3])
            if w >= 3:
                pe.wait_ge(*max_taken.after(s * MAX_UNITS + (w - 2)))
            elif type(s) is not int or s > 0:
                pe.wait_ge(*shift_taken.after((s - 1) * CHUNKS + w + 2))
            if full:
                t, k = w // CHUNKS, w % CHUNKS
                ins = nc.tensor.matmul(out, c.q_max[:, p, t * P:(t + 1) * P], c.k_max[:, p, k * CHUNK:(k + 1) * CHUNK],
                                       start=True, stop=True)
            else:
                for j in range(2):
                    t = 2 * w + j
                    half = out[:, j * 2 * P:(j + 1) * 2 * P]
                    nc.tensor.matmul(half, c.ident16[:], c.mask_q[:, window, 1 if t == 0 else 0, :], start=True, stop=False)
                    if t == 0:
                        ins = nc.tensor.matmul(half[:, P:2 * P], c.q_max[:, p, 0:P], c.k_max[:, p, 0:P], start=False, stop=True)
                    else:
                        ins = nc.tensor.matmul(half, c.q_max[:, p, t * P:(t + 1) * P], c.k_max[:, p, (t - 1) * P:(t + 1) * P],
                                               start=False, stop=True)
            ins.then_inc(max_ready.sem, 1)

        def exp_unit(u):
            q, k_ = c.q_exp[:, 1 - p], c.k_exp[:, 1 - p]
            done = (s - 1) * EXP_UNITS + (u - 1)
            if u >= 2 or type(s) is not int or s > 1:
                pe.wait_ge(*exp_done.after(done))
            chunks = (2, 4)[u] if full and u < 2 else min(u + 2, CHUNKS) if not full else 0
            if chunks:
                pe.wait_ge(*shift_taken.after((s - 1) * CHUNKS + chunks))
            at = 2 * (u % 2)
            if full:
                kb, half = u // 2, u % 2
                for j in range(2):
                    col = half * UNIT + j * CHUNK
                    ins = nc.tensor.matmul(bank(c, at + j), k_[:, kb * P:(kb + 1) * P], q[:, col:col + CHUNK],
                                           start=True, stop=True)
            else:
                for j in range(4):
                    kb = 4 * u + j
                    width = 2 * P if kb < TILES - 1 else P
                    out = c.ps[:, at * CHUNK + j * 2 * P:at * CHUNK + j * 2 * P + width]
                    nc.tensor.matmul(out, c.ident16[:], c.mask_k[:, window, 0:width], start=True, stop=False)
                    ins = nc.tensor.matmul(out, k_[:, kb * P:(kb + 1) * P], q[:, kb * P:kb * P + width], start=False, stop=True)
            ins.then_inc(st_ready.sem, 1)

        def pv_step(kb):
            v = c.v_head[:, 1 - p]
            for g in range(4):
                out = c.ps[OUT_ROWS * g:OUT_ROWS * (g + 1), 6 * CHUNK:7 * CHUNK]
                unit = c.prob[:, (2 * kb + g // 2) % P_UNITS, (g % 2) * CHUNK:(g % 2 + 1) * CHUNK]
                ins = nc.tensor.matmul(out, v[:, kb, :], unit, start=(kb == 0), stop=(kb == TILES - 1), skip_group_check=True)
            ins.then_inc(pv_done.sem, 1)

        def pv_window():
            v = c.v_head[:, 1 - p]
            half = EXP_UNITS * (1 - p)
            for j in range(TPC):
                if with_max and j >= 2:
                    shift_rows(pe, s, j - 2)
                for own in range(2):
                    for g in range(4):
                        t = TPC * g + j
                        kb = t if own else t - 1
                        if kb < 0:
                            continue
                        col = (kb % 4) * 2 * P + (0 if own else P)
                        first = j == 0 and (own == 0 or t == 0)
                        ins = nc.tensor.matmul(c.ps[OUT_ROWS * g:OUT_ROWS * (g + 1), 6 * CHUNK + j * P:6 * CHUNK + (j + 1) * P],
                                               v[:, kb, :], c.prob[:, half + kb // 4, col:col + P],
                                               start=first, stop=(own == 1), skip_group_check=True)
            ins.then_inc(pv_done.sem, 1)
            if with_max:
                shift_rows(pe, s, 2)
                shift_rows(pe, s, 3)

        w = 0
        if with_max:
            pe.wait_ge(*stack_loaded[p].after((i + 1) * LOADS * 16))
        if with_exp:
            pe.wait_ge(*stack_copied[1 - p].after((i + p) * COPIES * 16))
        if with_exp and full:
            for kb in range(TILES + 1):
                todo = ["max"] + ["exp", "max"] * 2 if kb < TILES else []
                todo += (["pv", "max"] if kb else []) + (["max"] if kb % 2 else [])
                half = 0
                for what in todo:
                    if what == "exp":
                        exp_unit(2 * kb + half)
                        if with_max and kb == TILES - 1:
                            shift_rows(pe, s, half)
                        half += 1
                    elif what == "pv":
                        pv_wait(pe, s, kb - 1)
                        pv_step(kb - 1)
                        if with_max and kb >= TILES - 1:
                            shift_rows(pe, s, 2 + kb - (TILES - 1))
                    elif with_max and w < MAX_UNITS:
                        max_unit(w)
                        w += 1
            assert w == (MAX_UNITS if with_max else 0)
        elif with_exp:
            for u in range(EXP_UNITS):
                if with_max:
                    max_unit(2 * u)
                    max_unit(2 * u + 1)
                exp_unit(u)
            pv_wait(pe, s, 0)
            pv_window()
        else:
            for w in range(MAX_UNITS):
                max_unit(w)
            for k in range(CHUNKS):
                shift_rows(pe, s, k)

    def shift_rows(pe, s, k):
        if k == 0:
            pe.wait_ge(*small.after((s + 1) * SMALL))
        if k == CHUNKS - 1:
            pe.wait_ge(*shift_taken.after(s * CHUNKS + 1))
        for j in range(TPC):
            ins = nc.tensor.matmul(bank(c, SHIFT_BANKS[k])[SHIFT_AT:SHIFT_AT + PARTS, j * P:(j + 1) * P],
                                   c.shift[:, :, k * TPC + j], c.ident16[:], start=True, stop=True)
        ins.then_inc(shift_ready.sem, 1)

    def take_shift(act, p, s, k):
        act.wait_ge(*shift_ready.after(s * CHUNKS + k + 1))
        nc.scalar.activation(c.q_exp[SHIFT_AT:SHIFT_AT + PARTS, p, k * CHUNK:(k + 1) * CHUNK],
                             bank(c, SHIFT_BANKS[k])[SHIFT_AT:SHIFT_AT + PARTS], ACT.Copy).then_inc(shift_taken.sem, 1)

    def pv_wait(pe, s, kb):
        if kb == 0:
            pe.wait_ge(*v_staged.after(s))
            if type(s) is not int or s > 1:
                pe.wait_ge(*out_taken.after(s - 1))
        units = 2 * (kb + 1) if full else EXP_UNITS
        pe.wait_ge(*exp_done.after((s - 1) * EXP_UNITS + units))

    def step_scalar(act, p, i, with_max, with_exp):
        s = 2 * i + p
        if not with_exp:
            for k in range(CHUNKS):
                take_shift(act, p, s, k)
            return
        for u in range(EXP_UNITS):
            act.wait_ge(*st_ready.after((s - 1) * EXP_UNITS + u + 1))
            if full:
                buf = u % P_UNITS
                if u >= P_UNITS or type(s) is not int or s > 1:
                    act.wait_ge(*pv_done.after((s - 1) * PV_STEPS + (u - P_UNITS) // 2 + 1))
            else:
                buf = EXP_UNITS * (1 - p) + u
                if type(s) is not int or s > 2:
                    act.wait_ge(*pv_done.after(s - 2))
            width = UNIT if full or u < EXP_UNITS - 1 else UNIT - P
            nc.scalar.activation(c.prob[:, buf, 0:width], c.ps[:, 2 * (u % 2) * CHUNK:2 * (u % 2) * CHUNK + width],
                                 ACT.Exp, scale=scale).then_inc(exp_done.sem, 1)
            if full and with_max and u >= EXP_UNITS - 2:
                take_shift(act, p, s, u - (EXP_UNITS - 2))
        if with_max:
            for k in range(2 if full else 0, CHUNKS):
                take_shift(act, p, s, k)

    def step_vector(dve, p, i, with_max, with_exp):
        s = 2 * i + p
        if with_max:
            for w in range(MAX_UNITS):
                dve.wait_ge(*max_ready.after(s * MAX_UNITS + w + 1))
                if full:
                    nc.vector.reduce_max(c.mx[:, w // CHUNKS, w % CHUNKS:w % CHUNKS + 1], bank(c, MAX_BANKS[w % 3]), AX.X)\
                        .then_inc(max_taken.sem, 1)
                else:
                    nc.vector.reduce_max(c.mx[:, 2 * w:2 * w + 2, 0], bank(c, MAX_BANKS[w % 3]).rearrange("p (a n) -> p a n", a=2), AX.X)\
                        .then_inc(max_taken.sem, 1)
            dve.wait_ge(*max_taken.after((s + 1) * MAX_UNITS))
            cols = CHUNKS if full else 1
            base = s * SMALL
            nc.vector.tensor_reduce(c.rowmax[:], c.mx[:, :, 0:cols], AX.X, ALU.max, negate=True).then_inc(small.sem, 1)
            dve.wait_ge(*small.after(base + 1))
            if type(s) is not int or s > 0:
                dve.wait_ge(*shift_ready.after(s * CHUNKS))
            nc.vector.tensor_copy(c.shift[:, 0, :], c.rowmax[:]).then_inc(small.sem, 1)
            dve.wait_ge(*small.after(base + 2))
            nc.vector.tensor_tensor(c.rowmax[:], c.rowmax[:], c.shift[:, 0, :], ALU.subtract).then_inc(small.sem, 1)
            dve.wait_ge(*small.after(base + 3))
            nc.vector.tensor_copy(c.shift[:, 1, :], c.rowmax[:]).then_inc(small.sem, 1)
            dve.wait_ge(*small.after(base + 4))
            nc.vector.tensor_tensor(c.shift[:, 2, :], c.rowmax[:], c.shift[:, 1, :], ALU.subtract).then_inc(small.sem, 1)
        if with_exp:
            dve.wait_ge(*pv_done.after(s * PV_STEPS))
            if type(s) is not int or s > 2:
                dve.wait_ge(*out_stored[1 - p].after((i - 1 + p) * 16))
            nc.vector.tensor_copy(c.out_head[:, 1 - p, :], bank(c, 6)).then_inc(out_taken.sem, 1)

    def step_pool(pool, p, i):
        s = 2 * i + p
        if type(s) is not int or s > 1:
            pool.wait_ge(*pv_done.after((s - 1) * PV_STEPS))
        cols = slice(s * HD, (s + 1) * HD) if type(s) is int else bass.ds(s * HD, HD)
        pool.tensor_copy(c.v_head[:, p, :, 0:HD], c.v[:, :, cols]).then_inc(v_staged.sem, 1)

    def load_stacks(sp, p, i):
        s = 2 * i + p
        if type(s) is not int or s > 1:
            sp.wait_ge(*st_ready.after((s - 2) * EXP_UNITS + 1))
        rows = slice(s * HD, (s + 1) * HD) if type(s) is int else bass.ds(s * HD, HD)
        q, k = (c.parts_dram[n, :, rows, :] for n in range(2))
        for a in range(PARTS):
            group = slice(a * PARTS * HD, (a + 1) * PARTS * HD)
            same = q[a:a + 1].broadcast_to((PARTS, HD, N_TOK))
            sp.dma_start(c.q_max[group, p, :], same).then_inc(stack_loaded[p].sem, 16)
            sp.dma_start(c.k_max[group, p, :], k).then_inc(stack_loaded[p].sem, 16)

    def copy_stacks(sp, p, i):
        s = 2 * i + p
        if type(s) is not int or s > 1:
            sp.wait_ge(*pv_done.after((s - 1) * PV_STEPS))
        sp.wait_ge(*stack_loaded[p].after((i + 1) * LOADS * 16))
        sp.dma_start(c.q_exp[0:STACK, p, :], c.q_max[0:STACK, p, :]).then_inc(stack_copied[p].sem, 16)
        sp.dma_start(c.k_exp[0:STACK, p, :], c.k_max[0:STACK, p, :]).then_inc(stack_copied[p].sem, 16)

    def store_out(pool, p, i):
        s = 2 * i + p
        pool.wait_ge(*out_taken.after(s))
        dst = c.out_dram[s - 1] if type(s) is int else c.out_dram[bass.ds(s - 1, 1)].rearrange("o p n -> (o p) n")
        pool.dma_start(dst, c.out_head[:, 1 - p, :]).then_inc(out_stored[1 - p].sem, 16)

    with nc.Block() as block:

        @block.tensor
        def _(pe):
            step_tensor(pe, 0, 0, True, False)
            step_tensor(pe, 1, 0, True, True)
            with pe.Fori(1, HEADS // 2) as i:
                step_tensor(pe, 0, i, True, True)
                step_tensor(pe, 1, i, True, True)
            step_tensor(pe, 0, HEADS // 2, False, True)

        @block.scalar
        def _(act):
            step_scalar(act, 0, 0, True, False)
            step_scalar(act, 1, 0, True, True)
            with act.Fori(1, HEADS // 2) as i:
                step_scalar(act, 0, i, True, True)
                step_scalar(act, 1, i, True, True)
            step_scalar(act, 0, HEADS // 2, False, True)

        @block.vector
        def _(dve):
            step_vector(dve, 0, 0, True, False)
            step_vector(dve, 1, 0, True, True)
            with dve.Fori(1, HEADS // 2) as i:
                step_vector(dve, 0, i, True, True)
                step_vector(dve, 1, i, True, True)
            step_vector(dve, 0, HEADS // 2, False, True)

        @block.gpsimd
        def _(pool):
            step_pool(pool, 0, 0)
            step_pool(pool, 1, 0)
            store_out(pool, 1, 0)
            with pool.Fori(1, HEADS // 2) as i:
                step_pool(pool, 0, i)
                store_out(pool, 0, i)
                step_pool(pool, 1, i)
                store_out(pool, 1, i)
            store_out(pool, 0, HEADS // 2)
            for p in range(2):
                pool.wait_ge(*out_stored[p].after(HEADS // 2 * 16))

        @block.sync
        def _(sp):
            load_stacks(sp, 0, 0)
            load_stacks(sp, 1, 0)
            copy_stacks(sp, 0, 0)
            with sp.Fori(1, HEADS // 2) as i:
                load_stacks(sp, 0, i)
                copy_stacks(sp, 1, i - 1)
                load_stacks(sp, 1, i)
                copy_stacks(sp, 0, i)
            copy_stacks(sp, 1, HEADS // 2 - 1)

    for p in range(2):
        stack_loaded[p].passed(HEADS // 2 * LOADS * 16)
        stack_copied[p].passed(HEADS // 2 * COPIES * 16)
        out_stored[p].passed(HEADS // 2 * 16)
    for sig, n in ((v_staged, HEADS), (max_ready, HEADS * MAX_UNITS),
                   (max_taken, HEADS * MAX_UNITS), (shift_ready, HEADS * CHUNKS),
                   (shift_taken, HEADS * CHUNKS), (small, HEADS * SMALL),
                   (st_ready, HEADS * EXP_UNITS),
                   (exp_done, HEADS * EXP_UNITS), (pv_done, HEADS * PV_STEPS), (out_taken, HEADS)):
        sig.passed(n)


def output_stage(c, w, dst):
    nc = c.nc
    fetched = c.count("out_fetched")
    inverse = c.count("out_inverse")
    ctx_ready = c.count("out_ctx_ready")
    out_ready = c.count("out_ready")
    added = c.count("out_added")
    with nc.Block() as block:

        @block.sync
        def _(sp):
            for k in range(CHUNKS):
                for n in range(2):
                    at = OUT_ROWS * k + n * HD
                    sp.dma_start(c.big[:, n, k * CHUNK:(k + 1) * CHUNK], c.out_dram[:, at:at + HD, :])\
                        .then_inc(fetched.sem, 16)

        @block.vector
        def _(dve):
            dve.wait_ge(*fetched.after(2 * CHUNKS * 16))
            for k in range(CHUNKS):
                num, den = (c.big[:, n, k * CHUNK:(k + 1) * CHUNK] for n in range(2))
                nc.vector.reciprocal(den, den).then_inc(inverse.sem, 1)
                dve.wait_ge(*inverse.after(k + 1))
                nc.vector.tensor_tensor(num, num, den, ALU.mult).then_inc(ctx_ready.sem, 1)
            for k in range(CHUNKS):
                dve.wait_ge(*out_ready.after(k + 1))
                tiles = dst[:, k * TPC:(k + 1) * TPC, :]
                nc.vector.tensor_tensor(tiles, tiles, bank(c, k).rearrange("p (t d) -> p t d", d=D), ALU.add).then_inc(added.sem, 1)

        @block.tensor
        def _(pe):
            for t in range(TILES):
                if t % TPC == 0:
                    pe.wait_ge(*ctx_ready.after(t // TPC + 1))
                ins = nc.tensor.matmul(bank(c, t // TPC)[:, (t % TPC) * P:(t % TPC + 1) * P], c.big[:, 0, t * P:(t + 1) * P],
                                       c.proj[:, w + 3, :], start=True, stop=True)
                if t % TPC == TPC - 1:
                    ins.then_inc(out_ready.sem, 1)

    fetched.passed(2 * CHUNKS * 16)
    inverse.passed(CHUNKS)
    ctx_ready.passed(CHUNKS)
    out_ready.passed(CHUNKS)
    added.passed(CHUNKS)


def feed_forward_stage(c, dst):
    nc = c.nc
    up_ready = c.count("ff_up_ready")
    act_ready = c.count("ff_act_ready")
    out_ready = c.count("ff_out_ready")
    added = c.count("ff_added")
    blocks = D_FF // P
    with nc.Block() as block:

        @block.tensor
        def _(pe):
            def down(k):
                pe.wait_ge(*act_ready.after(blocks * (k + 1)))
                if k >= 2:
                    pe.wait_ge(*added.after(k - 1))
                for t in range(TPC):
                    for b in range(blocks):
                        ins = nc.tensor.matmul(bank(c, 4 + k % 2)[:, t * P:(t + 1) * P], c.hid[:, k % 2, b, t * P:(t + 1) * P],
                                               c.w2[:, b, :], start=(b == 0), stop=(b == blocks - 1))
                ins.then_inc(out_ready.sem, 1)

            for k in range(CHUNKS):
                for b in range(blocks):
                    n = k * blocks + b
                    if n >= 4:
                        pe.wait_ge(*act_ready.after(n - 3))
                    nc.tensor.matmul(bank(c, n % 4), c.w1[:, b * P:(b + 1) * P], c.ht[:, k * CHUNK:(k + 1) * CHUNK],
                                     start=True, stop=True).then_inc(up_ready.sem, 1)
                if k:
                    down(k - 1)
            down(CHUNKS - 1)

        @block.scalar
        def _(act):
            for n in range(CHUNKS * blocks):
                k, b = n // blocks, n % blocks
                act.wait_ge(*up_ready.after(n + 1))
                if k >= 2:
                    act.wait_ge(*out_ready.after(k - 1))
                nc.scalar.activation(c.hid[:, k % 2, b, :], bank(c, n % 4), ACT.Gelu_apprx_tanh,
                                     bias=c.columns["L0_attn_b_b1"][:, b:b + 1]).then_inc(act_ready.sem, 1)

        @block.vector
        def _(dve):
            for k in range(CHUNKS):
                dve.wait_ge(*out_ready.after(k + 1))
                tiles = dst[:, k * TPC:(k + 1) * TPC, :]
                nc.vector.tensor_tensor(tiles, tiles, bank(c, 4 + k % 2).rearrange("p (t d) -> p t d", d=D), ALU.add)\
                    .then_inc(added.sem, 1)

    up_ready.passed(CHUNKS * blocks)
    act_ready.passed(CHUNKS * blocks)
    out_ready.passed(CHUNKS)
    added.passed(CHUNKS)


def experts_stage(c, router, soft_of_probs, gate_w, up_w, down_w, inner, shared=None):
    nc = c.nc
    weights_loaded = [c.count(f"moe_weights_loaded_{p}") for p in range(2)]
    weights_high = c.count("moe_weights_high_ready")
    weights_split = c.count("moe_weights_split")
    high_ready = c.count("moe_ht_high_ready")
    low_ready = c.count("moe_ht_low_ready")
    logits_ready = c.count("moe_logits_ready")
    shifted_ready = c.count("moe_shifted_ready")
    router_exp = c.count("moe_router_exp_ready")
    chain_s = c.count("dve_chain")
    cw_ready = c.count("moe_cw_ready")
    cw_staged = c.count("moe_cw_staged")
    gate_ready = c.count("moe_gate_ready")
    up_ready = c.count("moe_up_ready")
    silu_ready = c.count("moe_silu_ready")
    hid_ready = c.count("moe_hidden_ready")
    out_ready = c.count("moe_out_ready")
    out_added = c.count("moe_out_added")
    J = (inner + P - 1) // P
    sizes = [min(P, inner - j * P) for j in range(J)]
    whole = inner // P
    LOADS = 3 + (1 if inner % P else 0)
    SPLITS = 2
    PAIRS = 4
    UNITS = CHUNKS * J
    E = router.shape[1]
    links = [0]

    def load(sp, p, i, src=None):
        n = 2 * i + p
        if type(n) is not int or n > 1:
            sp.wait_ge(*out_ready.after((n - 1) * CHUNKS))
        if src is None:
            if type(n) is int:
                src = gate_w[n], up_w[n], down_w[n]
            else:
                src = [w[bass.ds(n, 1)].rearrange("o a b -> (o a) b") for w in (gate_w, up_w, down_w)]
        g, u, d = src
        sp.dma_start(c.wg[:, p, 0:inner], g).then_inc(weights_loaded[p].sem, 16)
        sp.dma_start(c.wu[:, p, 0:inner], u).then_inc(weights_loaded[p].sem, 16)
        sp.dma_start(c.wd[:, p, 0:whole, :], d[0:whole * P, :].rearrange("(j p) d -> p j d", p=P)).then_inc(weights_loaded[p].sem, 16)
        if inner % P:
            sp.dma_start(c.wd[0:inner % P, p, whole, :], d[whole * P:inner, :]).then_inc(weights_loaded[p].sem, 16)

    def weight_pieces(p):
        return ((c.wg[:, p, 0:inner], c.wg_part[:, p, :, 0:inner]), (c.wu[:, p, 0:inner], c.wu_part[:, p, :, 0:inner]))

    def high_weights(act, p, i):
        n = 2 * i + p
        act.wait_ge(*weights_loaded[p].after((i + 1) * LOADS * 16))
        if type(n) is not int or n > 1:
            act.wait_ge(*up_ready.after((n - 1) * UNITS))
        for w, part in weight_pieces(p):
            nc.scalar.activation(part[:, 0], w, ACT.Copy).then_inc(weights_high.sem, 1)

    def low_weights(pool, p, i):
        n = 2 * i + p
        for k, (w, part) in enumerate(weight_pieces(p)):
            pool.wait_ge(*weights_high.after(2 * n + k + 1))
            pool.tensor_tensor(part[:, 1], w, part[:, 0], ALU.subtract).then_inc(weights_split.sem, 1)

    PASSES = ((0, 0), (0, 1), (1, 0))

    def expert_tensor(pe, p, i):
        n = 2 * i + p
        pe.wait_ge(*weights_split.after((n + 1) * SPLITS))

        def up(k, j):
            unit = k * J + j
            m = sizes[j]
            for w, at, read, ready in ((c.wg_part, 0, silu_ready, gate_ready), (c.wu_part, 2, hid_ready, up_ready)):
                if unit >= 2 or type(n) is not int or n > 0:
                    pe.wait_ge(*read.after(n * UNITS + unit - 1))
                for a, (u, v) in enumerate(PASSES):
                    ins = nc.tensor.matmul(bank(c, at + unit % 2)[0:m], w[:, p, u, j * P:j * P + m],
                                           c.ht_part[:, v, k * CHUNK:(k + 1) * CHUNK], start=(a == 0), stop=(a == 2))
                ins.then_inc(ready.sem, 1)

        def down(k, tiles):
            if 0 in tiles:
                pe.wait_ge(*hid_ready.after(n * UNITS + (k + 1) * J))
                if k >= 2 or type(n) is not int or n > 0:
                    pe.wait_ge(*out_added.after(n * CHUNKS + k - 1))
            for t in tiles:
                for j in range(J):
                    m = sizes[j]
                    ins = nc.tensor.matmul(bank(c, 4 + k % 2)[:, t * P:(t + 1) * P], c.hid[0:m, k % 2, j, t * P:(t + 1) * P],
                                           c.wd[0:m, p, j, :], start=(j == 0), stop=(j == J - 1))
            if TPC - 1 in tiles:
                ins.then_inc(out_ready.sem, 1)

        for k in range(CHUNKS):
            if type(n) is int and n == 0:
                pe.wait_ge(*low_ready.after(k + 1))
            for j in range(J):
                up(k, j)
                if k:
                    down(k - 1, range(j * TPC // J, (j + 1) * TPC // J))
        down(CHUNKS - 1, range(TPC))

    def expert_scalar(act, p, i):
        n = 2 * i + p
        for unit in range(UNITS):
            m = sizes[unit % J]
            act.wait_ge(*gate_ready.after(n * UNITS + unit + 1))
            if unit >= 2 or type(n) is not int or n > 0:
                act.wait_ge(*hid_ready.after(n * UNITS + unit - 1))
            nc.scalar.activation(c.silu[0:m, unit % 2, :], bank(c, unit % 2)[0:m], ACT.Silu).then_inc(silu_ready.sem, 1)
            if type(n) is int and n == 0 and unit == J - 1:
                router_scalar(act)
            if unit == UNITS // 2 and (type(n) is not int or n < 2 * PAIRS):
                high_weights(act, 1 - p, i + p)

    def add(dve, p, n, k, weighted):
        dve.wait_ge(*out_ready.after(n * CHUNKS + k + 1))
        if k == 0 and weighted:
            dve.wait_ge(*cw_staged.after(n + 1))
        for t in range(TPC):
            tile = c.x[:, k * TPC + t, :]
            out = bank(c, 4 + k % 2)[:, t * P:(t + 1) * P]
            if weighted:
                ins = nc.vector.scalar_tensor_tensor(tile, out, c.cw_now[:, p, k * TPC + t:k * TPC + t + 1], tile,
                                                     ALU.mult, ALU.add)
            else:
                ins = nc.vector.tensor_tensor(tile, tile, out, ALU.add)
        ins.then_inc(out_added.sem, 1)

    def expert_vector(dve, p, i, weighted=True):
        n = 2 * i + p
        for k in range(CHUNKS):
            for j in range(J):
                unit = k * J + j
                m = sizes[j]
                dve.wait_ge(*silu_ready.after(n * UNITS + unit + 1))
                dve.wait_ge(*up_ready.after(n * UNITS + unit + 1))
                if j == 0 and (k >= 2 or type(n) is not int or n > 0):
                    dve.wait_ge(*out_ready.after(n * CHUNKS + k - 1))
                nc.vector.tensor_tensor(c.hid[0:m, k % 2, j, :], c.silu[0:m, unit % 2, :], bank(c, 2 + unit % 2)[0:m],
                                        ALU.mult).then_inc(hid_ready.sem, 1)
            if type(n) is int and n == 0 and k == 0:
                router_vector(dve)
            if k:
                add(dve, p, n, k - 1, weighted)
            elif type(n) is not int or n > 0:
                add(dve, 1 - p, n - 1, CHUNKS - 1, True)
    def expert_pool(pool, p, i):
        n = 2 * i + p
        if type(n) is not int or n > 1:
            pool.wait_ge(*out_added.after((n - 1) * CHUNKS))
        if type(n) is int and n == 0:
            pool.wait_ge(*cw_ready.after(1))
        src = c.cw[:, n, :] if type(n) is int else c.cw[:, bass.ds(n, 1), :].rearrange("p o t -> p (o t)")
        pool.tensor_copy(c.cw_now[:, p, :], src).then_inc(cw_staged.sem, 1)

    def router_scalar(act):
        act.wait_ge(*shifted_ready.after(1))
        nc.scalar.activation(c.probs[:, :, 0:E], c.logits[:, :, 0:E], ACT.Exp).then_inc(router_exp.sem, 1)
        act.wait_ge(*shifted_ready.after(2))
        nc.scalar.activation(c.top_gap[:], c.top_gap[:], ACT.Exp).then_inc(router_exp.sem, 1)

    def router_vector(dve):
        chain = Chain(dve, chain_s)
        v = nc.vector
        logits = c.logits[:, :, 0:E]

        def wide(a):
            return a.broadcast_to((P, TILES, E))

        dve.wait_ge(*logits_ready.after(1))
        chain.link(v.tensor_copy(logits, bank(c, 6, TILES * 16).rearrange("p (t e) -> p t e", e=16)[:, :, 0:E]))
        for t in range(TILES):
            ins = v.max(c.top[:, t, :], c.logits[:, t, 0:E])
        chain.link(ins)
        for t in range(TILES):
            ins = v.max_index(c.top_i[:, t, :], c.top[:, t, :], c.logits[:, t, 0:E])
        chain.link(ins)
        v.tensor_tensor(logits, logits, wide(c.top[:, :, 0:1]), ALU.subtract).then_inc(shifted_ready.sem, 1)
        chain.link(v.tensor_copy(c.top_f[:], c.top_i[:, :, 0:2]))
        if soft_of_probs:
            chain.link(v.tensor_tensor(c.pick[:, :, 0:E], c.ids_wide(E), wide(c.top_f[:, :, 1:2]), ALU.is_equal))
            dve.wait_ge(*router_exp.after(1))
            chain.link(v.reduce_sum(c.total[:], c.probs[:, :, 0:E], AX.X))
            chain.link(v.reciprocal(c.total[:], c.total[:]))
            chain.link(v.tensor_tensor(c.pick[:, :, 0:E], c.pick[:, :, 0:E], c.probs[:, :, 0:E], ALU.mult))
            chain.link(v.reduce_sum(c.second[:], c.pick[:, :, 0:E], AX.X))
            chain.link(v.tensor_scalar(c.second[:], c.second[:], 1.0, None, ALU.subtract))
            v.tensor_tensor(c.top_gap[:], c.second[:], c.total[:], ALU.mult).then_inc(shifted_ready.sem, 1)
        else:
            v.tensor_tensor(c.top_gap[:], c.top[:, :, 1], c.top[:, :, 0], ALU.subtract).then_inc(shifted_ready.sem, 1)
        dve.wait_ge(*router_exp.after(2))
        chain.link(v.tensor_scalar(c.total[:], c.top_gap[:], 1.0, None, ALU.add))
        chain.link(v.reciprocal(c.total[:], c.total[:]))
        chain.link(v.tensor_tensor(c.second[:], c.top_gap[:], c.total[:], ALU.mult))
        out = c.cw[:, 0:E, :].rearrange("p e t -> p t e")
        for n, weight in enumerate((c.total, c.second)):
            chain.link(v.tensor_tensor(c.pick[:, :, 0:E], c.ids_wide(E), wide(c.top_f[:, :, n:n + 1]), ALU.is_equal))
            w3 = wide(weight[:].rearrange("p (t o) -> p t o", o=1))
            chain.link(v.tensor_tensor(c.probs[:, :, 0:E] if n else out, c.pick[:, :, 0:E], w3, ALU.mult))
        v.tensor_tensor(out, out, c.probs[:, :, 0:E], ALU.add).then_inc(cw_ready.sem, 1)
        links[0] = chain.n

    with nc.Block() as block:

        @block.sync
        def _(sp):
            load(sp, 0, 0)
            load(sp, 1, 0)
            with sp.Fori(1, PAIRS) as i:
                load(sp, 0, i)
                load(sp, 1, i)
            load(sp, 0, PAIRS, shared)

        @block.tensor
        def _(pe):
            for t in range(TILES):
                ins = nc.tensor.matmul(bank(c, 6)[:, t * 16:t * 16 + E], c.ht[:, t * P:(t + 1) * P], router[:, 0:E],
                                       start=True, stop=True)
            ins.then_inc(logits_ready.sem, 1)
            expert_tensor(pe, 0, 0)
            expert_tensor(pe, 1, 0)
            with pe.Fori(1, PAIRS) as i:
                expert_tensor(pe, 0, i)
                expert_tensor(pe, 1, i)
            expert_tensor(pe, 0, PAIRS)

        @block.scalar
        def _(act):
            for k in range(CHUNKS):
                cols = slice(k * CHUNK, (k + 1) * CHUNK)
                nc.scalar.activation(c.ht_part[:, 0, cols], c.ht[:, cols], ACT.Copy).then_inc(high_ready.sem, 1)
                if k == 0:
                    high_weights(act, 0, 0)
            expert_scalar(act, 0, 0)
            expert_scalar(act, 1, 0)
            with act.Fori(1, PAIRS) as i:
                expert_scalar(act, 0, i)
                expert_scalar(act, 1, i)
            expert_scalar(act, 0, PAIRS)

        @block.vector
        def _(dve):
            for k in range(CHUNKS):
                cols = slice(k * CHUNK, (k + 1) * CHUNK)
                dve.wait_ge(*high_ready.after(k + 1))
                nc.vector.tensor_tensor(c.ht_part[:, 1, cols], c.ht[:, cols], c.ht_part[:, 0, cols], ALU.subtract)\
                    .then_inc(low_ready.sem, 1)
            expert_vector(dve, 0, 0)
            expert_vector(dve, 1, 0)
            with dve.Fori(1, PAIRS) as i:
                expert_vector(dve, 0, i)
                expert_vector(dve, 1, i)
            expert_vector(dve, 0, PAIRS, weighted=shared is None)
            add(dve, 0, 2 * PAIRS, CHUNKS - 1, shared is None)

        @block.gpsimd
        def _(pool):
            low_weights(pool, 0, 0)
            low_weights(pool, 1, 0)
            expert_pool(pool, 0, 0)
            expert_pool(pool, 1, 0)
            with pool.Fori(1, PAIRS) as i:
                low_weights(pool, 0, i)
                expert_pool(pool, 0, i)
                low_weights(pool, 1, i)
                expert_pool(pool, 1, i)
            low_weights(pool, 0, PAIRS)
            if shared is None:
                expert_pool(pool, 0, PAIRS)

    N = 2 * PAIRS + 1
    for p in range(2):
        weights_loaded[p].passed((PAIRS + 1 - p) * LOADS * 16)
    for s, n in ((weights_high, N * 2), (weights_split, N * SPLITS), (high_ready, CHUNKS), (low_ready, CHUNKS), (logits_ready, 1),
                 (shifted_ready, 2), (router_exp, 2), (chain_s, links[0]), (cw_ready, 1),
                 (cw_staged, N if shared is None else N - 1), (gate_ready, N * UNITS), (up_ready, N * UNITS), (silu_ready, N * UNITS),
                 (hid_ready, N * UNITS), (out_ready, N * CHUNKS),
                 (out_added, N * CHUNKS)):
        s.passed(n)


def store_stage(c, out):
    nc = c.nc
    stored = c.count("result_stored")
    with nc.Block() as block:
        @block.sync
        def _(sp):
            sp.dma_start(out.rearrange("b (t p) d -> p (b t) d", p=P), c.x[:]).then_inc(stored.sem, 16)
            sp.wait_ge(*stored.after(16))
    stored.passed(16)


PROJ = [f"L0_attn_b_W{x}" for x in "qkvo"] + [f"L1_attn_a_W{x}_T" for x in "qkvo"] + [f"L1_ffn_w{x}" for x in "qkvo"]


def hybrid_stack(nc, i, out, layers="abcdefgh"):
    with ExitStack() as ctx:
        c = Core(nc, ctx)
        c.i = i
        c.x = c.sbuf("x", [P, TILES, D])
        c.h = c.sbuf("h", [P, TILES, D])
        c.n = c.sbuf("n", [P, TILES, D])
        c.ht = c.sbuf("ht", [P, N_TOK])
        c.decay = c.sbuf("decay", [P, 1])
        c.mx = c.sbuf("mx", [P, TILES, CHUNKS])
        c.rowmax = c.sbuf("rowmax", [P, TILES])
        c.shift = c.sbuf("shift", [P, PARTS, TILES], bf16)
        c.ident = c.sbuf("ident", [P, P])
        c.ident16 = c.sbuf("ident16", [P, P], bf16)
        c.flip = c.sbuf("flip", [P, P])
        c.mask_q = c.sbuf("mask_q", [P, 2, 2, 2 * P], bf16)
        c.mask_k = c.sbuf("mask_k", [P, 2, 2 * P], bf16)
        c.bn = c.sbuf("bn", [P, TILES, 6])
        c.mv = c.sbuf("mv", [P, TILES, 2])
        c.mean2 = c.sbuf("mean2", [P, TILES])
        c.rstd = c.sbuf("rstd", [P, TILES])
        c.minus_half = c.sbuf("minus_half", [P, TILES])
        c.expert_ids_i = c.sbuf("expert_ids_i", [P, 16], mybir.dt.int32)
        c.expert_ids = c.sbuf("expert_ids", [P, 16])
        c.ids_wide = lambda e: c.expert_ids[:, 0:e].rearrange("p (o e) -> p o e", o=1).broadcast_to((P, TILES, e))
        c.logits = c.sbuf("logits", [P, TILES, 16])
        c.probs = c.sbuf("probs", [P, TILES, 16])
        c.pick = c.sbuf("pick", [P, TILES, 16])
        c.top = c.sbuf("top", [P, TILES, 8])
        c.top_i = c.sbuf("top_i", [P, TILES, 8], u32)
        c.top_f = c.sbuf("top_f", [P, TILES, 2])
        c.top_gap = c.sbuf("top_gap", [P, TILES])
        c.total = c.sbuf("total", [P, TILES])
        c.second = c.sbuf("second", [P, TILES])
        c.cw = c.sbuf("cw", [P, 9, TILES])
        c.cw_now = c.sbuf("cw_now", [P, 2, TILES])
        c.conv_w = c.sbuf("conv_w", [P, 2, TAPS])
        c.w_in = c.sbuf("w_in", [P, 2 * INNER])
        c.w_b = c.sbuf("w_b", [P, 2, STATE])
        c.w_c = c.sbuf("w_c", [STATE, INNER])
        c.w_out = c.sbuf("w_out", [P, 2, D])
        c.w1 = c.sbuf("w1", [P, D_FF])
        c.w2 = c.sbuf("w2", [P, D_FF // P, D])
        c.router0 = c.sbuf("router0", [P, 9])
        c.router1 = c.sbuf("router1", [P, 8])
        c.proj_names = PROJ
        c.proj = c.sbuf("proj", [P, len(PROJ), D])
        c.keys_twice = c.sbuf("keys_twice", [2, 2 * D])
        c.circ = c.sbuf("circ", [P, 2, D])
        c.circ_a = c.sbuf("circ_a", [P, D])
        c.circ_b = c.sbuf("circ_b", [P, D])
        c.columns = {name: c.sbuf("col_" + name, [P, n])[:] for name, n in (
            ("L0_attn_a_conv_b", 2), ("L0_attn_a_D_param", 2), ("L0_attn_b_bq", 1), ("L0_attn_b_bk", 1),
            ("L0_attn_b_ln1_w", 1), ("L0_attn_b_ln1_b", 1), ("L0_attn_b_ln2_w", 1), ("L0_attn_b_ln2_b", 1),
            ("L0_attn_b_b1", 4), ("L1_ffn_norm1_w", 1), ("L1_ffn_norm2_w", 1))}
        c.rows = {name: c.sbuf("row_" + name, [P, n])[:] for name, n in (
            ("L0_attn_a_ln_gamma", D), ("L0_attn_a_ln_beta", D), ("L0_attn_b_bv", D), ("L0_attn_b_bo", D),
            ("L0_attn_b_b2", D), ("L1_attn_b_decay", 1), ("L1_attn_b_gate", 1))}
        c.ps = ctx.enter_context(nc.psum_tensor("ps", [P, 8 * CHUNK], fp32))
        c.parts_dram = nc.dram_tensor("parts_dram", (2, 3, D, N_TOK), bf16).ap()
        c.out_dram = nc.dram_tensor("out_dram", (HEADS, P, CHUNK), fp32).ap()
        c.keys_dram = nc.dram_tensor("keys_dram", (2, 2 * D), fp32).ap()

        constants_stage(c)

        def state_space():
            held, m = c.layer((("big", [P, 6, N_TOK], fp32), ("conv", [P, 2, N_TOK], fp32)))
            with held:
                c.big, c.conv = m["big"], m["conv"]
                c.bu, c.state = c.conv[:, 0, :], c.conv[:, 1, :]
                norm_stage(c, c.x, c.h, transpose=True)
                state_space_stage(c)
                norm_stage(c, c.h, c.n)
                add_stage(c, c.x, c.n, scale_row=c.rows["L0_attn_a_ln_gamma"], row=c.rows["L0_attn_a_ln_beta"])

        def experts(router, soft_of_probs, weights, inner, shared=None):
            J = (inner + P - 1) // P
            held, m = c.layer((("ht_part", [P, 2, N_TOK], fp32r), ("wg", [P, 2, inner], fp32), ("wu", [P, 2, inner], fp32),
                               ("wd", [P, 2, J, D], fp32), ("wg_part", [P, 2, 2, inner], fp32r),
                               ("wu_part", [P, 2, 2, inner], fp32r), ("silu", [P, 2, CHUNK], fp32),
                               ("hid", [P, 2, J, CHUNK], fp32)))
            with held:
                c.ht_part, c.silu, c.hid = m["ht_part"], m["silu"], m["hid"]
                c.wg, c.wu, c.wd = m["wg"], m["wu"], m["wd"]
                c.wg_part, c.wu_part = m["wg_part"], m["wu_part"]
                experts_stage(c, router, soft_of_probs, *(i[w] for w in weights), inner,
                              shared=[i[w] for w in shared] if shared else None)

        def experts0():
            norm_stage(c, c.x, c.h, transpose=True)
            experts(c.router0, False, ("L0_ffn_Wg", "L0_ffn_Wu", "L0_ffn_Wd"), 352)

        def attention(w, window=None, dst=None, bq=None, bk=None, bv=None):
            held, m = c.layer((("qk", [P, 2, N_TOK], fp32), ("prob", [P, P_UNITS, UNIT], fp32),
                               ("parts", [P, 2, PARTS, N_TOK], bf16), ("q_max", [P, 2, N_TOK], bf16),
                               ("q_exp", [P, 2, N_TOK], bf16), ("k_max", [P, 2, N_TOK], bf16),
                               ("k_exp", [P, 2, N_TOK], bf16), ("v", [P, TILES, D], fp32),
                               ("v_head", [P, 2, TILES, OUT_ROWS], fp32), ("out_head", [P, 2, CHUNK], fp32)))
            with held:
                c.big, c.prob, c.parts, c.v = m["qk"], m["prob"], m["parts"], m["v"]
                c.q_max, c.q_exp, c.k_max, c.k_exp = m["q_max"], m["q_exp"], m["k_max"], m["k_exp"]
                c.v_head, c.out_head = m["v_head"], m["out_head"]
                project_stage(c, w, bq, bk, bv)
                heads_stage(c, window)
                output_stage(c, w, dst)

        def experts1():
            norm_stage(c, c.x, c.h)
            norm_stage(c, c.h, c.n, rms=True, transpose=True, scale=c.columns["L1_ffn_norm1_w"])
            attention(8, dst=c.h)
            norm_stage(c, c.h, c.n, rms=True, transpose=True, scale=c.columns["L1_ffn_norm2_w"])
            add_stage(c, c.x, c.h)
            experts(c.router1, True, ("L1_ffn_e_gate", "L1_ffn_e_up", "L1_ffn_e_down"), 256,
                    shared=("L1_ffn_sh_gate", "L1_ffn_sh_up", "L1_ffn_sh_down"))

        def local_attention():
            norm_stage(c, c.x, c.h)
            norm_stage(c, c.h, c.n, transpose=True, scale=c.columns["L0_attn_b_ln1_w"], shift=c.columns["L0_attn_b_ln1_b"])
            attention(0, window=0, dst=c.h, bq=c.columns["L0_attn_b_bq"], bk=c.columns["L0_attn_b_bk"],
                      bv=c.rows["L0_attn_b_bv"])
            add_stage(c, c.h, row=c.rows["L0_attn_b_bo"])
            norm_stage(c, c.h, c.n, transpose=True, scale=c.columns["L0_attn_b_ln2_w"], shift=c.columns["L0_attn_b_ln2_b"])
            held, m = c.layer((("ff_hid", [P, 2, D_FF // P, CHUNK], fp32),))
            with held:
                c.hid = m["ff_hid"]
                feed_forward_stage(c, c.h)
            add_stage(c, c.x, c.h, row=c.rows["L0_attn_b_b2"])

        def hologram():
            norm_stage(c, c.x, c.h, transpose=True)
            held, m = c.layer((("scan", [P, 1, N_TOK], fp32),))
            with held:
                c.big = m["scan"]
                hologram_stage(c)
            add_stage(c, c.x, c.h)

        if "a" in layers:
            state_space()
        if "b" in layers:
            experts0()
        if "c" in layers:
            local_attention()
        if "d" in layers:
            experts0()
        if "e" in layers:
            norm_stage(c, c.x, c.h, transpose=True)
            attention(4, window=1, dst=c.x)
        if "f" in layers:
            experts1()
        if "g" in layers:
            hologram()
        if "h" in layers:
            experts1()
        store_stage(c, out)


TRANSPOSED = ("L0_attn_a_W_in", "L0_attn_a_W_B", "L0_attn_a_W_C", "L0_attn_a_W_out",
              "L1_attn_a_Wq", "L1_attn_a_Wk", "L1_attn_a_Wv", "L1_attn_a_Wo")


def kernel(**inputs):
    import numpy as _np
    import concourse.bacc as _bacc
    from concourse import mybir as _mybir
    from concourse.bass_utils import run_bass_kernel_spmd as _run

    nc = _bacc.Bacc("TRN2", target_bir_lowering=False, num_devices=1)
    arrays, aps = {}, {}
    for name, a in inputs.items():
        a = _np.asarray(a)
        if name in TRANSPOSED:
            name, a = name + "_T", a.T
        a = _np.ascontiguousarray(a if a.ndim else a.reshape(1))
        arrays[f"in_{name}_dram"] = a
        aps[name] = nc.dram_tensor(f"in_{name}_dram", a.shape, _mybir.dt.from_np(a.dtype), kind="ExternalInput").ap()
    out = nc.dram_tensor("out_0_dram", (1, N_TOK, D), fp32, kind="ExternalOutput").ap()
    hybrid_stack(nc, aps, out)
    r = _run(nc, [arrays], core_ids=[0])
    return r.results[0]["out_0_dram"]
```

```python
import concourse.bass as bass
from concourse import mybir
from contextlib import ExitStack
from functools import partial

fp32 = mybir.dt.float32
bf16 = mybir.dt.bfloat16
fp32r = mybir.dt.float32r
u32 = mybir.dt.uint32
ALU = mybir.AluOpType
ACT = mybir.ActivationFunctionType
AX = mybir.AxisListType

P = 128
N_TOK = 2048
D = 128
TILES = N_TOK // P
CHUNK = 512
CHUNKS = N_TOK // CHUNK
TPC = CHUNK // P
HEADS = 16
HD = D // HEADS
EARLY = HEADS - 2
INNER = 256
STATE = 64
TAPS = 4
D_FF = 512
LN_EPS = 1e-5
RMS_EPS = 1e-6
MASKED = -1.0e30
PARTS = 3
STACK = PARTS * PARTS * HD
SHIFT_AT = 96
UNIT = 1024
WINDOWS = (128, 63)
BEFORE = (128, 64)
P_UNITS = 8
OUT_ROWS = 32


class Count:

    def __init__(self, sem):
        self.sem = sem
        self.at = 0

    def after(self, n):
        return self.sem, self.at + n

    def passed(self, n):
        self.at = self.at + n


class Core:

    def __init__(self, nc, ctx):
        self.nc = nc
        self.ctx = ctx
        self.counts = {}
        self.layers = 0

    def sbuf(self, name, shape, dt=fp32):
        return self.ctx.enter_context(self.nc.sbuf_tensor(name, shape, dt))

    def layer(self, buffers):
        held = ExitStack()
        self.layers = self.layers + 1
        made = {name: held.enter_context(self.nc.sbuf_tensor(f"{name}_{self.layers}", shape, dt))
                for name, shape, dt in buffers}
        return held, made

    def count(self, name):
        if name not in self.counts:
            self.counts[name] = Count(self.ctx.enter_context(self.nc.semaphore(name)))
        return self.counts[name]


class Chain:

    def __init__(self, engine, steps):
        self.engine = engine
        self.steps = steps
        self.n = 0
        self.offset = 0

    def mark(self, ins):
        ins.then_inc(self.steps.sem, 1)
        self.n += 1

    def link(self, ins):
        self.mark(ins)
        self.engine.wait_ge(*self.steps.after(self.offset + self.n))


def along(row):
    return row.rearrange("p (o d) -> p o d", o=1).broadcast_to((P, TILES, D))


def bank(c, n, width=CHUNK):
    return c.ps[:, n * CHUNK:n * CHUNK + width]


def constants_stage(c):
    nc = c.nc
    built = c.count("const_built")
    loaded = c.count("const_loaded")
    n_pool = [0]
    with nc.Block() as block:

        @block.gpsimd
        def _(pool):
            def step(ins):
                ins.then_inc(built.sem, 1)
                n_pool[0] += 1
                pool.wait_ge(*built.after(n_pool[0]))

            step(pool.memset(c.minus_half[:], -0.5))
            step(pool.memset(c.ident[:], 0.0))
            step(pool.affine_select(out=c.ident[:], in_=c.ident[:], compare_op=ALU.not_equal, fill=1.0,
                                    base=0, pattern=[[-1, P]], channel_multiplier=1))

        @block.sync
        def _(sp):
            sp.dma_start(c.x[:], c.i["L0_attn_a_x"].rearrange("b (t p) d -> p (b t) d", p=P)).then_inc(loaded.sem, 16)
            sp.wait_ge(*loaded.after(16))

    built.passed(n_pool[0])
    loaded.passed(16)


def load_first_layer(c, sp):
    loaded = c.count("const_first_layer_loaded")
    w_in = c.i["L0_attn_a_W_in_T"]
    columns = [(c.columns[name][:, n:n + 1], c.i[name][n * P:(n + 1) * P].rearrange("(p o) -> p o", o=1))
               for name in ("L0_attn_a_conv_b", "L0_attn_a_D_param") for n in range(2)]
    loads = [(c.w_in[:], w_in), (c.conv_w[:], c.i["L0_attn_a_conv_w"].rearrange("(n p) o k -> p n (o k)", p=P))] + columns
    loads += [(c.rows[name], c.i[name].partition_broadcast(P)) for name in ("L0_attn_a_ln_gamma", "L0_attn_a_ln_beta")]
    loads += [(c.w_b[:], c.i["L0_attn_a_W_B_T"].rearrange("(n p) s -> p n s", p=P)), (c.w_c[:], c.i["L0_attn_a_W_C_T"]),
              (c.w_out[:], c.i["L0_attn_a_W_out_T"].rearrange("(n p) d -> p n d", p=P))]
    for dst, src in loads:
        sp.dma_start(dst, src).then_inc(loaded.sem, 16)
    sp.wait_ge(*loaded.after(16 * len(loads)))
    return len(loads)


def build_later_constants(c, pool):
    built = c.count("const_later_built")
    n_built = [0]

    def step(ins):
        ins.then_inc(built.sem, 1)
        n_built[0] += 1
        pool.wait_ge(*built.after(n_built[0]))

    def keep(view, width, base, coef, step_, fill):
        step(pool.affine_select(out=view, in_=view, compare_op=ALU.is_ge, fill=fill, base=base,
                                pattern=[[step_, width]], channel_multiplier=coef))

    step(pool.tensor_copy(c.ident16[:], c.ident[:]))
    step(pool.memset(c.flip[:], 0.0))
    for total in (0, D):
        step(pool.affine_select(out=c.flip[:], in_=c.flip[:], compare_op=ALU.not_equal, fill=1.0,
                                base=-total, pattern=[[1, P]], channel_multiplier=1))
    step(pool.iota(c.expert_ids_i[:], pattern=[[1, 16]], base=0, channel_multiplier=0))
    step(pool.tensor_copy(c.expert_ids[:], c.expert_ids_i[:]))
    for n, back in enumerate(WINDOWS):
        for first in (False, True):
            m = c.mask_q[:, n, 1 if first else 0, :]
            step(pool.memset(m, 0.0))
            keep(m, 2 * P, P, 1, -1, MASKED)
            keep(m, 2 * P, back - P, -1, 1, MASKED)
            if first:
                keep(m, 2 * P, -P, 0, 1, MASKED)
        m = c.mask_k[:, n, :]
        step(pool.memset(m, 0.0))
        keep(m, 2 * P, 0, -1, 1, MASKED)
        keep(m, 2 * P, back, 1, -1, MASKED)
    return n_built[0]


def load_later_constants(c, sp):
    n_loaded = 0
    loaded = c.count("const_later_loaded")

    def load(dst, src):
        sp.dma_start(dst, src).then_inc(loaded.sem, 16)

    columns = [(name, dst) for name, dst in c.columns.items() if not name.startswith("L0_attn_a")]
    for name, dst in columns:
        for n in range(dst.shape[1]):
            load(dst[:, n:n + 1], c.i[name][n * P:(n + 1) * P].rearrange("(p o) -> p o", o=1))
            n_loaded += 1
    for name, dst in c.rows.items():
        if not name.startswith("L0_attn_a"):
            load(dst, c.i[name].partition_broadcast(P))
            n_loaded += 1
    load(c.w1[:], c.i["L0_attn_b_W1"])
    load(c.w2[:], c.i["L0_attn_b_W2"].rearrange("(n p) d -> p n d", p=P))
    load(c.router0[:], c.i["L0_ffn_Wr"])
    load(c.router1[:], c.i["L1_ffn_router_w"])
    n_loaded += 4
    for n, name in enumerate(c.proj_names):
        load(c.proj[:, n, :], c.i[name])
        n_loaded += 1
    for s, name in enumerate(("bind", "unbind")):
        key = c.i[f"L1_attn_b_{name}_key"].rearrange("(o n) -> o n", o=1)
        for half in range(2):
            load(c.keys_twice[s:s + 1, half * D:(half + 1) * D], key)
            n_loaded += 1
    sp.wait_ge(*loaded.after(16 * n_loaded))
    return n_loaded


def later_constants_stage(c):
    n_loaded = [0]
    n_built = [0]
    with c.nc.Block() as block:
        @block.sync
        def _(sp):
            n_loaded[0] = load_later_constants(c, sp)

        @block.gpsimd
        def _(pool):
            n_built[0] = build_later_constants(c, pool)
    c.count("const_later_loaded").passed(16 * n_loaded[0])
    c.count("const_later_built").passed(n_built[0])


def norm_stage(c, src, dst, rms=False, transpose=False, scale=None, shift=None, first=False, router=None, onto=None,
               experts=None):
    nc = c.nc
    eps = RMS_EPS if rms else LN_EPS
    chain_s = c.count("dve_chain")
    stats_ready = c.count("norm_stats_ready")
    rstd_ready = c.count("norm_rstd_ready")
    tile_ready = c.count("norm_tile_ready")
    bank_ready = c.count("norm_bank_ready")
    bank_taken = c.count("norm_bank_taken")
    links = [0]
    logits_ready = c.count("router_logits_ready")
    high_ready = c.count("norm_ht_high_ready")
    inner = experts[0].shape[2] if experts is not None else 0
    summed = c.count("norm_onto_summed")
    n_loaded = [0]
    with nc.Block() as block:

        def rank(chain):
            E = router.shape[1]
            for k in range(CHUNKS):
                tiles = range(k * TPC, (k + 1) * TPC)
                chain.engine.wait_ge(*logits_ready.after(k + 1))
                logits = bank(c, 4 + k, TPC * 16).rearrange("p (t e) -> p t e", e=16)[:, :, 0:E]
                cols = slice(k * CHUNK, (k + 1) * CHUNK)
                chain.engine.wait_ge(*high_ready.after(k + 1))
                nc.vector.tensor_tensor(c.ht_part[:, 1, cols], c.ht[:, cols], c.ht_part[:, 0, cols], ALU.subtract)
                chain.link(nc.vector.tensor_copy(c.logits[:, k * TPC:(k + 1) * TPC, 0:E], logits))
                for t in tiles:
                    ins = nc.vector.max(c.top[:, t, :], c.logits[:, t, 0:E])
                chain.link(ins)
                for t in tiles:
                    nc.vector.max_index(c.top_i[:, t, :], c.top[:, t, :], c.logits[:, t, 0:E])

        @block.vector
        def _(dve):
            chain = Chain(dve, chain_s)

            def statistics(g):
                tiles = slice(g * TPC, (g + 1) * TPC)
                for t in range(g * TPC, (g + 1) * TPC):
                    ins = nc.vector.bn_stats(c.bn[:, t, :], src[:, t, :])
                chain.link(ins)
                for t in range(g * TPC, (g + 1) * TPC):
                    ins = nc.vector.bn_aggr(c.mv[:, t, :], c.bn[:, t, :])
                if rms:
                    chain.link(ins)
                    mean = c.mv[:, tiles, 0]
                    chain.link(nc.vector.tensor_tensor(c.mean2[:, tiles], mean, mean, ALU.mult))
                    ins = nc.vector.tensor_tensor(c.mv[:, tiles, 1], c.mv[:, tiles, 1], c.mean2[:, tiles], ALU.add)
                ins.then_inc(stats_ready.sem, 1)

            def normalise(g):
                dve.wait_ge(*rstd_ready.after(2 * (g + 1)))
                for t in range(g * TPC, (g + 1) * TPC):
                    if rms:
                        ins = nc.vector.tensor_scalar(dst[:, t, :], src[:, t, :], c.rstd[:, t:t + 1], None, ALU.mult)
                    else:
                        ins = nc.vector.tensor_scalar(dst[:, t, :], src[:, t, :], c.mv[:, t, 0:1], c.rstd[:, t:t + 1],
                                                      ALU.subtract, ALU.mult)
                    ins.then_inc(tile_ready.sem, 1)

            lag = 2 if router is None else 1
            for g in range(CHUNKS + lag):
                if g < CHUNKS:
                    statistics(g)
                if g >= lag:
                    normalise(g - lag)
            if router is not None:
                rank(chain)
            links[0] = chain.n

        @block.gpsimd
        def _(pool):
            for g in range(CHUNKS):
                tiles = slice(g * TPC, (g + 1) * TPC)
                pool.wait_ge(*stats_ready.after(g + 1))
                pool.tensor_scalar(c.rstd[:, tiles], c.mv[:, tiles, 1], eps, None, ALU.add).then_inc(rstd_ready.sem, 1)
                pool.wait_ge(*rstd_ready.after(2 * g + 1))
                pool.tensor_tensor(c.rstd[:, tiles], c.rstd[:, tiles], c.minus_half[:, tiles], ALU.pow)\
                    .then_inc(rstd_ready.sem, 1)
            if experts is not None:
                make_low_weights(c, pool, 0, inner, 0)
            if onto is not None:
                pool.tensor_tensor(onto[:], onto[:], src[:], ALU.add).then_inc(summed.sem, 1)

        if experts is not None:
            @block.sync
            def _(sp):
                for p in range(2):
                    load_expert(c, sp, p, [w[p] for w in experts])

        if first:
            @block.sync
            def _(sp):
                n_loaded[0] = load_first_layer(c, sp)

        def route(pe, k):
            pe.wait_ge(*bank_taken.after(k + 1))
            E = router.shape[1]
            for t in range(k * TPC, (k + 1) * TPC):
                ins = nc.tensor.matmul(bank(c, 4 + k)[:, (t % TPC) * 16:(t % TPC) * 16 + E], c.ht[:, t * P:(t + 1) * P], router[:, 0:E],
                                       start=True, stop=True)
            ins.then_inc(logits_ready.sem, 1)

        if transpose:
            @block.tensor
            def _(pe):
                for t in range(TILES):
                    pe.wait_ge(*tile_ready.after(t + 1))
                    out = bank(c, t // TPC)[:, (t % TPC) * P:(t % TPC + 1) * P]
                    ins = nc.tensor.transpose(out, dst[:, t, :], c.ident[:])
                    if t % TPC == TPC - 1:
                        ins.then_inc(bank_ready.sem, 1)
                        if router is not None and t > TPC:
                            route(pe, t // TPC - 1)
                if router is not None:
                    route(pe, CHUNKS - 1)

            @block.scalar
            def _(act):
                for b in range(CHUNKS):
                    act.wait_ge(*bank_ready.after(b + 1))
                    outs = [(c.ht[:, b * CHUNK:(b + 1) * CHUNK], bank_taken)]
                    if experts is not None:
                        outs.append((c.ht_part[:, 0, b * CHUNK:(b + 1) * CHUNK], high_ready))
                    for out, taken in outs:
                        if scale is None:
                            nc.scalar.activation(out, bank(c, b), ACT.Copy).then_inc(taken.sem, 1)
                        else:
                            nc.scalar.activation(out, bank(c, b), ACT.Identity, scale=scale,
                                                 bias=shift if shift is not None else 0.0).then_inc(taken.sem, 1)
                    if experts is not None and b == 0:
                        act.wait_ge(*c.count("moe_weights_loaded_0").after(loads_of_expert(inner) * 16))
                        make_high_weights(c, 0, inner)

    chain_s.passed(links[0])
    stats_ready.passed(CHUNKS)
    rstd_ready.passed(2 * CHUNKS)
    tile_ready.passed(TILES)
    if router is not None:
        logits_ready.passed(CHUNKS)
        high_ready.passed(CHUNKS)
    if onto is not None:
        summed.passed(1)
    if first:
        c.count("const_first_layer_loaded").passed(16 * n_loaded[0])
    if transpose:
        bank_ready.passed(CHUNKS)
        bank_taken.passed(CHUNKS)


def state_space_stage(c):
    nc = c.nc
    proj_ready = c.count("ss_proj_ready")
    proj_taken = c.count("ss_proj_taken")
    conv_ready = c.count("ss_conv_ready")
    u_ready = c.count("ss_u_ready")
    bu_ready = c.count("ss_bu_ready")
    bu_taken = c.count("ss_bu_taken")
    state_ready = c.count("ss_state_ready")
    y_ready = c.count("ss_y_ready")
    y_taken = c.count("ss_y_taken")
    out_ready = c.count("ss_out_ready")
    added = c.count("ss_added")
    chain_s = c.count("dve_chain")
    blocks = INNER // P
    xin, u, gate = c.big[:, 0:2, :], c.big[:, 2:4, :], c.big[:, 4:6, :]
    bu, state = c.bu, c.state
    PAD = TAPS - 1
    beta_added = c.count("ss_beta_added")
    links = [0]
    n_loaded = [0]
    n_built = [0]
    with nc.Block() as block:

        @block.sync
        def _(sp):
            n_loaded[0] = load_later_constants(c, sp)

        @block.gpsimd
        def _(pool):
            n_built[0] = build_later_constants(c, pool)
            pool.tensor_tensor(c.x[:], c.x[:], along(c.rows["L0_attn_a_ln_beta"]), ALU.add).then_inc(beta_added.sem, 1)

        @block.tensor
        def _(pe):
            def project(k):
                for b in range(2 * blocks):
                    n = k * 2 * blocks + b
                    if n >= 8:
                        pe.wait_ge(*proj_taken.after(n - 7))
                    nc.tensor.matmul(bank(c, n % 8), c.w_in[:, b * P:(b + 1) * P],
                                     c.ht[:, k * CHUNK:(k + 1) * CHUNK], start=True, stop=True).then_inc(proj_ready.sem, 1)

            def into_state(k):
                pe.wait_ge(*u_ready.after(blocks * (k + 1)))
                if k >= 2:
                    pe.wait_ge(*bu_taken.after(k - 1))
                for b in range(blocks):
                    ins = nc.tensor.matmul(bank(c, k % 2)[0:STATE, :], c.w_b[:, b, :], u[:, b, k * CHUNK:(k + 1) * CHUNK],
                                           start=(b == 0), stop=(b == blocks - 1))
                ins.then_inc(bu_ready.sem, 1)

            def from_state(k):
                pe.wait_ge(*state_ready.after(k + 1))
                if k >= 2:
                    pe.wait_ge(*y_taken.after(k - 1))
                for b in range(blocks):
                    ins = nc.tensor.matmul(bank(c, 2 + k % 2 * blocks + b), c.w_c[:, b * P:(b + 1) * P],
                                           state[0:STATE, k * CHUNK:(k + 1) * CHUNK], start=True, stop=True)
                ins.then_inc(y_ready.sem, 1)

            def output(k):
                pe.wait_ge(*y_taken.after(k + 1))
                if k >= 2:
                    pe.wait_ge(*added.after(k - 1))
                for t in range(k * TPC, (k + 1) * TPC):
                    for b in range(blocks):
                        ins = nc.tensor.matmul(bank(c, 6 + k % 2)[:, (t % TPC) * P:(t % TPC + 1) * P],
                                               u[:, b, t * P:(t + 1) * P], c.w_out[:, b, :], start=(b == 0), stop=(b == blocks - 1))
                ins.then_inc(out_ready.sem, 1)

            for k in range(CHUNKS):
                project(k)
            pe.wait_ge(*proj_taken.after(2 * blocks * CHUNKS))
            into_state(0)
            into_state(1)
            for k in range(CHUNKS):
                from_state(k)
                if k:
                    output(k - 1)
                if k + 2 < CHUNKS:
                    into_state(k + 2)
            output(CHUNKS - 1)

        @block.scalar
        def _(act):
            def take_projection(k):
                cols = slice(k * CHUNK, (k + 1) * CHUNK)
                for b in range(2 * blocks):
                    n = k * 2 * blocks + b
                    act.wait_ge(*proj_ready.after(n + 1))
                    if b < blocks:
                        nc.scalar.activation(xin[:, b, cols], bank(c, n % 8), ACT.Copy).then_inc(proj_taken.sem, 1)
                    else:
                        nc.scalar.activation(gate[:, b - blocks, cols], bank(c, n % 8), ACT.Silu).then_inc(proj_taken.sem, 1)

            def take_conv(k):
                cols = slice(k * CHUNK, (k + 1) * CHUNK)
                act.wait_ge(*conv_ready.after(k + 1))
                for b in range(blocks):
                    nc.scalar.activation(u[:, b, cols], c.conv[:, b, cols], ACT.Silu).then_inc(u_ready.sem, 1)

            def take_bu(k):
                act.wait_ge(*bu_ready.after(k + 1))
                nc.scalar.activation(bu[0:STATE, k * CHUNK:(k + 1) * CHUNK], bank(c, k % 2)[0:STATE, :], ACT.Copy,
                                     scale=0.05).then_inc(bu_taken.sem, 1)

            for k in range(CHUNKS - 1):
                take_projection(k)
            take_conv(0)
            take_projection(CHUNKS - 1)
            take_conv(1)
            for k in range(CHUNKS):
                take_bu(k)
                if k + 2 < CHUNKS:
                    take_conv(k + 2)

        @block.vector
        def _(dve):
            chain = Chain(dve, chain_s)

            def conv(k):
                dve.wait_ge(*proj_taken.after(k * 2 * blocks + blocks))
                at, end = k * CHUNK, (k + 1) * CHUNK
                for b in range(blocks):
                    ins = nc.vector.tensor_scalar(c.conv[:, b, at:end], xin[:, b, at:end], c.conv_w[:, b, PAD:TAPS],
                                                  c.columns["L0_attn_a_conv_b"][:, b:b + 1], ALU.mult, ALU.add)
                for back in range(1, TAPS):
                    chain.link(ins)
                    first = max(at, back)
                    for b in range(blocks):
                        tail = c.conv[:, b, first:end]
                        ins = nc.vector.scalar_tensor_tensor(tail, xin[:, b, first - back:end - back],
                                                             c.conv_w[:, b, PAD - back:TAPS - back], tail, ALU.mult, ALU.add)
                ins.then_inc(conv_ready.sem, 1)

            def scan(k):
                at, end = k * CHUNK, (k + 1) * CHUNK
                dve.wait_ge(*bu_taken.after(k + 1))
                if k:
                    dve.wait_ge(*state_ready.after(k))
                nc.vector.tensor_tensor_scan(state[0:STATE, at:end], c.decay[0:STATE, 0:1].broadcast_to((STATE, CHUNK)),
                                             bu[0:STATE, at:end], state[0:STATE, at - 1:at] if k else 0.0,
                                             ALU.mult, ALU.add).then_inc(state_ready.sem, 1)

            def gated(k):
                cols = slice(k * CHUNK, (k + 1) * CHUNK)
                dve.wait_ge(*y_ready.after(k + 1))
                for b in range(blocks):
                    ins = nc.vector.scalar_tensor_tensor(u[:, b, cols], u[:, b, cols], c.columns["L0_attn_a_D_param"][:, b:b + 1],
                                                         bank(c, 2 + k % 2 * blocks + b), ALU.mult, ALU.add)
                chain.link(ins)
                for b in range(blocks):
                    ins = nc.vector.tensor_tensor(u[:, b, cols], u[:, b, cols], gate[:, b, cols], ALU.mult)
                ins.then_inc(y_taken.sem, 1)

            def add(k):
                dve.wait_ge(*out_ready.after(k + 1))
                tiles = c.h[:, k * TPC:(k + 1) * TPC, :]
                nc.vector.tensor_tensor(tiles, tiles, bank(c, 6 + k % 2).rearrange("p (t d) -> p t d", d=D), ALU.add).then_inc(added.sem, 1)

            chain.link(nc.vector.memset(c.decay[:], 0.95))
            conv(0)
            conv(1)
            for k in range(CHUNKS):
                scan(k)
                if k + 2 < CHUNKS:
                    conv(k + 2)
                gated(k)
                if k:
                    add(k - 1)
            add(CHUNKS - 1)
            links[0] = chain.n

    c.count("const_later_loaded").passed(16 * n_loaded[0])
    c.count("const_later_built").passed(n_built[0])
    chain_s.passed(links[0])
    proj_ready.passed(2 * blocks * CHUNKS)
    proj_taken.passed(2 * blocks * CHUNKS)
    conv_ready.passed(CHUNKS)
    u_ready.passed(blocks * CHUNKS)
    beta_added.passed(1)
    bu_ready.passed(CHUNKS)
    bu_taken.passed(CHUNKS)
    state_ready.passed(CHUNKS)
    y_ready.passed(CHUNKS)
    y_taken.passed(CHUNKS)
    out_ready.passed(CHUNKS)
    added.passed(CHUNKS)


def add_scaled_stage(c, dst, term, row):
    nc = c.nc
    chain_s = c.count("dve_chain")
    links = [0]
    with nc.Block() as block:
        @block.vector
        def _(dve):
            chain = Chain(dve, chain_s)
            chain.link(nc.vector.tensor_tensor(term[:], term[:], along(row), ALU.mult))
            chain.link(nc.vector.tensor_tensor(dst[:], dst[:], term[:], ALU.add))
            links[0] = chain.n
    chain_s.passed(links[0])


def hologram_stage(c):
    nc = c.nc
    written = c.count("holo_keys_written")
    circ_loaded = c.count("holo_circ_loaded")
    decay_ready = c.count("holo_decay_ready")
    scan_ready = c.count("holo_scan_ready")
    unbind_ready = c.count("holo_unbind_ready")
    unbind_taken = c.count("holo_unbind_taken")
    map_ready = c.count("holo_map_ready")
    map_taken = c.count("holo_map_taken")
    out_ready = c.count("holo_out_ready")
    added = c.count("holo_added")
    passed_on = c.count("holo_h_passed_on")
    with nc.Block() as block:

        @block.sync
        def _(sp):
            sp.dma_start(c.keys_dram, c.keys_twice[0:2, :]).then_inc(written.sem, 16)
            sp.wait_ge(*written.after(16))
            for s in range(2):
                src = bass.AP(c.keys_dram.tensor, s * 2 * D, [[1, D], [1, D]])
                sp.dma_start(c.circ[:, s, :], src).then_inc(circ_loaded.sem, 16)

        @block.gpsimd
        def _(pool):
            pool.tensor_tensor(c.x[:], c.x[:], c.h[:], ALU.add).then_inc(passed_on.sem, 1)

        @block.scalar
        def _(act):
            nc.scalar.activation(c.decay[:], c.rows["L1_attn_b_decay"], ACT.Sigmoid).then_inc(decay_ready.sem, 1)

        @block.tensor
        def _(pe):
            pe.wait_ge(*circ_loaded.after(32))
            nc.tensor.matmul(bank(c, 0, P), c.circ[:, 1, :], c.flip[:], start=True, stop=True).then_inc(unbind_ready.sem, 1)
            pe.wait_ge(*unbind_taken.after(1))
            nc.tensor.matmul(bank(c, 1, P), c.circ[:, 0, :], c.circ_a[:], start=True, stop=True).then_inc(unbind_ready.sem, 1)
            pe.wait_ge(*unbind_taken.after(2))
            nc.tensor.matmul(bank(c, 2, P), c.flip[:], c.circ_b[:], start=True, stop=True).then_inc(map_ready.sem, 1)
            pe.wait_ge(*map_taken.after(1))
            pe.wait_ge(*scan_ready.after(1))
            for t in range(TILES):
                ins = nc.tensor.matmul(bank(c, 4 + t // TPC)[:, (t % TPC) * P:(t % TPC + 1) * P],
                                       c.big[:, 0, t * P:(t + 1) * P], c.circ_a[:], start=True, stop=True)
                if t % TPC == TPC - 1:
                    ins.then_inc(out_ready.sem, 1)

        @block.vector
        def _(dve):
            dve.wait_ge(*unbind_ready.after(1))
            nc.vector.tensor_copy(c.circ_a[:], bank(c, 0, P)).then_inc(unbind_taken.sem, 1)
            dve.wait_ge(*unbind_ready.after(2))
            nc.vector.tensor_copy(c.circ_b[:], bank(c, 1, P)).then_inc(unbind_taken.sem, 1)
            dve.wait_ge(*map_ready.after(1))
            nc.vector.tensor_scalar(c.circ_a[:], bank(c, 2, P), c.rows["L1_attn_b_gate"], None, ALU.mult).then_inc(map_taken.sem, 1)
            dve.wait_ge(*decay_ready.after(1))
            nc.vector.tensor_tensor_scan(c.big[:, 0, :], c.decay[:, 0:1].broadcast_to((P, N_TOK)), c.ht[:], 0.0,
                                         ALU.mult, ALU.add).then_inc(scan_ready.sem, 1)
            dve.wait_ge(*passed_on.after(1))
            for k in range(CHUNKS):
                dve.wait_ge(*out_ready.after(k + 1))
                tiles = c.x[:, k * TPC:(k + 1) * TPC, :]
                nc.vector.tensor_tensor(tiles, tiles, bank(c, 4 + k).rearrange("p (t d) -> p t d", d=D), ALU.add).then_inc(added.sem, 1)

    for s, n in ((written, 16), (passed_on, 1), (circ_loaded, 32), (decay_ready, 1), (scan_ready, 1), (unbind_ready, 2),
                 (unbind_taken, 2), (map_ready, 1), (map_taken, 1), (out_ready, CHUNKS), (added, CHUNKS)):
        s.passed(n)


def project_stage(c, w, bq=None, bk=None, bv=None):
    nc = c.nc
    qk_ready = c.count("proj_qk_ready")
    q_taken = c.count("proj_q_taken")
    k_taken = c.count("proj_k_taken")
    v_ready = c.count("proj_v_ready")
    v_taken = c.count("proj_v_taken")
    q_split = c.count("proj_q_split")
    k_split = c.count("proj_k_split")
    stored = c.count("proj_parts_stored")
    zeroed = c.count("proj_rows_zeroed")
    SPLIT_STEPS = 3
    with nc.Block() as block:

        @block.tensor
        def _(pe):
            for n in range(2):
                for k in range(CHUNKS):
                    nc.tensor.matmul(bank(c, n * CHUNKS + k), c.proj[:, w + n, :], c.ht[:, k * CHUNK:(k + 1) * CHUNK],
                                     start=True, stop=True).then_inc(qk_ready.sem, 1)
            for t in range(TILES):
                if t % TPC == 0:
                    pe.wait_ge(*q_taken.after(2 * (t // TPC + 1)))
                ins = nc.tensor.matmul(bank(c, t // TPC)[:, (t % TPC) * P:(t % TPC + 1) * P], c.ht[:, t * P:(t + 1) * P],
                                       c.proj[:, w + 2, :], start=True, stop=True)
                if t % TPC == TPC - 1:
                    ins.then_inc(v_ready.sem, 1)

        @block.scalar
        def _(act):
            for n, (b, taken) in enumerate(((bq, q_taken), (bk, k_taken))):
                for k in range(CHUNKS):
                    cols = slice(k * CHUNK, (k + 1) * CHUNK)
                    act.wait_ge(*qk_ready.after(n * CHUNKS + k + 1))
                    for out in (c.big[:, n, cols], c.parts[:, n, 0, cols]):
                        nc.scalar.activation(out, bank(c, n * CHUNKS + k), ACT.Identity,
                                             bias=b if b is not None else 0.0).then_inc(taken.sem, 1)
            for k in range(CHUNKS):
                act.wait_ge(*v_ready.after(k + 1))
                nc.scalar.activation(c.v[:, k * TPC:(k + 1) * TPC, :].rearrange("p t d -> p (t d)"), bank(c, k),
                                     ACT.Copy).then_inc(v_taken.sem, 1)

        @block.vector
        def _(dve):
            for n, (taken, split_done) in enumerate(((q_taken, q_split), (k_taken, k_split))):
                for k in range(CHUNKS):
                    cols = slice(k * CHUNK, (k + 1) * CHUNK)
                    x, part = c.big[:, n, cols], c.parts[:, n, :, cols]
                    dve.wait_ge(*taken.after(2 * (k + 1)))
                    nc.vector.tensor_tensor(x, x, part[:, 0, :], ALU.subtract).then_inc(split_done.sem, 1)
                    dve.wait_ge(*split_done.after(SPLIT_STEPS * k + 1))
                    nc.vector.tensor_copy(part[:, 1, :], x).then_inc(split_done.sem, 1)
                    dve.wait_ge(*split_done.after(SPLIT_STEPS * k + 2))
                    nc.vector.tensor_tensor(part[:, 2, :], x, part[:, 1, :], ALU.subtract).then_inc(split_done.sem, 1)
            if bv is not None:
                dve.wait_ge(*v_taken.after(CHUNKS))
                nc.vector.tensor_tensor(c.v[:], c.v[:], bv.rearrange("p (o d) -> p o d", o=1).broadcast_to((P, TILES, D)),
                                        ALU.add)

        @block.gpsimd
        def _(pool):
            for n, (rows, value) in enumerate(((c.q_max[64:P], 0.0), (c.q_exp[64:P], 0.0), (c.k_max[64:P], 0.0),
                                               (c.k_exp[64:SHIFT_AT], 0.0), (c.k_exp[SHIFT_AT:P], 1.0),
                                               (c.v_head[:], 0.0), (c.v_head[:, :, :, HD:2 * HD], 1.0))):
                if n:
                    pool.wait_ge(*zeroed.after(n))
                pool.memset(rows, value).then_inc(zeroed.sem, 1)

        @block.sync
        def _(sp):
            for n, ready in enumerate((q_split, k_split)):
                for k in range(CHUNKS):
                    cols = slice(k * CHUNK, (k + 1) * CHUNK)
                    sp.wait_ge(*ready.after(SPLIT_STEPS * (k + 1)))
                    sp.dma_start(c.parts_dram[n, :, :, cols].rearrange("s p n -> p s n"), c.parts[:, n, :, cols])\
                        .then_inc(stored.sem, 16)
            sp.wait_ge(*stored.after(2 * CHUNKS * 16))

    qk_ready.passed(2 * CHUNKS)
    q_taken.passed(2 * CHUNKS)
    k_taken.passed(2 * CHUNKS)
    v_ready.passed(CHUNKS)
    v_taken.passed(CHUNKS)
    q_split.passed(CHUNKS * SPLIT_STEPS)
    k_split.passed(CHUNKS * SPLIT_STEPS)
    stored.passed(2 * CHUNKS * 16)
    zeroed.passed(7)


def heads_stage(c, window=None, biases=()):
    nc = c.nc
    stack_loaded = [c.count(f"head_stack_loaded_{p}") for p in range(2)]
    stack_copied = [c.count(f"head_stack_copied_{p}") for p in range(2)]
    v_staged = c.count("head_v_staged")
    max_ready = c.count("head_max_scores_ready")
    max_taken = c.count("head_max_scores_taken")
    shift_ready = c.count("head_shift_rows_ready")
    shift_taken = c.count("head_shift_rows_taken")
    st_ready = c.count("head_scores_ready")
    exp_done = c.count("head_exp_done")
    pv_done = c.count("head_pv_done")
    out_taken = c.count("head_out_taken")
    out_stored = [c.count(f"head_out_stored_{p}") for p in range(2)]
    last_stored = c.count("head_last_out_stored")
    biased = c.count("head_streams_biased")
    sums_loaded = c.count("out_sums_loaded")
    sums_inverted = c.count("out_sums_inverted")
    inverse_stored = c.count("out_inverse_stored")
    fetched = c.count("out_fetched")
    small = c.count("head_small_steps")
    full = window is None
    before = BEFORE[window] if not full else 0
    scale = float(HD) ** -0.5
    MAX_UNITS = TILES * CHUNKS if full else TILES // 2
    EXP_UNITS = TILES * N_TOK // UNIT if full else TILES * 2 * P // UNIT
    PV_STEPS = TILES if full else 1
    LOADS = 2 * PARTS
    COPIES = 2
    SMALL = 5
    MAX_BANKS = (4, 5, 7)
    SHIFT_BANKS = (7, 4, 5, 7)

    def step_tensor(pe, p, i, with_max, with_exp):
        s = 2 * i + p

        def max_unit(w):
            out = bank(c, MAX_BANKS[w % 3])
            if w >= 3:
                pe.wait_ge(*max_taken.after(s * MAX_UNITS + (w - 2)))
            elif type(s) is not int or s > 0:
                pe.wait_ge(*shift_taken.after((s - 1) * CHUNKS + w + 2))
            if full:
                t, k = w // CHUNKS, w % CHUNKS
                ins = nc.tensor.matmul(out, c.q_max[:, p, t * P:(t + 1) * P], c.k_max[:, p, k * CHUNK:(k + 1) * CHUNK],
                                       start=True, stop=True)
            else:
                for j in range(2):
                    t = 2 * w + j
                    half = out[:, j * 2 * P:(j + 1) * 2 * P]
                    nc.tensor.matmul(half[:, P - before:2 * P], c.ident16[:], c.mask_q[:, window, 1 if t == 0 else 0, P - before:2 * P],
                                     start=True, stop=False)
                    if t == 0:
                        ins = nc.tensor.matmul(half[:, P:2 * P], c.q_max[:, p, 0:P], c.k_max[:, p, 0:P], start=False, stop=True)
                    else:
                        ins = nc.tensor.matmul(half[:, P - before:2 * P], c.q_max[:, p, t * P:(t + 1) * P],
                                               c.k_max[:, p, t * P - before:(t + 1) * P], start=False, stop=True)
            ins.then_inc(max_ready.sem, 1)

        def exp_unit(u):
            q, k_ = c.q_exp[:, 1 - p], c.k_exp[:, 1 - p]
            done = (s - 1) * EXP_UNITS + (u - 1)
            if u >= 2 or type(s) is not int or s > 1:
                pe.wait_ge(*exp_done.after(done))
            chunks = (2, 4)[u] if full and u < 2 else min(u + 2, CHUNKS) if not full else 0
            if chunks:
                pe.wait_ge(*shift_taken.after((s - 1) * CHUNKS + chunks))
            at = 2 * (u % 2)
            if full:
                kb, half = u // 2, u % 2
                for j in range(2):
                    col = half * UNIT + j * CHUNK
                    ins = nc.tensor.matmul(bank(c, at + j), k_[:, kb * P:(kb + 1) * P], q[:, col:col + CHUNK],
                                           start=True, stop=True)
            else:
                for j in range(4):
                    kb = 4 * u + j
                    width = P + before if kb < TILES - 1 else P
                    out = c.ps[:, at * CHUNK + j * 2 * P:at * CHUNK + j * 2 * P + width]
                    nc.tensor.matmul(out, c.ident16[:], c.mask_k[:, window, 0:width], start=True, stop=False)
                    ins = nc.tensor.matmul(out, k_[:, kb * P:(kb + 1) * P], q[:, kb * P:kb * P + width], start=False, stop=True)
            ins.then_inc(st_ready.sem, 1)

        def pv_step(kb):
            v = c.v_head[:, 1 - p]
            for g in range(4):
                out = c.ps[OUT_ROWS * g:OUT_ROWS * (g + 1), 6 * CHUNK:7 * CHUNK]
                unit = c.prob[:, (2 * kb + g // 2) % P_UNITS, (g % 2) * CHUNK:(g % 2 + 1) * CHUNK]
                ins = nc.tensor.matmul(out, v[:, kb, :], unit, start=(kb == 0), stop=(kb == TILES - 1), skip_group_check=True)
            ins.then_inc(pv_done.sem, 1)

        def pv_window():
            v = c.v_head[:, 1 - p]
            half = EXP_UNITS * (1 - p)
            for j in range(TPC):
                if with_max and j >= 2:
                    shift_rows(pe, s, j - 2)
                for own in range(2):
                    for g in range(4):
                        t = TPC * g + j
                        kb = t if own else t - 1
                        if kb < 0:
                            continue
                        col = (kb % 4) * 2 * P + (0 if own else P)
                        width = P if own else before
                        first = j == 0 and (own == 0 or t == 0)
                        ins = nc.tensor.matmul(c.ps[OUT_ROWS * g:OUT_ROWS * (g + 1), 6 * CHUNK + j * P:6 * CHUNK + j * P + width],
                                               v[:, kb, :], c.prob[:, half + kb // 4, col:col + width],
                                               start=first, stop=(own == 1), skip_group_check=True)
            ins.then_inc(pv_done.sem, 1)
            for k in range(2, CHUNKS) if with_max else ():
                shift_rows(pe, s, k)

        w = 0
        if with_max:
            pe.wait_ge(*stack_loaded[p].after((i + 1) * LOADS * 16))
        if with_exp:
            pe.wait_ge(*stack_copied[1 - p].after((i + p) * COPIES * 16))
        if with_exp and full:
            for kb in range(TILES + 1):
                todo = ["max"] + ["exp", "max"] * 2 if kb < TILES else []
                todo += (["pv", "max"] if kb else []) + (["max"] if kb % 2 else [])
                half = 0
                for what in todo:
                    if what == "exp":
                        exp_unit(2 * kb + half)
                        half += 1
                    elif what == "pv":
                        pv_wait(pe, s, kb - 1)
                        pv_step(kb - 1)
                        if with_max and kb >= TILES - 1:
                            shift_rows(pe, s, 2 * (kb - TILES + 1))
                            shift_rows(pe, s, 2 * (kb - TILES + 1) + 1)
                    elif with_max and w < MAX_UNITS:
                        max_unit(w)
                        w += 1
            assert w == (MAX_UNITS if with_max else 0)
        elif with_exp:
            for u, maxima in enumerate(((0, 1, 2), (3, 4), (5, 6), (7,))):
                exp_unit(u)
                for w in maxima if with_max else ():
                    max_unit(w)
            pv_wait(pe, s, 0)
            pv_window()
        else:
            for w in range(MAX_UNITS):
                max_unit(w)
            for k in range(CHUNKS):
                shift_rows(pe, s, k)

    def shift_rows(pe, s, k):
        if k == 0:
            pe.wait_ge(*small.after((s + 1) * SMALL))
        if k == CHUNKS - 1:
            pe.wait_ge(*shift_taken.after(s * CHUNKS + 1))
        for j in range(TPC):
            ins = nc.tensor.matmul(bank(c, SHIFT_BANKS[k])[SHIFT_AT:SHIFT_AT + PARTS, j * P:(j + 1) * P],
                                   c.shift[:, :, k * TPC + j], c.ident16[:], start=True, stop=True)
        ins.then_inc(shift_ready.sem, 1)

    def take_shift(act, p, s, k):
        act.wait_ge(*shift_ready.after(s * CHUNKS + k + 1))
        nc.scalar.activation(c.q_exp[SHIFT_AT:SHIFT_AT + PARTS, p, k * CHUNK:(k + 1) * CHUNK],
                             bank(c, SHIFT_BANKS[k])[SHIFT_AT:SHIFT_AT + PARTS], ACT.Copy).then_inc(shift_taken.sem, 1)

    def pv_wait(pe, s, kb):
        if kb == 0:
            pe.wait_ge(*v_staged.after(s))
            if type(s) is not int or s > 1:
                pe.wait_ge(*out_taken.after(s - 1))
        units = 2 * (kb + 1) if full else EXP_UNITS
        pe.wait_ge(*exp_done.after((s - 1) * EXP_UNITS + units))

    def step_scalar(act, p, i, with_max, with_exp):
        s = 2 * i + p
        if not with_exp:
            for k in range(CHUNKS):
                take_shift(act, p, s, k)
            return
        for u in range(EXP_UNITS):
            act.wait_ge(*st_ready.after((s - 1) * EXP_UNITS + u + 1))
            if full:
                buf = u % P_UNITS
                if u >= P_UNITS or type(s) is not int or s > 1:
                    act.wait_ge(*pv_done.after((s - 1) * PV_STEPS + (u - P_UNITS) // 2 + 1))
            else:
                buf = EXP_UNITS * (1 - p) + u
                if type(s) is not int or s > 2:
                    act.wait_ge(*pv_done.after(s - 2))
            scores, probs = c.ps[:, 2 * (u % 2) * CHUNK:2 * (u % 2) * CHUNK + UNIT], c.prob[:, buf, :]
            if not full:
                scores, probs = (x.rearrange("p (a n) -> p a n", n=2 * P)[:, :, 0:P + before] for x in (scores, probs))
                if u == EXP_UNITS - 1:
                    nc.scalar.activation(probs[:, 0:3], scores[:, 0:3], ACT.Exp, scale=scale)
                    scores, probs = scores[:, 3, 0:P], probs[:, 3, 0:P]
            nc.scalar.activation(probs, scores, ACT.Exp, scale=scale).then_inc(exp_done.sem, 1)
        for k in range(CHUNKS) if with_max else ():
            take_shift(act, p, s, k)

    def step_vector(dve, p, i, with_max, with_exp):
        s = 2 * i + p
        if with_max:
            for w in range(MAX_UNITS):
                dve.wait_ge(*max_ready.after(s * MAX_UNITS + w + 1))
                if full:
                    nc.vector.reduce_max(c.mx[:, w // CHUNKS, w % CHUNKS:w % CHUNKS + 1], bank(c, MAX_BANKS[w % 3]), AX.X)\
                        .then_inc(max_taken.sem, 1)
                else:
                    nc.vector.reduce_max(c.mx[:, 2 * w:2 * w + 2, 0], bank(c, MAX_BANKS[w % 3]).rearrange("p (a n) -> p a n", a=2)[:, :, P - before:2 * P], AX.X)\
                        .then_inc(max_taken.sem, 1)
            dve.wait_ge(*max_taken.after((s + 1) * MAX_UNITS))
            cols = CHUNKS if full else 1
            base = s * SMALL
            nc.vector.tensor_reduce(c.rowmax[:], c.mx[:, :, 0:cols], AX.X, ALU.max, negate=True).then_inc(small.sem, 1)
            dve.wait_ge(*small.after(base + 1))
            if type(s) is not int or s > 0:
                dve.wait_ge(*shift_ready.after(s * CHUNKS))
            nc.vector.tensor_copy(c.shift[:, 0, :], c.rowmax[:]).then_inc(small.sem, 1)
            dve.wait_ge(*small.after(base + 2))
            nc.vector.tensor_tensor(c.rowmax[:], c.rowmax[:], c.shift[:, 0, :], ALU.subtract).then_inc(small.sem, 1)
            dve.wait_ge(*small.after(base + 3))
            nc.vector.tensor_copy(c.shift[:, 1, :], c.rowmax[:]).then_inc(small.sem, 1)
            dve.wait_ge(*small.after(base + 4))
            nc.vector.tensor_tensor(c.shift[:, 2, :], c.rowmax[:], c.shift[:, 1, :], ALU.subtract).then_inc(small.sem, 1)
        if with_exp:
            dve.wait_ge(*pv_done.after(s * PV_STEPS))
            if type(s) is not int or s > 2:
                dve.wait_ge(*out_stored[1 - p].after((i - 1 + p) * 16))
            nc.vector.tensor_copy(c.out_head[:, 1 - p, :], bank(c, 6)).then_inc(out_taken.sem, 1)

    def step_pool(pool, p, i):
        s = 2 * i + p
        if type(s) is not int or s > 1:
            pool.wait_ge(*pv_done.after((s - 1) * PV_STEPS))
        cols = slice(s * HD, (s + 1) * HD) if type(s) is int else bass.ds(s * HD, HD)
        pool.tensor_copy(c.v_head[:, p, :, 0:HD], c.v[:, :, cols]).then_inc(v_staged.sem, 1)

    def load_stacks(sp, p, i):
        s = 2 * i + p
        if type(s) is not int or s > 1:
            sp.wait_ge(*st_ready.after((s - 2) * EXP_UNITS + 1))
        rows = slice(s * HD, (s + 1) * HD) if type(s) is int else bass.ds(s * HD, HD)
        q, k = (c.parts_dram[n, :, rows, :] for n in range(2))
        for a in range(PARTS):
            group = slice(a * PARTS * HD, (a + 1) * PARTS * HD)
            same = q[a:a + 1].broadcast_to((PARTS, HD, N_TOK))
            sp.dma_start(c.q_max[group, p, :], same).then_inc(stack_loaded[p].sem, 16)
            sp.dma_start(c.k_max[group, p, :], k).then_inc(stack_loaded[p].sem, 16)

    def copy_stacks(sp, p, i):
        s = 2 * i + p
        if type(s) is not int or s > 1:
            sp.wait_ge(*pv_done.after((s - 1) * PV_STEPS))
        sp.wait_ge(*stack_loaded[p].after((i + 1) * LOADS * 16))
        sp.dma_start(c.q_exp[0:STACK, p, :], c.q_max[0:STACK, p, :]).then_inc(stack_copied[p].sem, 16)
        sp.dma_start(c.k_exp[0:STACK, p, :], c.k_max[0:STACK, p, :]).then_inc(stack_copied[p].sem, 16)

    def store_out(pool, p, i):
        s = 2 * i + p
        pool.wait_ge(*out_taken.after(s))
        dst = c.out_dram[s - 1] if type(s) is int else c.out_dram[bass.ds(s - 1, 1)].rearrange("o p n -> (o p) n")
        pool.dma_start(dst, c.out_head[:, 1 - p, :]).then_inc(out_stored[1 - p].sem, 16)

    with nc.Block() as block:

        @block.tensor
        def _(pe):
            step_tensor(pe, 0, 0, True, False)
            step_tensor(pe, 1, 0, True, True)
            with pe.Fori(1, HEADS // 2) as i:
                step_tensor(pe, 0, i, True, True)
                step_tensor(pe, 1, i, True, True)
            step_tensor(pe, 0, HEADS // 2, False, True)

        @block.scalar
        def _(act):
            step_scalar(act, 0, 0, True, False)
            step_scalar(act, 1, 0, True, True)
            with act.Fori(1, HEADS // 2) as i:
                step_scalar(act, 0, i, True, True)
                step_scalar(act, 1, i, True, True)
            step_scalar(act, 0, HEADS // 2, False, True)

        @block.vector
        def _(dve):
            step_vector(dve, 0, 0, True, False)
            step_vector(dve, 1, 0, True, True)
            with dve.Fori(1, HEADS // 2) as i:
                step_vector(dve, 0, i, True, True)
                step_vector(dve, 1, i, True, True)
            dve.wait_ge(*sums_loaded.after(16))
            nc.vector.reciprocal(c.sums[0:EARLY * CHUNKS, :], c.sums[0:EARLY * CHUNKS, :]).then_inc(sums_inverted.sem, 1)
            step_vector(dve, 0, HEADS // 2, False, True)

        @block.gpsimd
        def _(pool):
            step_pool(pool, 0, 0)
            step_pool(pool, 1, 0)
            for stream, row in biases:
                pool.tensor_tensor(stream[:], stream[:], along(row), ALU.add).then_inc(biased.sem, 1)
            store_out(pool, 1, 0)
            with pool.Fori(1, HEADS // 2) as i:
                step_pool(pool, 0, i)
                store_out(pool, 0, i)
                step_pool(pool, 1, i)
                store_out(pool, 1, i)
            pool.wait_ge(*out_stored[0].after(HEADS // 2 * 16))

        @block.sync
        def _(sp):
            load_stacks(sp, 0, 0)
            load_stacks(sp, 1, 0)
            copy_stacks(sp, 0, 0)
            with sp.Fori(1, HEADS // 2) as i:
                load_stacks(sp, 0, i)
                copy_stacks(sp, 1, i - 1)
                load_stacks(sp, 1, i)
                copy_stacks(sp, 0, i)
            copy_stacks(sp, 1, HEADS // 2 - 1)
            for p in range(2):
                sp.wait_ge(*out_stored[p].after((HEADS // 2 - 1) * 16))
            sp.dma_start(c.sums[0:EARLY * CHUNKS, :], c.out_dram[0:EARLY].rearrange("h (k r) q -> h k r q", k=CHUNKS)[:, :, HD, :])\
                .then_inc(sums_loaded.sem, 16)
            for k in range(CHUNKS):
                sp.dma_start(c.big[0:EARLY * HD, 0, k * CHUNK:(k + 1) * CHUNK],
                             c.out_dram[0:EARLY, OUT_ROWS * k:OUT_ROWS * k + HD, :]).then_inc(fetched.sem, 16)
            sp.wait_ge(*sums_inverted.after(1))
            sp.dma_start(c.inverse_dram[0:EARLY].rearrange("h (k q) -> (h k) q", k=CHUNKS), c.sums[0:EARLY * CHUNKS, :])\
                .then_inc(inverse_stored.sem, 16)
            sp.wait_ge(*inverse_stored.after(16))
            fetch_inverse(c, sp, 0, EARLY).then_inc(fetched.sem, 16)
            sp.wait_ge(*out_taken.after(HEADS))
            sp.dma_start(c.out_dram[HEADS - 1], c.out_head[:, 1, :]).then_inc(last_stored.sem, 16)
            sp.wait_ge(*last_stored.after(16))

    fetched.passed((CHUNKS + 1) * 16)
    sums_loaded.passed(16)
    sums_inverted.passed(1)
    inverse_stored.passed(16)
    last_stored.passed(16)
    biased.passed(len(biases))
    for p in range(2):
        stack_loaded[p].passed(HEADS // 2 * LOADS * 16)
        stack_copied[p].passed(HEADS // 2 * COPIES * 16)
        out_stored[p].passed((HEADS // 2 - p) * 16)
    for sig, n in ((v_staged, HEADS), (max_ready, HEADS * MAX_UNITS),
                   (max_taken, HEADS * MAX_UNITS), (shift_ready, HEADS * CHUNKS),
                   (shift_taken, HEADS * CHUNKS), (small, HEADS * SMALL),
                   (st_ready, HEADS * EXP_UNITS),
                   (exp_done, HEADS * EXP_UNITS), (pv_done, HEADS * PV_STEPS), (out_taken, HEADS)):
        sig.passed(n)


def fetch_inverse(c, engine, first, end):
    src = bass.AP(c.inverse_dram.tensor, first * N_TOK, [[N_TOK, end - first], [0, HD], [1, N_TOK]])
    return engine.dma_start(c.big[first * HD:end * HD, 1, :], src)


def output_stage(c, w, dst):
    nc = c.nc
    fetched = c.count("out_fetched")
    sums_loaded = c.count("out_sums_loaded")
    sums_inverted = c.count("out_sums_inverted")
    inverse_stored = c.count("out_inverse_stored")
    ctx_ready = c.count("out_ctx_ready")
    out_ready = c.count("out_ready")
    added = c.count("out_added")
    LATE = HEADS - EARLY
    PIECE = CHUNK // HD
    ROWS = LATE * CHUNKS * HD
    with nc.Block() as block:

        @block.sync
        def _(sp):
            for h in range(LATE):
                src = bass.AP(c.out_dram.tensor, ((EARLY + h) * P + HD) * CHUNK,
                              [[OUT_ROWS * CHUNK, CHUNKS], [CHUNK + PIECE, HD], [1, PIECE]])
                sp.dma_start(c.late_sums[h * CHUNKS * HD:(h + 1) * CHUNKS * HD, :], src).then_inc(sums_loaded.sem, 16)
            sp.wait_ge(*sums_inverted.after(1))
            sp.dma_start(c.inverse_dram[EARLY:HEADS].rearrange("h (r q) -> (h r) q", q=PIECE), c.late_sums[0:ROWS, :])\
                .then_inc(inverse_stored.sem, 16)
            sp.wait_ge(*inverse_stored.after(16))
            fetch_inverse(c, sp, EARLY, HEADS).then_inc(fetched.sem, 16)

        @block.scalar
        def _(act):
            for h in range(EARLY, HEADS):
                rows = c.out_dram[h].rearrange("(k r) q -> r k q", k=CHUNKS)[0:HD]
                act.dma_start(c.big[h * HD:(h + 1) * HD, 0, :].rearrange("r (k q) -> r k q", k=CHUNKS), rows)\
                    .then_inc(fetched.sem, 16)

        @block.vector
        def _(dve):
            dve.wait_ge(*sums_loaded.after(LATE * 16))
            nc.vector.reciprocal(c.late_sums[0:ROWS, :], c.late_sums[0:ROWS, :]).then_inc(sums_inverted.sem, 1)
            dve.wait_ge(*fetched.after((LATE + 1) * 16))
            for k in range(CHUNKS):
                num, inverse = (c.big[:, n, k * CHUNK:(k + 1) * CHUNK] for n in range(2))
                nc.vector.tensor_tensor(num, num, inverse, ALU.mult).then_inc(ctx_ready.sem, 1)
            for k in range(CHUNKS):
                dve.wait_ge(*out_ready.after(k + 1))
                tiles = dst[:, k * TPC:(k + 1) * TPC, :]
                nc.vector.tensor_tensor(tiles, tiles, bank(c, k).rearrange("p (t d) -> p t d", d=D), ALU.add).then_inc(added.sem, 1)

        @block.tensor
        def _(pe):
            for t in range(TILES):
                if t % TPC == 0:
                    pe.wait_ge(*ctx_ready.after(t // TPC + 1))
                ins = nc.tensor.matmul(bank(c, t // TPC)[:, (t % TPC) * P:(t % TPC + 1) * P], c.big[:, 0, t * P:(t + 1) * P],
                                       c.proj[:, w + 3, :], start=True, stop=True)
                if t % TPC == TPC - 1:
                    ins.then_inc(out_ready.sem, 1)

    fetched.passed((LATE + 1) * 16)
    sums_loaded.passed(LATE * 16)
    sums_inverted.passed(1)
    inverse_stored.passed(16)
    ctx_ready.passed(CHUNKS)
    out_ready.passed(CHUNKS)
    added.passed(CHUNKS)


def feed_forward_stage(c, dst):
    nc = c.nc
    up_ready = c.count("ff_up_ready")
    act_ready = c.count("ff_act_ready")
    out_ready = c.count("ff_out_ready")
    added = c.count("ff_added")
    blocks = D_FF // P
    with nc.Block() as block:

        @block.tensor
        def _(pe):
            def down(k):
                pe.wait_ge(*act_ready.after(blocks * (k + 1)))
                if k >= 2:
                    pe.wait_ge(*added.after(k - 1))
                for t in range(TPC):
                    for b in range(blocks):
                        ins = nc.tensor.matmul(bank(c, 4 + k % 2)[:, t * P:(t + 1) * P], c.hid[:, k % 2, b, t * P:(t + 1) * P],
                                               c.w2[:, b, :], start=(b == 0), stop=(b == blocks - 1))
                ins.then_inc(out_ready.sem, 1)

            for k in range(CHUNKS):
                for b in range(blocks):
                    n = k * blocks + b
                    if n >= 4:
                        pe.wait_ge(*act_ready.after(n - 3))
                    nc.tensor.matmul(bank(c, n % 4), c.w1[:, b * P:(b + 1) * P], c.ht[:, k * CHUNK:(k + 1) * CHUNK],
                                     start=True, stop=True).then_inc(up_ready.sem, 1)
                if k:
                    down(k - 1)
            down(CHUNKS - 1)

        @block.scalar
        def _(act):
            for n in range(CHUNKS * blocks):
                k, b = n // blocks, n % blocks
                act.wait_ge(*up_ready.after(n + 1))
                if k >= 2:
                    act.wait_ge(*out_ready.after(k - 1))
                nc.scalar.activation(c.hid[:, k % 2, b, :], bank(c, n % 4), ACT.Gelu_apprx_tanh,
                                     bias=c.columns["L0_attn_b_b1"][:, b:b + 1]).then_inc(act_ready.sem, 1)

        @block.vector
        def _(dve):
            for k in range(CHUNKS):
                dve.wait_ge(*out_ready.after(k + 1))
                tiles = dst[:, k * TPC:(k + 1) * TPC, :]
                nc.vector.tensor_tensor(tiles, tiles, bank(c, 4 + k % 2).rearrange("p (t d) -> p t d", d=D), ALU.add)\
                    .then_inc(added.sem, 1)

    up_ready.passed(CHUNKS * blocks)
    act_ready.passed(CHUNKS * blocks)
    out_ready.passed(CHUNKS)
    added.passed(CHUNKS)


def load_expert(c, sp, p, weights):
    loaded = c.count(f"moe_weights_loaded_{p}")
    g, u, d = weights
    inner = g.shape[1]
    whole = inner // P
    sp.dma_start(c.wg[:, p, 0:inner], g).then_inc(loaded.sem, 16)
    sp.dma_start(c.wu[:, p, 0:inner], u).then_inc(loaded.sem, 16)
    sp.dma_start(c.wd[:, p, 0:whole, :], d[0:whole * P, :].rearrange("(j p) d -> p j d", p=P)).then_inc(loaded.sem, 16)
    if inner % P:
        sp.dma_start(c.wd[0:inner % P, p, whole, :], d[whole * P:inner, :]).then_inc(loaded.sem, 16)


def loads_of_expert(inner):
    return 3 + (1 if inner % P else 0)


def weight_pieces(c, p, inner):
    return ((c.wg[:, p, 0:inner], c.wg_part[:, p, :, 0:inner]), (c.wu[:, p, 0:inner], c.wu_part[:, p, :, 0:inner]))


def make_high_weights(c, p, inner):
    for w, part in weight_pieces(c, p, inner):
        c.nc.scalar.activation(part[:, 0], w, ACT.Copy).then_inc(c.count("moe_weights_high_ready").sem, 1)


def make_low_weights(c, pool, p, inner, n):
    for k, (w, part) in enumerate(weight_pieces(c, p, inner)):
        pool.wait_ge(*c.count("moe_weights_high_ready").after(2 * n + k + 1))
        pool.tensor_tensor(part[:, 1], w, part[:, 0], ALU.subtract).then_inc(c.count("moe_weights_split").sem, 1)


def experts_stage(c, router, soft_of_probs, gate_w, up_w, down_w, inner, shared=None):
    nc = c.nc
    weights_loaded = [c.count(f"moe_weights_loaded_{p}") for p in range(2)]
    weights_high = c.count("moe_weights_high_ready")
    weights_split = c.count("moe_weights_split")
    shifted_ready = c.count("moe_shifted_ready")
    router_exp = c.count("moe_router_exp_ready")
    chain_s = c.count("dve_chain")
    cw_ready = c.count("moe_cw_ready")
    cw_staged = c.count("moe_cw_staged")
    gate_ready = c.count("moe_gate_ready")
    up_ready = c.count("moe_up_ready")
    silu_ready = c.count("moe_silu_ready")
    hid_ready = c.count("moe_hidden_ready")
    out_ready = c.count("moe_out_ready")
    out_added = c.count("moe_out_added")
    J = (inner + P - 1) // P
    sizes = [min(P, inner - j * P) for j in range(J)]
    LOADS = loads_of_expert(inner)
    SPLITS = 2
    PAIRS = 4
    UNITS = CHUNKS * J
    E = router.shape[1]
    links = [0]

    def load(sp, p, i, src=None):
        n = 2 * i + p
        sp.wait_ge(*out_ready.after((n - 1) * CHUNKS))
        if src is None:
            src = [w[bass.ds(n, 1)].rearrange("o a b -> (o a) b") if type(n) is not int else w[n] for w in (gate_w, up_w, down_w)]
        load_expert(c, sp, p, src)

    def high_weights(act, p, i):
        n = 2 * i + p
        act.wait_ge(*weights_loaded[p].after((i + 1) * LOADS * 16))
        if type(n) is not int or n > 1:
            act.wait_ge(*up_ready.after((n - 1) * UNITS))
        make_high_weights(c, p, inner)

    def low_weights(pool, p, i):
        make_low_weights(c, pool, p, inner, 2 * i + p)

    PASSES = ((0, 0), (0, 1), (1, 0))

    def expert_tensor(pe, p, i):
        n = 2 * i + p
        pe.wait_ge(*weights_split.after((n + 1) * SPLITS))

        def up(k, j):
            unit = k * J + j
            m = sizes[j]
            for w, at, read, ready in ((c.wg_part, 0, silu_ready, gate_ready), (c.wu_part, 2, hid_ready, up_ready)):
                if unit >= 2 or type(n) is not int or n > 0:
                    pe.wait_ge(*read.after(n * UNITS + unit - 1))
                for a, (u, v) in enumerate(PASSES):
                    ins = nc.tensor.matmul(bank(c, at + unit % 2)[0:m], w[:, p, u, j * P:j * P + m],
                                           c.ht_part[:, v, k * CHUNK:(k + 1) * CHUNK], start=(a == 0), stop=(a == 2))
                ins.then_inc(ready.sem, 1)

        def down(k, tiles):
            if 0 in tiles:
                pe.wait_ge(*hid_ready.after(n * UNITS + (k + 1) * J))
                if k >= 2 or type(n) is not int or n > 0:
                    pe.wait_ge(*out_added.after(n * CHUNKS + k - 1))
            for t in tiles:
                for j in range(J):
                    m = sizes[j]
                    ins = nc.tensor.matmul(bank(c, 4 + k % 2)[:, t * P:(t + 1) * P], c.hid[0:m, k % 2, j, t * P:(t + 1) * P],
                                           c.wd[0:m, p, j, :], start=(j == 0), stop=(j == J - 1))
            if TPC - 1 in tiles:
                ins.then_inc(out_ready.sem, 1)

        for k in range(CHUNKS):
            for j in range(J):
                up(k, j)
                if k:
                    down(k - 1, range(j * TPC // J, (j + 1) * TPC // J))
        down(CHUNKS - 1, range(TPC))

    def expert_scalar(act, p, i):
        n = 2 * i + p
        for unit in range(UNITS):
            m = sizes[unit % J]
            act.wait_ge(*gate_ready.after(n * UNITS + unit + 1))
            if unit >= 2 or type(n) is not int or n > 0:
                act.wait_ge(*hid_ready.after(n * UNITS + unit - 1))
            nc.scalar.activation(c.silu[0:m, unit % 2, :], bank(c, unit % 2)[0:m], ACT.Silu).then_inc(silu_ready.sem, 1)
            if type(n) is int and n == 0 and unit == J - 1:
                router_scalar(act)
            if unit == UNITS // 2 and (type(n) is not int or n < 2 * PAIRS):
                high_weights(act, 1 - p, i + p)

    def add(dve, p, n, k, weighted):
        dve.wait_ge(*out_ready.after(n * CHUNKS + k + 1))
        if k == 0 and weighted:
            dve.wait_ge(*cw_staged.after(n + 1))
        for t in range(TPC):
            tile = c.x[:, k * TPC + t, :]
            out = bank(c, 4 + k % 2)[:, t * P:(t + 1) * P]
            if weighted:
                ins = nc.vector.scalar_tensor_tensor(tile, out, c.cw_now[:, p, k * TPC + t:k * TPC + t + 1], tile,
                                                     ALU.mult, ALU.add)
            else:
                ins = nc.vector.tensor_tensor(tile, tile, out, ALU.add)
        ins.then_inc(out_added.sem, 1)

    def expert_vector(dve, p, i, weighted=True):
        n = 2 * i + p
        for k in range(CHUNKS):
            for j in range(J):
                unit = k * J + j
                m = sizes[j]
                dve.wait_ge(*silu_ready.after(n * UNITS + unit + 1))
                dve.wait_ge(*up_ready.after(n * UNITS + unit + 1))
                if j == 0 and (k >= 2 or type(n) is not int or n > 0):
                    dve.wait_ge(*out_ready.after(n * CHUNKS + k - 1))
                nc.vector.tensor_tensor(c.hid[0:m, k % 2, j, :], c.silu[0:m, unit % 2, :], bank(c, 2 + unit % 2)[0:m],
                                        ALU.mult).then_inc(hid_ready.sem, 1)
            if type(n) is int and n == 0 and k == 0:
                router_vector(dve)
            if k:
                add(dve, p, n, k - 1, weighted)
            elif type(n) is not int or n > 0:
                add(dve, 1 - p, n - 1, CHUNKS - 1, True)
    def expert_pool(pool, p, i):
        n = 2 * i + p
        if type(n) is not int or n > 1:
            pool.wait_ge(*out_added.after((n - 1) * CHUNKS))
        if type(n) is int and n == 0:
            pool.wait_ge(*cw_ready.after(1))
        src = c.cw[:, n, :] if type(n) is int else c.cw[:, bass.ds(n, 1), :].rearrange("p o t -> p (o t)")
        pool.tensor_copy(c.cw_now[:, p, :], src).then_inc(cw_staged.sem, 1)

    def router_scalar(act):
        act.wait_ge(*shifted_ready.after(1))
        nc.scalar.activation(c.probs[:, :, 0:E], c.logits[:, :, 0:E], ACT.Exp).then_inc(router_exp.sem, 1)
        act.wait_ge(*shifted_ready.after(2))
        nc.scalar.activation(c.top_gap[:], c.top_gap[:], ACT.Exp).then_inc(router_exp.sem, 1)

    def router_vector(dve):
        chain = Chain(dve, chain_s)
        v = nc.vector
        logits = c.logits[:, :, 0:E]

        def wide(a):
            return a.broadcast_to((P, TILES, E))

        v.tensor_tensor(logits, logits, wide(c.top[:, :, 0:1]), ALU.subtract).then_inc(shifted_ready.sem, 1)
        chain.link(v.tensor_copy(c.top_f[:], c.top_i[:, :, 0:2]))
        if soft_of_probs:
            chain.link(v.tensor_tensor(c.pick[:, :, 0:E], c.ids_wide(E), wide(c.top_f[:, :, 1:2]), ALU.is_equal))
            dve.wait_ge(*router_exp.after(1))
            chain.link(v.reduce_sum(c.total[:], c.probs[:, :, 0:E], AX.X))
            chain.link(v.reciprocal(c.total[:], c.total[:]))
            chain.link(v.tensor_tensor(c.pick[:, :, 0:E], c.pick[:, :, 0:E], c.probs[:, :, 0:E], ALU.mult))
            chain.link(v.reduce_sum(c.second[:], c.pick[:, :, 0:E], AX.X))
            chain.link(v.tensor_scalar(c.second[:], c.second[:], 1.0, None, ALU.subtract))
            v.tensor_tensor(c.top_gap[:], c.second[:], c.total[:], ALU.mult).then_inc(shifted_ready.sem, 1)
        else:
            v.tensor_tensor(c.top_gap[:], c.top[:, :, 1], c.top[:, :, 0], ALU.subtract).then_inc(shifted_ready.sem, 1)
        dve.wait_ge(*router_exp.after(2))
        chain.link(v.tensor_scalar(c.total[:], c.top_gap[:], 1.0, None, ALU.add))
        chain.link(v.reciprocal(c.total[:], c.total[:]))
        chain.link(v.tensor_tensor(c.second[:], c.top_gap[:], c.total[:], ALU.mult))
        out = c.cw[:, 0:E, :].rearrange("p e t -> p t e")
        for n, weight in enumerate((c.total, c.second)):
            chain.link(v.tensor_tensor(c.pick[:, :, 0:E], c.ids_wide(E), wide(c.top_f[:, :, n:n + 1]), ALU.is_equal))
            w3 = wide(weight[:].rearrange("p (t o) -> p t o", o=1))
            chain.link(v.tensor_tensor(c.probs[:, :, 0:E] if n else out, c.pick[:, :, 0:E], w3, ALU.mult))
        v.tensor_tensor(out, out, c.probs[:, :, 0:E], ALU.add).then_inc(cw_ready.sem, 1)
        links[0] = chain.n

    with nc.Block() as block:

        @block.sync
        def _(sp):
            with sp.Fori(1, PAIRS) as i:
                load(sp, 0, i)
                load(sp, 1, i)
            load(sp, 0, PAIRS, shared)

        @block.tensor
        def _(pe):
            expert_tensor(pe, 0, 0)
            expert_tensor(pe, 1, 0)
            with pe.Fori(1, PAIRS) as i:
                expert_tensor(pe, 0, i)
                expert_tensor(pe, 1, i)
            expert_tensor(pe, 0, PAIRS)

        @block.scalar
        def _(act):
            expert_scalar(act, 0, 0)
            expert_scalar(act, 1, 0)
            with act.Fori(1, PAIRS) as i:
                expert_scalar(act, 0, i)
                expert_scalar(act, 1, i)
            expert_scalar(act, 0, PAIRS)

        @block.vector
        def _(dve):
            expert_vector(dve, 0, 0)
            expert_vector(dve, 1, 0)
            with dve.Fori(1, PAIRS) as i:
                expert_vector(dve, 0, i)
                expert_vector(dve, 1, i)
            expert_vector(dve, 0, PAIRS, weighted=shared is None)
            add(dve, 0, 2 * PAIRS, CHUNKS - 1, shared is None)

        @block.gpsimd
        def _(pool):
            low_weights(pool, 1, 0)
            expert_pool(pool, 0, 0)
            expert_pool(pool, 1, 0)
            with pool.Fori(1, PAIRS) as i:
                low_weights(pool, 0, i)
                expert_pool(pool, 0, i)
                low_weights(pool, 1, i)
                expert_pool(pool, 1, i)
            low_weights(pool, 0, PAIRS)
            if shared is None:
                expert_pool(pool, 0, PAIRS)

    N = 2 * PAIRS + 1
    for p in range(2):
        weights_loaded[p].passed((PAIRS + 1 - p) * LOADS * 16)
    for s, n in ((weights_high, N * 2), (weights_split, N * SPLITS), 
                 (shifted_ready, 2), (router_exp, 2), (chain_s, links[0]), (cw_ready, 1),
                 (cw_staged, N if shared is None else N - 1), (gate_ready, N * UNITS), (up_ready, N * UNITS), (silu_ready, N * UNITS),
                 (hid_ready, N * UNITS), (out_ready, N * CHUNKS),
                 (out_added, N * CHUNKS)):
        s.passed(n)


def store_stage(c, out):
    nc = c.nc
    stored = c.count("result_stored")
    with nc.Block() as block:
        @block.sync
        def _(sp):
            sp.dma_start(out.rearrange("b (t p) d -> p (b t) d", p=P), c.x[:]).then_inc(stored.sem, 16)
            sp.wait_ge(*stored.after(16))
    stored.passed(16)


PROJ = [f"L0_attn_b_W{x}" for x in "qkvo"] + [f"L1_attn_a_W{x}_T" for x in "qkvo"] + [f"L1_ffn_w{x}" for x in "qkvo"]


def hybrid_stack(nc, i, out, layers="abcdefgh"):
    with ExitStack() as ctx:
        c = Core(nc, ctx)
        c.i = i
        c.x = c.sbuf("x", [P, TILES, D])
        c.h = c.sbuf("h", [P, TILES, D])
        c.n = c.sbuf("n", [P, TILES, D])
        c.ht = c.sbuf("ht", [P, N_TOK])
        c.decay = c.sbuf("decay", [P, 1])
        c.mx = c.sbuf("mx", [P, TILES, CHUNKS])
        c.rowmax = c.sbuf("rowmax", [P, TILES])
        c.shift = c.sbuf("shift", [P, PARTS, TILES], bf16)
        c.ident = c.sbuf("ident", [P, P])
        c.ident16 = c.sbuf("ident16", [P, P], bf16)
        c.flip = c.sbuf("flip", [P, P])
        c.mask_q = c.sbuf("mask_q", [P, 2, 2, 2 * P], bf16)
        c.mask_k = c.sbuf("mask_k", [P, 2, 2 * P], bf16)
        c.bn = c.sbuf("bn", [P, TILES, 6])
        c.mv = c.sbuf("mv", [P, TILES, 2])
        c.mean2 = c.sbuf("mean2", [P, TILES])
        c.rstd = c.sbuf("rstd", [P, TILES])
        c.minus_half = c.sbuf("minus_half", [P, TILES])
        c.expert_ids_i = c.sbuf("expert_ids_i", [P, 16], mybir.dt.int32)
        c.expert_ids = c.sbuf("expert_ids", [P, 16])
        c.ids_wide = lambda e: c.expert_ids[:, 0:e].rearrange("p (o e) -> p o e", o=1).broadcast_to((P, TILES, e))
        c.logits = c.sbuf("logits", [P, TILES, 16])
        c.probs = c.sbuf("probs", [P, TILES, 16])
        c.pick = c.sbuf("pick", [P, TILES, 16])
        c.top = c.sbuf("top", [P, TILES, 8])
        c.top_i = c.sbuf("top_i", [P, TILES, 8], u32)
        c.top_f = c.sbuf("top_f", [P, TILES, 2])
        c.top_gap = c.sbuf("top_gap", [P, TILES])
        c.total = c.sbuf("total", [P, TILES])
        c.second = c.sbuf("second", [P, TILES])
        c.cw = c.sbuf("cw", [P, 9, TILES])
        c.cw_now = c.sbuf("cw_now", [P, 2, TILES])
        c.conv_w = c.sbuf("conv_w", [P, 2, TAPS])
        c.w_in = c.sbuf("w_in", [P, 2 * INNER])
        c.w_b = c.sbuf("w_b", [P, 2, STATE])
        c.w_c = c.sbuf("w_c", [STATE, INNER])
        c.w_out = c.sbuf("w_out", [P, 2, D])
        c.w1 = c.sbuf("w1", [P, D_FF])
        c.w2 = c.sbuf("w2", [P, D_FF // P, D])
        c.router0 = c.sbuf("router0", [P, 9])
        c.router1 = c.sbuf("router1", [P, 8])
        c.proj_names = PROJ
        c.proj = c.sbuf("proj", [P, len(PROJ), D])
        c.keys_twice = c.sbuf("keys_twice", [2, 2 * D])
        c.circ = c.sbuf("circ", [P, 2, D])
        c.circ_a = c.sbuf("circ_a", [P, D])
        c.circ_b = c.sbuf("circ_b", [P, D])
        c.columns = {name: c.sbuf("col_" + name, [P, n])[:] for name, n in (
            ("L0_attn_a_conv_b", 2), ("L0_attn_a_D_param", 2), ("L0_attn_b_bq", 1), ("L0_attn_b_bk", 1),
            ("L0_attn_b_ln1_w", 1), ("L0_attn_b_ln1_b", 1), ("L0_attn_b_ln2_w", 1), ("L0_attn_b_ln2_b", 1),
            ("L0_attn_b_b1", 4), ("L1_ffn_norm1_w", 1), ("L1_ffn_norm2_w", 1))}
        c.rows = {name: c.sbuf("row_" + name, [P, n])[:] for name, n in (
            ("L0_attn_a_ln_gamma", D), ("L0_attn_a_ln_beta", D), ("L0_attn_b_bv", D), ("L0_attn_b_bo", D),
            ("L0_attn_b_b2", D), ("L1_attn_b_decay", 1), ("L1_attn_b_gate", 1))}
        c.ps = ctx.enter_context(nc.psum_tensor("ps", [P, 8 * CHUNK], fp32))
        c.parts_dram = nc.dram_tensor("parts_dram", (2, 3, D, N_TOK), bf16).ap()
        c.out_dram = nc.dram_tensor("out_dram", (HEADS, P, CHUNK), fp32).ap()
        c.inverse_dram = nc.dram_tensor("inverse_dram", (HEADS, N_TOK), fp32).ap()
        c.keys_dram = nc.dram_tensor("keys_dram", (2, 2 * D), fp32).ap()

        constants_stage(c)

        def state_space():
            held, m = c.layer((("big", [P, 6, N_TOK], fp32), ("conv", [P, 2, N_TOK], fp32),
                               ("bu", [STATE, N_TOK], fp32), ("state", [STATE, N_TOK], fp32)))
            with held:
                c.big, c.conv = m["big"], m["conv"]
                c.bu, c.state = m["bu"][:], m["state"][:]
                norm_stage(c, c.x, c.h, transpose=True, first=True)
                state_space_stage(c)
                norm_stage(c, c.h, c.n)
                add_scaled_stage(c, c.x, c.n, c.rows["L0_attn_a_ln_gamma"])

        def experts(norm, router, soft_of_probs, weights, inner, shared=None):
            J = (inner + P - 1) // P
            held, m = c.layer((("ht_part", [P, 2, N_TOK], fp32r), ("wg", [P, 2, inner], fp32), ("wu", [P, 2, inner], fp32),
                               ("wd", [P, 2, J, D], fp32), ("wg_part", [P, 2, 2, inner], fp32r),
                               ("wu_part", [P, 2, 2, inner], fp32r), ("silu", [P, 2, CHUNK], fp32),
                               ("hid", [P, 2, J, CHUNK], fp32)))
            with held:
                c.ht_part, c.silu, c.hid = m["ht_part"], m["silu"], m["hid"]
                c.wg, c.wu, c.wd = m["wg"], m["wu"], m["wd"]
                c.wg_part, c.wu_part = m["wg_part"], m["wu_part"]
                norm(router=router, experts=[i[w] for w in weights])
                experts_stage(c, router, soft_of_probs, *(i[w] for w in weights), inner,
                              shared=[i[w] for w in shared] if shared else None)

        def experts0():
            experts(partial(norm_stage, c, c.x, c.h, transpose=True), c.router0, False, ("L0_ffn_Wg", "L0_ffn_Wu", "L0_ffn_Wd"), 352)

        def attention(w, window=None, dst=None, bq=None, bk=None, bv=None, biases=()):
            held, m = c.layer((("qk", [P, 2, N_TOK], fp32), ("prob", [P, P_UNITS, UNIT], fp32),
                               ("parts", [P, 2, PARTS, N_TOK], bf16), ("q_max", [P, 2, N_TOK], bf16),
                               ("q_exp", [P, 2, N_TOK], bf16), ("k_max", [P, 2, N_TOK], bf16),
                               ("k_exp", [P, 2, N_TOK], bf16), ("v", [P, TILES, D], fp32),
                               ("v_head", [P, 2, TILES, OUT_ROWS], fp32), ("out_head", [P, 2, CHUNK], fp32),
                               ("sums", [EARLY * CHUNKS, CHUNK], fp32),
                               ("late_sums", [(HEADS - EARLY) * CHUNKS * HD, CHUNK // HD], fp32)))
            with held:
                c.big, c.prob, c.parts, c.v = m["qk"], m["prob"], m["parts"], m["v"]
                c.q_max, c.q_exp, c.k_max, c.k_exp = m["q_max"], m["q_exp"], m["k_max"], m["k_exp"]
                c.v_head, c.out_head = m["v_head"], m["out_head"]
                c.sums, c.late_sums = m["sums"], m["late_sums"]
                project_stage(c, w, bq, bk, bv)
                heads_stage(c, window, biases)
                output_stage(c, w, dst)

        def experts1():
            norm_stage(c, c.x, c.h)
            norm_stage(c, c.h, c.n, rms=True, transpose=True, scale=c.columns["L1_ffn_norm1_w"])
            attention(8, dst=c.h)
            norm = partial(norm_stage, c, c.h, c.n, rms=True, transpose=True, scale=c.columns["L1_ffn_norm2_w"], onto=c.x)
            experts(norm, c.router1, True, ("L1_ffn_e_gate", "L1_ffn_e_up", "L1_ffn_e_down"), 256,
                    shared=("L1_ffn_sh_gate", "L1_ffn_sh_up", "L1_ffn_sh_down"))

        def local_attention():
            norm_stage(c, c.x, c.h)
            norm_stage(c, c.h, c.n, transpose=True, scale=c.columns["L0_attn_b_ln1_w"], shift=c.columns["L0_attn_b_ln1_b"])
            attention(0, window=0, dst=c.h, bq=c.columns["L0_attn_b_bq"], bk=c.columns["L0_attn_b_bk"],
                      bv=c.rows["L0_attn_b_bv"],
                      biases=((c.h, c.rows["L0_attn_b_bo"]), (c.x, c.rows["L0_attn_b_b2"])))
            norm_stage(c, c.h, c.n, transpose=True, scale=c.columns["L0_attn_b_ln2_w"], shift=c.columns["L0_attn_b_ln2_b"],
                       onto=c.x)
            held, m = c.layer((("ff_hid", [P, 2, D_FF // P, CHUNK], fp32),))
            with held:
                c.hid = m["ff_hid"]
                feed_forward_stage(c, c.x)

        def hologram():
            norm_stage(c, c.x, c.h, transpose=True)
            held, m = c.layer((("scan", [P, 1, N_TOK], fp32),))
            with held:
                c.big = m["scan"]
                hologram_stage(c)

        if "a" in layers:
            state_space()
        else:
            later_constants_stage(c)
        if "b" in layers:
            experts0()
        if "c" in layers:
            local_attention()
        if "d" in layers:
            experts0()
        if "e" in layers:
            norm_stage(c, c.x, c.h, transpose=True)
            attention(4, window=1, dst=c.x)
        if "f" in layers:
            experts1()
        if "g" in layers:
            hologram()
        if "h" in layers:
            experts1()
        store_stage(c, out)


TRANSPOSED = ("L0_attn_a_W_in", "L0_attn_a_W_B", "L0_attn_a_W_C", "L0_attn_a_W_out",
              "L1_attn_a_Wq", "L1_attn_a_Wk", "L1_attn_a_Wv", "L1_attn_a_Wo")


def kernel(**inputs):
    import numpy as _np
    import concourse.bacc as _bacc
    from concourse import mybir as _mybir
    from concourse.bass_utils import run_bass_kernel_spmd as _run

    nc = _bacc.Bacc("TRN2", target_bir_lowering=False, num_devices=1)
    arrays, aps = {}, {}
    for name, a in inputs.items():
        a = _np.asarray(a)
        if name in TRANSPOSED:
            name, a = name + "_T", a.T
        a = _np.ascontiguousarray(a if a.ndim else a.reshape(1))
        arrays[f"in_{name}_dram"] = a
        aps[name] = nc.dram_tensor(f"in_{name}_dram", a.shape, _mybir.dt.from_np(a.dtype), kind="ExternalInput").ap()
    out = nc.dram_tensor("out_0_dram", (1, N_TOK, D), fp32, kind="ExternalOutput").ap()
    hybrid_stack(nc, aps, out)
    r = _run(nc, [arrays], core_ids=[0])
    return r.results[0]["out_0_dram"]
```
